# Optimizing a Trainium2 kernel written in Bass

```python
import numpy as np
import jax
import jax.numpy as jnp

def _softmax(x, axis=-1):
    return jax.nn.softmax(x, axis=axis)

def _gelu(x):
    return jax.nn.gelu(x, approximate=True)

def _silu(x):
    return jax.nn.silu(x)

def _sigmoid(x):
    return jax.nn.sigmoid(x)

def _layernorm(x, axis=-1, eps=1e-05):
    m = jnp.mean(x, axis=axis, keepdims=True)
    v = jnp.var(x, axis=axis, keepdims=True)
    return (x - m) / jnp.sqrt(v + eps)

def _scatter_add(tgt, idx, src, axis=0):
    return tgt.at[idx].add(src)

def _segment_sum(src, seg, n):
    return jax.ops.segment_sum(src, seg, n)
kernel_name = 'mk_conv_seq_d4_conv_nchw64_r4_4caf64'

def setup_inputs(seed: int=0):
    np.random.seed(seed)
    _w = jnp.asarray

    def _rec_inputs():
        import jax
        import jax.numpy as jnp
        _gk = jax.random.key(seed)
        x = -0.000125 + 0.9999 * jax.random.normal(jax.random.fold_in(_gk, 1), (8, 16, 64, 64), jnp.float32)
        return x
    x = _rec_inputs()

    def _L0_conv_setup():
        import jax, jax.numpy as jnp
        import numpy as np
        from jax import lax
        B, C, H, W = (8, 16, 64, 64)
        GROUPS, EPS = (8, 1e-05)

        def _group_norm(x, w, b):
            b_, c, h, wd = x.shape
            xg = x.reshape(b_, GROUPS, c // GROUPS, h, wd)
            mu = xg.mean(axis=(2, 3, 4), keepdims=True)
            var = xg.var(axis=(2, 3, 4), keepdims=True)
            xn = ((xg - mu) * lax.rsqrt(var + EPS)).reshape(b_, c, h, wd)
            return xn * w[None, :, None, None] + b[None, :, None, None]

        def _gated_scan(gate_f, u_f):

            def step(s, gu):
                g, u = gu
                s = g * s + (1.0 - g) * u
                return (s, s)
            _, ys = lax.scan(step, jnp.zeros_like(u_f[0]), (gate_f, u_f))
            return ys
        key = jax.random.key(seed)
        ks = jax.random.split(key, 7)
        scale = 1.0 / np.sqrt(C)
        return {'x': jax.random.normal(ks[0], (B, C, H, W), dtype=jnp.float32), 'gn_w': jnp.ones((C,), dtype=jnp.float32), 'gn_b': jnp.zeros((C,), dtype=jnp.float32), 'gate_w': jax.random.normal(ks[1], (C, C), dtype=jnp.float32) * scale, 'gate_b': jnp.zeros((C,), dtype=jnp.float32), 'upd_w': jax.random.normal(ks[2], (C, C), dtype=jnp.float32) * scale, 'upd_b': jnp.zeros((C,), dtype=jnp.float32)}
    _L0_conv_all = _L0_conv_setup()
    _L0_conv_in = {k: v for k, v in _L0_conv_all.items() if k in ('gn_w', 'gn_b', 'gate_w', 'gate_b', 'upd_w', 'upd_b')}
    del _L0_conv_all

    def _L1_conv_setup():
        import jax, jax.numpy as jnp
        import numpy as np
        from jax import lax
        EPS = 1e-05
        B, C, H, W = (16, 16, 56, 56)
        HID, E, OUP = (96, 8, 16)

        def _bn(x, g, b, m, v):
            scale = g * lax.rsqrt(v + EPS)
            return (x - m[:, None, None]) * scale[:, None, None] + b[:, None, None]

        def _relu6(x):
            return jnp.clip(x, 0.0, 6.0)
        key = jax.random.key(seed)
        ks = jax.random.split(key, 6)
        x = jax.random.normal(ks[0], (B, C, H, W), dtype=jnp.float32)
        w1 = jax.random.normal(ks[1], (HID, C), dtype=jnp.float32) * 0.05
        wd = jax.random.normal(ks[2], (HID, 1, 3, 3), dtype=jnp.float32) * 0.05
        we = jax.random.normal(ks[3], (E, OUP, HID), dtype=jnp.float32) * 0.05
        wr = jax.random.normal(ks[4], (E, C), dtype=jnp.float32) * 0.05
        br = jnp.zeros((E,), dtype=jnp.float32)
        return dict(x=x, w1=w1, g1=jnp.ones(HID), b1=jnp.zeros(HID), m1=jnp.zeros(HID), v1=jnp.ones(HID), wd=wd, g2=jnp.ones(HID), b2=jnp.zeros(HID), m2=jnp.zeros(HID), v2=jnp.ones(HID), we=we, g3=jnp.ones(OUP), b3=jnp.zeros(OUP), m3=jnp.zeros(OUP), v3=jnp.ones(OUP), wr=wr, br=br)
    _L1_conv_all = _L1_conv_setup()
    _L1_conv_in = {k: v for k, v in _L1_conv_all.items() if k in ('w1', 'g1', 'b1', 'm1', 'v1', 'wd', 'g2', 'b2', 'm2', 'v2', 'we', 'g3', 'b3', 'm3', 'v3', 'wr', 'br')}
    del _L1_conv_all

    def _L2_conv_setup():
        import jax, jax.numpy as jnp
        import numpy as np
        B, C, H, W = (4, 16, 32, 32)
        K = 9
        OFFSET_SCALE = 1.0
        EPS = 1e-05

        def conv2d(x, w, b):
            out = jax.lax.conv_general_dilated(x, w, (1, 1), 'SAME', dimension_numbers=('NCHW', 'OIHW', 'NCHW'))
            return out + b[None, :, None, None]

        def deform_conv(x, w, b, ow, ob):
            Bn, Cin, Hh, Ww = x.shape
            off = conv2d(x, ow, ob).reshape(Bn, K, 2, Hh, Ww) * OFFSET_SCALE
            dy = jnp.array([-1, -1, -1, 0, 0, 0, 1, 1, 1], jnp.float32)
            dx = jnp.array([-1, 0, 1, -1, 0, 1, -1, 0, 1], jnp.float32)
            iy = jnp.arange(Hh, dtype=jnp.float32)
            ix = jnp.arange(Ww, dtype=jnp.float32)
            cy = iy[None, None, :, None] + dy[None, :, None, None] + off[:, :, 0]
            cx = ix[None, None, None, :] + dx[None, :, None, None] + off[:, :, 1]
            y0 = jnp.floor(cy)
            x0 = jnp.floor(cx)
            wy = cy - y0
            wx = cx - x0
            y0i = y0.astype(jnp.int32)
            x0i = x0.astype(jnp.int32)
            vals = x.reshape(Bn, Cin, Hh * Ww)

            def gather(yi, xi, wgt):
                valid = ((yi >= 0) & (yi < Hh) & (xi >= 0) & (xi < Ww)).astype(x.dtype)
                idx = (jnp.clip(yi, 0, Hh - 1) * Ww + jnp.clip(xi, 0, Ww - 1)).reshape(Bn, 1, K * Hh * Ww)
                g = jnp.take_along_axis(vals, idx, axis=2).reshape(Bn, Cin, K, Hh, Ww)
                return g * (wgt * valid)[:, None]
            samp = gather(y0i, x0i, (1 - wy) * (1 - wx)) + gather(y0i, x0i + 1, (1 - wy) * wx) + gather(y0i + 1, x0i, wy * (1 - wx)) + gather(y0i + 1, x0i + 1, wy * wx)
            out = jnp.einsum('bckhw,ock->bohw', samp, w.reshape(w.shape[0], Cin, K))
            return out + b[None, :, None, None]

        def group_norm1(x, gamma, beta):
            m = jnp.mean(x, axis=(1, 2, 3), keepdims=True)
            v = jnp.var(x, axis=(1, 2, 3), keepdims=True)
            return (x - m) * jax.lax.rsqrt(v + EPS) * gamma[None, :, None, None] + beta[None, :, None, None]
        key = jax.random.key(seed)
        ks = jax.random.split(key, 6)
        n = lambda k, shape, s: jax.random.normal(k, shape, dtype=jnp.float32) * s
        return {'x': jax.random.normal(ks[0], (B, C, H, W), dtype=jnp.float32), 'w1': n(ks[1], (C, C, 3, 3), 0.05), 'b1': jnp.zeros((C,), jnp.float32), 'ow1': n(ks[2], (2 * K, C, 3, 3), 0.01), 'ob1': jnp.zeros((2 * K,), jnp.float32), 'g1': jnp.ones((C,), jnp.float32), 'be1': jnp.zeros((C,), jnp.float32), 'w2': n(ks[3], (C, C, 3, 3), 0.05), 'b2': jnp.zeros((C,), jnp.float32), 'ow2': n(ks[4], (2 * K, C, 3, 3), 0.01), 'ob2': jnp.zeros((2 * K,), jnp.float32), 'g2': jnp.ones((C,), jnp.float32), 'be2': jnp.zeros((C,), jnp.float32)}
    _L2_conv_all = _L2_conv_setup()
    _L2_conv_in = {k: v for k, v in _L2_conv_all.items() if k in ('w1', 'b1', 'ow1', 'ob1', 'g1', 'be1', 'w2', 'b2', 'ow2', 'ob2', 'g2', 'be2')}
    del _L2_conv_all

    def _L3_conv_setup():
        import jax, jax.numpy as jnp
        import numpy as np
        from jax import lax
        BN_EPS = 1e-05
        D2_EPS = 1e-12

        def _conv_dt(x, centers):
            B, C, H, W = x.shape
            patches = lax.conv_general_dilated_patches(x, filter_shape=(3, 3), window_strides=(1, 1), padding=((1, 1), (1, 1)))
            p = patches.transpose(0, 2, 3, 1).reshape(-1, C * 9)
            p2 = jnp.sum(p * p, axis=-1, keepdims=True)
            c2 = jnp.sum(centers * centers, axis=-1)
            d2 = p2 - 2.0 * (p @ centers.T) + c2
            d = jnp.sqrt(jnp.maximum(d2, D2_EPS))
            return d.reshape(B, H, W, -1).transpose(0, 3, 1, 2)

        def _bn(y, gamma, beta):
            mu = jnp.mean(y, axis=(0, 2, 3), keepdims=True)
            var = jnp.var(y, axis=(0, 2, 3), keepdims=True)
            yhat = (y - mu) * lax.rsqrt(var + BN_EPS)
            return yhat * gamma[None, :, None, None] + beta[None, :, None, None]
        key = jax.random.key(seed)
        ks = jax.random.split(key, 7)
        C = 16
        D = C * 9
        x = jax.random.normal(ks[0], (32, C, 56, 56), dtype=jnp.float32)
        centers1 = jax.random.normal(ks[1], (C, D), dtype=jnp.float32) * (1.0 / np.sqrt(D))
        gamma1 = jnp.ones((C,), dtype=jnp.float32)
        beta1 = jnp.zeros((C,), dtype=jnp.float32)
        centers2 = jax.random.normal(ks[2], (C, D), dtype=jnp.float32) * (1.0 / np.sqrt(D))
        gamma2 = jnp.ones((C,), dtype=jnp.float32)
        beta2 = jnp.zeros((C,), dtype=jnp.float32)
        return {'x': x, 'centers1': centers1, 'gamma1': gamma1, 'beta1': beta1, 'centers2': centers2, 'gamma2': gamma2, 'beta2': beta2}
    _L3_conv_all = _L3_conv_setup()
    _L3_conv_in = {k: v for k, v in _L3_conv_all.items() if k in ('centers1', 'gamma1', 'beta1', 'centers2', 'gamma2', 'beta2')}
    del _L3_conv_all
    return {'x': x, 'L0_conv_gn_w': _L0_conv_in['gn_w'], 'L0_conv_gn_b': _L0_conv_in['gn_b'], 'L0_conv_gate_w': _L0_conv_in['gate_w'], 'L0_conv_gate_b': _L0_conv_in['gate_b'], 'L0_conv_upd_w': _L0_conv_in['upd_w'], 'L0_conv_upd_b': _L0_conv_in['upd_b'], 'L1_conv_w1': _L1_conv_in['w1'], 'L1_conv_g1': _L1_conv_in['g1'], 'L1_conv_b1': _L1_conv_in['b1'], 'L1_conv_m1': _L1_conv_in['m1'], 'L1_conv_v1': _L1_conv_in['v1'], 'L1_conv_wd': _L1_conv_in['wd'], 'L1_conv_g2': _L1_conv_in['g2'], 'L1_conv_b2': _L1_conv_in['b2'], 'L1_conv_m2': _L1_conv_in['m2'], 'L1_conv_v2': _L1_conv_in['v2'], 'L1_conv_we': _L1_conv_in['we'], 'L1_conv_g3': _L1_conv_in['g3'], 'L1_conv_b3': _L1_conv_in['b3'], 'L1_conv_m3': _L1_conv_in['m3'], 'L1_conv_v3': _L1_conv_in['v3'], 'L1_conv_wr': _L1_conv_in['wr'], 'L1_conv_br': _L1_conv_in['br'], 'L2_conv_w1': _L2_conv_in['w1'], 'L2_conv_b1': _L2_conv_in['b1'], 'L2_conv_ow1': _L2_conv_in['ow1'], 'L2_conv_ob1': _L2_conv_in['ob1'], 'L2_conv_g1': _L2_conv_in['g1'], 'L2_conv_be1': _L2_conv_in['be1'], 'L2_conv_w2': _L2_conv_in['w2'], 'L2_conv_b2': _L2_conv_in['b2'], 'L2_conv_ow2': _L2_conv_in['ow2'], 'L2_conv_ob2': _L2_conv_in['ob2'], 'L2_conv_g2': _L2_conv_in['g2'], 'L2_conv_be2': _L2_conv_in['be2'], 'L3_conv_centers1': _L3_conv_in['centers1'], 'L3_conv_gamma1': _L3_conv_in['gamma1'], 'L3_conv_beta1': _L3_conv_in['beta1'], 'L3_conv_centers2': _L3_conv_in['centers2'], 'L3_conv_gamma2': _L3_conv_in['gamma2'], 'L3_conv_beta2': _L3_conv_in['beta2']}

def reference(x, L0_conv_gn_w, L0_conv_gn_b, L0_conv_gate_w, L0_conv_gate_b, L0_conv_upd_w, L0_conv_upd_b, L1_conv_w1, L1_conv_g1, L1_conv_b1, L1_conv_m1, L1_conv_v1, L1_conv_wd, L1_conv_g2, L1_conv_b2, L1_conv_m2, L1_conv_v2, L1_conv_we, L1_conv_g3, L1_conv_b3, L1_conv_m3, L1_conv_v3, L1_conv_wr, L1_conv_br, L2_conv_w1, L2_conv_b1, L2_conv_ow1, L2_conv_ob1, L2_conv_g1, L2_conv_be1, L2_conv_w2, L2_conv_b2, L2_conv_ow2, L2_conv_ob2, L2_conv_g2, L2_conv_be2, L3_conv_centers1, L3_conv_gamma1, L3_conv_beta1, L3_conv_centers2, L3_conv_gamma2, L3_conv_beta2):
    import jax
    import jax.numpy as jnp

    def _L0_conv_ref(x, gn_w, gn_b, gate_w, gate_b, upd_w, upd_b):
        import jax, jax.numpy as jnp
        import numpy as np
        from jax import lax
        B, C, H, W = (8, 16, 64, 64)
        GROUPS, EPS = (8, 1e-05)

        def _group_norm(x, w, b):
            b_, c, h, wd = x.shape
            xg = x.reshape(b_, GROUPS, c // GROUPS, h, wd)
            mu = xg.mean(axis=(2, 3, 4), keepdims=True)
            var = xg.var(axis=(2, 3, 4), keepdims=True)
            xn = ((xg - mu) * lax.rsqrt(var + EPS)).reshape(b_, c, h, wd)
            return xn * w[None, :, None, None] + b[None, :, None, None]

        def _gated_scan(gate_f, u_f):

            def step(s, gu):
                g, u = gu
                s = g * s + (1.0 - g) * u
                return (s, s)
            _, ys = lax.scan(step, jnp.zeros_like(u_f[0]), (gate_f, u_f))
            return ys
        h = _group_norm(x, gn_w, gn_b)
        gate = jax.nn.sigmoid(jnp.einsum('oc,bchw->bohw', gate_w, h) + gate_b[None, :, None, None])
        u = jnp.einsum('oc,bchw->bohw', upd_w, h) + upd_b[None, :, None, None]
        hw = _gated_scan(gate.transpose(3, 0, 1, 2), u.transpose(3, 0, 1, 2))
        hw = hw.transpose(1, 2, 3, 0)
        hh = _gated_scan(gate.transpose(2, 0, 1, 3), hw.transpose(2, 0, 1, 3))
        hh = hh.transpose(1, 2, 0, 3)
        return x + hh

    def _L1_conv_ref(x, w1, g1, b1, m1, v1, wd, g2, b2, m2, v2, we, g3, b3, m3, v3, wr, br):
        import jax, jax.numpy as jnp
        import numpy as np
        from jax import lax
        EPS = 1e-05
        B, C, H, W = (16, 16, 56, 56)
        HID, E, OUP = (96, 8, 16)

        def _bn(x, g, b, m, v):
            scale = g * lax.rsqrt(v + EPS)
            return (x - m[:, None, None]) * scale[:, None, None] + b[:, None, None]

        def _relu6(x):
            return jnp.clip(x, 0.0, 6.0)
        pooled = jnp.mean(x, axis=(2, 3))
        routing = jax.nn.sigmoid(pooled @ wr.T + br)
        h = jnp.einsum('bchw,oc->bohw', x, w1)
        h = _relu6(_bn(h, g1, b1, m1, v1))
        h = lax.conv_general_dilated(h, wd, window_strides=(1, 1), padding=((1, 1), (1, 1)), feature_group_count=HID, dimension_numbers=('NCHW', 'OIHW', 'NCHW'))
        h = _relu6(_bn(h, g2, b2, m2, v2))
        k = jnp.einsum('be,eoc->boc', routing, we)
        out = jnp.einsum('bchw,boc->bohw', h, k)
        out = _bn(out, g3, b3, m3, v3)
        return x + out

    def _L2_conv_ref(x, w1, b1, ow1, ob1, g1, be1, w2, b2, ow2, ob2, g2, be2):
        import jax, jax.numpy as jnp
        import numpy as np
        B, C, H, W = (4, 16, 32, 32)
        K = 9
        OFFSET_SCALE = 1.0
        EPS = 1e-05

        def conv2d(x, w, b):
            out = jax.lax.conv_general_dilated(x, w, (1, 1), 'SAME', dimension_numbers=('NCHW', 'OIHW', 'NCHW'))
            return out + b[None, :, None, None]

        def deform_conv(x, w, b, ow, ob):
            Bn, Cin, Hh, Ww = x.shape
            off = conv2d(x, ow, ob).reshape(Bn, K, 2, Hh, Ww) * OFFSET_SCALE
            dy = jnp.array([-1, -1, -1, 0, 0, 0, 1, 1, 1], jnp.float32)
            dx = jnp.array([-1, 0, 1, -1, 0, 1, -1, 0, 1], jnp.float32)
            iy = jnp.arange(Hh, dtype=jnp.float32)
            ix = jnp.arange(Ww, dtype=jnp.float32)
            cy = iy[None, None, :, None] + dy[None, :, None, None] + off[:, :, 0]
            cx = ix[None, None, None, :] + dx[None, :, None, None] + off[:, :, 1]
            y0 = jnp.floor(cy)
            x0 = jnp.floor(cx)
            wy = cy - y0
            wx = cx - x0
            y0i = y0.astype(jnp.int32)
            x0i = x0.astype(jnp.int32)
            vals = x.reshape(Bn, Cin, Hh * Ww)

            def gather(yi, xi, wgt):
                valid = ((yi >= 0) & (yi < Hh) & (xi >= 0) & (xi < Ww)).astype(x.dtype)
                idx = (jnp.clip(yi, 0, Hh - 1) * Ww + jnp.clip(xi, 0, Ww - 1)).reshape(Bn, 1, K * Hh * Ww)
                g = jnp.take_along_axis(vals, idx, axis=2).reshape(Bn, Cin, K, Hh, Ww)
                return g * (wgt * valid)[:, None]
            samp = gather(y0i, x0i, (1 - wy) * (1 - wx)) + gather(y0i, x0i + 1, (1 - wy) * wx) + gather(y0i + 1, x0i, wy * (1 - wx)) + gather(y0i + 1, x0i + 1, wy * wx)
            out = jnp.einsum('bckhw,ock->bohw', samp, w.reshape(w.shape[0], Cin, K))
            return out + b[None, :, None, None]

        def group_norm1(x, gamma, beta):
            m = jnp.mean(x, axis=(1, 2, 3), keepdims=True)
            v = jnp.var(x, axis=(1, 2, 3), keepdims=True)
            return (x - m) * jax.lax.rsqrt(v + EPS) * gamma[None, :, None, None] + beta[None, :, None, None]
        h = jax.nn.relu(group_norm1(deform_conv(x, w1, b1, ow1, ob1), g1, be1)) + x
        h = jax.nn.relu(group_norm1(deform_conv(h, w2, b2, ow2, ob2), g2, be2)) + h
        return h

    def _L3_conv_ref(x, centers1, gamma1, beta1, centers2, gamma2, beta2):
        import jax, jax.numpy as jnp
        import numpy as np
        from jax import lax
        BN_EPS = 1e-05
        D2_EPS = 1e-12

        def _conv_dt(x, centers):
            B, C, H, W = x.shape
            patches = lax.conv_general_dilated_patches(x, filter_shape=(3, 3), window_strides=(1, 1), padding=((1, 1), (1, 1)))
            p = patches.transpose(0, 2, 3, 1).reshape(-1, C * 9)
            p2 = jnp.sum(p * p, axis=-1, keepdims=True)
            c2 = jnp.sum(centers * centers, axis=-1)
            d2 = p2 - 2.0 * (p @ centers.T) + c2
            d = jnp.sqrt(jnp.maximum(d2, D2_EPS))
            return d.reshape(B, H, W, -1).transpose(0, 3, 1, 2)

        def _bn(y, gamma, beta):
            mu = jnp.mean(y, axis=(0, 2, 3), keepdims=True)
            var = jnp.var(y, axis=(0, 2, 3), keepdims=True)
            yhat = (y - mu) * lax.rsqrt(var + BN_EPS)
            return yhat * gamma[None, :, None, None] + beta[None, :, None, None]
        out = jax.nn.relu(_bn(_conv_dt(x, centers1), gamma1, beta1))
        out = _bn(_conv_dt(out, centers2), gamma2, beta2)
        return jax.nn.relu(out + x)

    def _gn(v, G=32, eps=1e-05):
        B_, C_, H_, W_ = v.shape
        g = v.reshape(B_, G, C_ // G, H_, W_)
        m = jnp.mean(g, axis=(2, 3, 4), keepdims=True)
        s = jnp.var(g, axis=(2, 3, 4), keepdims=True)
        return ((g - m) / jnp.sqrt(s + eps)).reshape(v.shape)

    def _ln_c(v, eps=1e-06):
        m = jnp.mean(v, axis=1, keepdims=True)
        s = jnp.var(v, axis=1, keepdims=True)
        return (v - m) / jnp.sqrt(s + eps)

    def _ln_t(v, eps=1e-05):
        m = jnp.mean(v, axis=-1, keepdims=True)
        s = jnp.var(v, axis=-1, keepdims=True)
        return (v - m) / jnp.sqrt(s + eps)

    def _to_tokens(v):
        B_, C_, H_, W_ = v.shape
        return v.reshape(B_, C_, H_ * W_).transpose(0, 2, 1)

    def _from_tokens(t, like):
        B_, C_, H_, W_ = like.shape
        return t.transpose(0, 2, 1).reshape(B_, C_, H_, W_)
    x = _L0_conv_ref(x, L0_conv_gn_w, L0_conv_gn_b, L0_conv_gate_w, L0_conv_gate_b, L0_conv_upd_w, L0_conv_upd_b)
    x = _L1_conv_ref(x, L1_conv_w1, L1_conv_g1, L1_conv_b1, L1_conv_m1, L1_conv_v1, L1_conv_wd, L1_conv_g2, L1_conv_b2, L1_conv_m2, L1_conv_v2, L1_conv_we, L1_conv_g3, L1_conv_b3, L1_conv_m3, L1_conv_v3, L1_conv_wr, L1_conv_br)
    x = _L2_conv_ref(x, L2_conv_w1, L2_conv_b1, L2_conv_ow1, L2_conv_ob1, L2_conv_g1, L2_conv_be1, L2_conv_w2, L2_conv_b2, L2_conv_ow2, L2_conv_ob2, L2_conv_g2, L2_conv_be2)
    x = _L3_conv_ref(x, L3_conv_centers1, L3_conv_gamma1, L3_conv_beta1, L3_conv_centers2, L3_conv_gamma2, L3_conv_beta2)
    return x

_drawn_inputs = setup_inputs


def setup_inputs(seed=0):
    import zlib

    import numpy as np

    out = dict(_drawn_inputs(seed))
    spreads = {'L0_conv_gn_w': (1.0, 0.2),
     'L0_conv_gn_b': (0.0, 0.1),
     'L0_conv_gate_b': (0.0, 0.48),
     'L0_conv_upd_b': (0.0, 0.1),
     'L1_conv_g1': (1.0, 0.6),
     'L1_conv_b1': (0.0, 0.8),
     'L1_conv_m1': (0.0, 0.8),
     'L1_conv_v1': (1.0, 0.6),
     'L1_conv_g2': (1.0, 0.6),
     'L1_conv_b2': (0.0, 0.1),
     'L1_conv_m2': (0.0, 0.1),
     'L1_conv_v2': (1.0, 0.6),
     'L1_conv_g3': (1.0, 0.2),
     'L1_conv_b3': (0.0, 0.1),
     'L1_conv_m3': (0.0, 0.1),
     'L1_conv_v3': (1.0, 0.6),
     'L1_conv_br': (0.0, 0.8),
     'L2_conv_b1': (0.0, 0.1),
     'L2_conv_ob1': (0.0, 0.1),
     'L2_conv_g1': (1.0, 0.2),
     'L2_conv_be1': (0.0, 0.1),
     'L2_conv_b2': (0.0, 0.1),
     'L2_conv_ob2': (0.0, 0.1),
     'L2_conv_g2': (1.0, 0.2),
     'L2_conv_be2': (0.0, 0.1),
     'L3_conv_gamma1': (1.0, 0.6),
     'L3_conv_beta1': (0.0, 0.8),
     'L3_conv_gamma2': (1.0, 0.2),
     'L3_conv_beta2': (0.0, 0.1)}
    factors = {'L1_conv_w1': 4.597,
     'L1_conv_wd': 4.009,
     'L1_conv_wr': 8.0,
     'L3_conv_centers1': 8.0,
     'L3_conv_centers2': 8.0}
    for name, (base, spread) in spreads.items():
        noise = np.random.default_rng([zlib.crc32(name.encode()), seed]).standard_normal(out[name].shape)
        drawn = base * np.exp(spread * noise) if base else spread * noise
        out[name] = jnp.asarray(drawn.astype(out[name].dtype))
    for name, factor in factors.items():
        out[name] = (out[name] * factor).astype(out[name].dtype)
    return out
```

```python
from contextlib import ExitStack

import numpy as np
import concourse.bass as bass
from concourse import mybir

F32 = mybir.dt.float32
I32 = mybir.dt.int32
ALU = mybir.AluOpType
ACT = mybir.ActivationFunctionType
AX = mybir.AxisListType

P = 128
B, C, H, W = 8, 16, 64, 64
N = H * W
CH = 512
NCH = N // CH
CR = CH // W
HID, NT = 96, B * 96 // P
E = 8
K = 9
PW = W + 2
PADN = PW * PW
XW = W + 4
XN = XW * XW
BLK = 16
BR = H // BLK
BPX = BR * W
HR = BR + 4
HB = HR * XW
EPS = 1e-5
D2_EPS = 1e-12
REACH = 67
NG = 5

VEC = {}
for name, width in [("gn_w", 1), ("gn_b", 1), ("gate_b", 1), ("upd_b", 1), ("g3", 1), ("b3", 1), ("m3", 1),
                    ("v3", 1), ("dg0", 1), ("dbe0", 1), ("db0", 1), ("dg1", 1), ("dbe1", 1), ("db1", 1),
                    ("gamma0", 1), ("beta0", 1), ("gamma1", 1), ("beta1", 1),
                    ("g1", NT), ("b1", NT), ("m1", NT), ("v1", NT), ("g2", NT), ("b2", NT), ("m2", NT),
                    ("v2", NT), ("wd", NT * K), ("br", E), ("oby0", 1), ("obx0", 1), ("oby1", 1), ("obx1", 1)]:
    VEC[name] = (sum(w for _, w in VEC.values()), width)
NVEC = sum(w for _, w in VEC.values())

WREP = {}
for name, width in [("gate", C), ("upd", C), ("w1", HID), ("wr", E), ("ow0", 2 * K * K), ("ow1", 2 * K * K),
                    ("cw0", K * C), ("cw1", K * C), ("sw0", K * C), ("sw1", K * C), ("dt0", K * C),
                    ("dt1", K * C), ("cn0", K * C), ("cn1", K * C), ("we", NT * E * C)]:
    WREP[name] = (sum(w for _, w in WREP.values()), width)
NWREP = sum(w for _, w in WREP.values())

CONST = {}
for name, width in [("ident", P), ("same_image", P), ("same_channel", P), ("same_pair", P), ("px8", 8),
                    ("blkhot", BLK), ("steps", 2 * REACH + 1), ("rows", BR), ("columns", W)]:
    CONST[name] = (sum(w for _, w in CONST.values()), width)
NCONST = sum(w for _, w in CONST.values())


def constants():
    c = np.zeros((P, NCONST), np.float32)
    p = np.arange(P)

    def put(name, value):
        o, w = CONST[name]
        c[:, o:o + w] = value

    put("ident", p[:, None] == p[None, :])
    put("same_image", p[:, None] // C == p[None, :] // C)
    put("same_channel", p[:, None] % C == p[None, :] % C)
    put("same_pair", p[:, None] // 2 == p[None, :] // 2)
    put("px8", p[:, None] % 8 == np.arange(8)[None, :])
    put("blkhot", p[:, None] % BLK == np.arange(BLK)[None, :])
    put("steps", np.arange(-REACH, REACH + 1)[None, :])
    put("rows", np.arange(BR)[None, :])
    put("columns", np.arange(W)[None, :])
    return c


def build(nc, x, const, vectors, weights, out):
    with ExitStack() as ctx:
        SIZE = 53200
        arena = ctx.enter_context(nc.sbuf_tensor("arena", [P, SIZE], F32))
        taken = [0]

        def place(width, at=None):
            if at is None:
                at = taken[0]
                taken[0] += width
            assert at + width <= SIZE, (at, width)
            return at

        def ap(at, dims, p0=0, pn=P):
            return bass.AP(arena, at + p0 * SIZE, [[SIZE, pn]] + [list(d) for d in dims])

        def cols(at, n, p0=0, pn=P):
            return ap(at, [[1, n]], p0, pn)

        CON = place(NCONST)
        VE = place(NVEC)
        WR = place(NWREP)

        def con(name, i=0, n=None):
            o, w = CONST[name]
            return cols(CON + o + i, w if n is None else n)

        def vec(name, i=0, n=1, pn=P):
            o, _ = VEC[name]
            return cols(VE + o + i, n, 0, pn)

        SMALL = place(720)
        small_at = [SMALL]

        def small(n):
            small_at[0] += n
            assert small_at[0] <= SMALL + 720
            return small_at[0] - n

        MATS = place(2 * P + 2 * NT * P + K * P)
        W_GATE, W_UPD, W_HID = MATS, MATS + P, MATS + 2 * P
        W_OUT = W_HID + NT * P
        W_DIAG = W_OUT + NT * P
        W_OFF = place(K * 2 * B * K, MATS)
        W_SAMP = place(K * P, MATS + K * 2 * B * K)
        ZERO = place(P, W_SAMP + K * P)
        W_DT = place(K * P, MATS)

        BIG = taken[0]
        T_HID = [place(N) for _ in range(NT)]
        T_PAD = [place(PADN) for _ in range(4)]
        XIN = place(N)

        XA = T_PAD[0]
        XB = BIG
        GRP = BIG + C * HB
        GN_ = C * W
        OFFA = GRP
        YA = BIG
        OFFB = XA + XN
        TXY = OFFB + 2 * K * BPX
        TT = TXY + 6 * K * W
        TMP = TT + 3 * 9 * W
        ST = TMP + 3 * GN_
        YB = ST + 3 * GN_
        place(0, YB + GN_)

        xa_d = nc.dram_tensor("padded_image", [B, C, XN], F32, kind="Internal").ap()
        off_d = nc.dram_tensor("offsets", [2, K, B, N], F32, kind="Internal").ap()
        y_d = nc.dram_tensor("sampled", [C, B * BLK, BPX], F32, kind="Internal").ap()
        flag_d = nc.dram_tensor("reach", [K, BLK], I32, kind="Internal").ap()

        psum = ctx.enter_context(nc.psum_tensor("psum", [P, 8, CH], F32))

        def ps(bank, off, n, pn=P):
            return psum[0:pn, bank, off:off + n]

        def ap_ps(bank, dims):
            return bass.AP(psum, bank * CH, [[8 * CH, P]] + [list(d) for d in dims])

        def sem(name):
            return ctx.enter_context(nc.semaphore(name))

        s_const, s_vec, s_wrep, s_x = sem("const_loaded"), sem("vec_loaded"), sem("weights_loaded"), sem("x_loaded")
        s_out = sem("out_stored")
        s_v, s_a, s_g = sem("vector_chain"), sem("scalar_chain"), sem("gpsimd_chain")
        s_stat, s_grp, s_var, s_std, s_coef = (sem("stats_ready"), sem("group_sums_ready"), sem("variance_ready"),
                                               sem("deviation_ready"), sem("coefficients_ready"))
        s_w0, s_w1, s_wo = sem("gate_weights_ready"), sem("hidden_weights_ready"), sem("out_weights_ready")
        s_hn = sem("normed_ready")
        s_gate, s_upd = sem("gate_products_ready"), sem("update_products_ready")
        s_g_act, s_blend = sem("gate_chunks_ready"), sem("update_chunks_ready")
        s_xsum, s_pool_w, s_route, s_rsig = (sem("layer0_ready"), sem("pooled_weights_ready"),
                                             sem("routing_logits_ready"), sem("routing_ready"))
        s_rl = sem("routing_biased")
        s_bn, s_bnstd = sem("bn_variance_ready"), sem("bn_deviation_ready")
        s_bnc = sem("bn_coefficients_ready")
        s_padz = sem("hidden_padding_cleared")
        s_c1, s_c1_free = sem("hidden_products_ready"), sem("hidden_banks_free")
        s_relu = sem("hidden_chunks_written")
        s_clip_g = sem("hidden_clipped_by_gpsimd")
        s_dwv, s_dwa = sem("depthwise_by_vector"), sem("depthwise_by_tensor")
        s_dw, s_dw_free = sem("depthwise_products_ready"), sem("depthwise_banks_free")
        s_diag = sem("diagonals_ready")
        s_hid = sem("hidden_tiles_finished")
        s_proj, s_proj_free = sem("projection_ready"), sem("projection_banks_free")
        s_xa = sem("layer_result_in_padded_image")

        s_ow, s_sw = sem("offset_weights_ready"), sem("sample_weights_ready")
        s_oc, s_oe = sem("offset_products_ready"), sem("offsets_written")
        s_xd, s_xb, s_od, s_ob = (sem("padded_image_stored"), sem("block_image_loaded"), sem("offsets_stored"),
                                  sem("block_offsets_loaded"))
        s_am, s_amt, s_fl = sem("block_maxima_ready"), sem("block_maxima_turned"), sem("reach_ready")
        s_fd, s_fb = sem("reach_stored"), sem("reach_loaded")
        s_t = sem("tents_ready")
        s_gv, s_gp = sem("vector_groups_ready"), sem("gpsimd_groups_ready")
        s_tr, s_st, s_cn = sem("samples_turned"), sem("turned_samples_copied"), sem("samples_contracted")
        s_acc, s_yb, s_ys, s_ya = (sem("row_accumulated"), sem("row_copied"), sem("row_stored"),
                                   sem("convolution_loaded"))
        s_rw, s_ro, s_rs, s_rp = (sem("far_weights_ready"), sem("far_offsets_spread"), sem("far_samples_ready"),
                                  sem("far_products_ready"))
        s_any, s_fc = sem("farthest_known"), sem("far_chain")
        s_gc = sem("gpsimd_products_ready")
        s_z = sem("zeros_ready")
        s_held = sem("held")
        s_nrm = sem("normed_relu_ready")
        s_dw3, s_cz = sem("distance_weights_ready"), sem("second_padding_cleared")
        s_sq, s_box = sem("squares_ready"), sem("box_sums_ready")
        s_dp, s_d2, s_dist = sem("distance_products_ready"), sem("squared_distances_ready"), sem("distances_ready")
        s_x3, s_fin, s_res = sem("second_input_ready"), sem("final_sums_ready"), sem("results_ready")

        AHEAD = 3
        STEPS = BR * K

        block = ctx.enter_context(nc.Block())

        ORDER = [0, 4, 1, 2, 5, 3]
        PADBUF = {0: 0, 4: 3, 1: 1, 2: 2, 5: 3, 3: 0}
        BY_VECTOR, BY_TENSOR = [0, 1, 2, 3], [4, 5]

        STAT, MV, GV, NC_ = small(6 * NCH), small(4), small(4), small(4)
        ROUT, ROUTL = small(NT * E), small(NT * E)
        KO = small(NT * C)
        BN = small(4 * NT)
        BV = small(2 * NT + 1)
        S3, B3 = small(1), small(1)
        WDS = small(NT * K)
        XS = small(1)

        FMAX, FLAG, FLAG1 = small(2 * K), small(BLK), small(K * BLK + 1)
        C2 = small(1)

        T0, T1, T2, T3, T4, T5 = T_HID

        FSEL, FW = GRP, GRP + P
        FO, FE = FW + P, FW + P + 2 * BPX
        FMASK, FTY, FTX, FROW, FACC = (FE + 2 * BPX + i * BPX for i in range(5))

        SQ3 = BIG
        HS3 = SQ3 + XN
        V3 = HS3 + PW * W
        D3 = V3 + N
        XP3 = D3 + N
        OUT3 = V3
        assert XP3 + XN <= XA and OFFB == XA + XN
        def xa_rows(ch):
            return ap(XA + (ch * CR + 2) * XW + 2, [[XW, CR], [1, W]])

        def pad_rows(buf, row, col):
            return ap(buf + row * PW + col, [[PW, CR], [1, W]])

        def for_far(eng, L, body):
            flag = lambda i: eng.value_load(cols(FLAG1 + i, 1, 0, 1).bitcast(I32), min_val=0, max_val=REACH)
            with eng.If(flag(K * BLK) > 0):
                with eng.Fori(0, 3) as ky:
                    with eng.Fori(0, 3) as kx:
                        with eng.Fori(0, BLK) as blk:
                            far = flag(ky * (3 * BLK) + kx * BLK + blk)
                            with eng.If(far > 0):
                                body(ky, kx, blk, far)

        def neighbours(row, dx, j, i):
            return ap(XB + (j * XW + dx + i) + row * XW, [[HB, C], [1, W]])

        def tent(dx, m):
            return ap(TT + (dx * 9 + m) * W, [[0, C], [1, W]])

        @block.sync
        def _(sp):
            sp.dma_start(cols(XIN, N), x.rearrange("b c h w -> (b c) (h w)")).then_inc(s_x, 16)
            sp.dma_start(cols(CON, NCONST), const).then_inc(s_const, 16)
            sp.dma_start(cols(VE, NVEC), vectors).then_inc(s_vec, 16)
            sp.dma_start(cols(WR, NWREP), weights).then_inc(s_wrep, 16)
            sp.sem_inc(s_ys, 16)
            for L in range(2):
                sp.wait_ge(s_xa, NCH * (L + 1))
                sp.dma_start(xa_d.rearrange("b c n -> (b c) n"), cols(XA, XN)).then_inc(s_xd, 16)
                sp.wait_ge(s_xd, 16 * (L + 1))
                for b in range(B):
                    sp.dma_start(ap(XB, [[HB, C], [1, HB]], b * BLK, BLK),
                                 bass.AP(xa_d.tensor, b * C * XN, [[BR * XW, BLK], [XN, C], [1, HB]])
                                 ).then_inc(s_xb, 16)
                sp.wait_ge(s_oe, 2 * NCH * (L + 1) + 1)
                sp.dma_start(off_d.rearrange("a k b n -> (k b) a n"),
                             ap(OFFA, [[N, 2], [1, N]], 0, K * B)).then_inc(s_od, 16)
                sp.wait_ge(s_od, 16 * (L + 1))
                sp.dma_start(ap(OFFB, [[BPX, 2 * K], [1, BPX]]),
                             off_d.rearrange("a k b (q n) -> (b q) (a k) n", n=BPX)).then_inc(s_ob, 16)
                sp.wait_ge(s_fl, L + 1)
                sp.dma_start(flag_d, ap(FLAG, [[1, BLK]], 0, K).bitcast(I32)).then_inc(s_fd, 16)
                sp.wait_ge(s_fd, 16 * (L + 1))
                sp.dma_start(cols(FLAG1, K * BLK, 0, 1).bitcast(I32),
                             flag_d.rearrange("k q -> (k q)").unsqueeze(0)).then_inc(s_fb, 16)
                with sp.Fori(0, BR) as r:
                    sp.wait_ge(s_yb, r + (BR * L + 2))
                    sp.dma_start(y_d.rearrange("o p n -> p o n")[:, :, bass.ds(r * W, W)],
                                 ap(YB, [[W, C], [1, W]])).then_inc(s_ys, 16)
                sp.wait_ge(s_ys, 16 * BR * (L + 1) + 16)
                sp.dma_start(cols(YA, N),
                             y_d.rearrange("o (b q) n -> b o (q n)", b=B)).then_inc(s_ya, 16)
            for ch in range(NCH):
                sp.wait_ge(s_res, ch + 1)
                sp.dma_start(out.rearrange("b c h w -> (b c) (h w)")[:, ch * CH:(ch + 1) * CH],
                             cols(OUT3 + ch * CH, CH)).then_inc(s_out, 16)
            sp.wait_ge(s_out, 16 * NCH)
            sp.wait_ge(s_held, 2 * STEPS + 2 * BR)

        @block.vector
        def _(dve):
            v = nc.vector
            count = [0]

            def link(ins):
                count[0] += 1
                ins.then_inc(s_v, 1)
                dve.wait_ge(s_v, count[0])

            def channel_stats(n, src, mask_cols, shift=None):
                for ch in range(NCH):
                    ins = v.bn_stats(cols(STAT + 6 * ch, 6), cols(src + ch * CH, CH))
                link(ins)
                link(v.bn_aggr(cols(MV, 2), cols(STAT, 6 * NCH)))
                if shift is not None:
                    link(v.tensor_tensor(cols(MV, 1), cols(MV, 1), shift, ALU.add))
                v.scalar_tensor_tensor(cols(MV + 1, 1), cols(MV, 1), cols(MV, 1), cols(MV + 1, 1), ALU.mult,
                                       ALU.add).then_inc(s_stat, 1)

            def norm_coefficients(n, count_, gamma, beta, shift=None):
                dve.wait_ge(s_grp, n + 1)
                link(v.tensor_scalar(cols(GV, 2), ps(0, 0, 2), 1.0 / count_, None, ALU.mult))
                link(v.tensor_tensor(cols(GV + 2, 1), cols(GV, 1), cols(GV, 1), ALU.mult))
                link(v.tensor_tensor(cols(GV + 2, 1), cols(GV + 1, 1), cols(GV + 2, 1), ALU.subtract))
                v.tensor_scalar(cols(GV + 2, 1), cols(GV + 2, 1), EPS, None, ALU.add).then_inc(s_var, 1)
                dve.wait_ge(s_std, n + 1)
                link(v.reciprocal(cols(NC_ + 2, 1), cols(GV + 3, 1)))
                link(v.tensor_tensor(cols(NC_, 1), cols(NC_ + 2, 1), gamma, ALU.mult))
                if shift is not None:
                    link(v.tensor_tensor(cols(GV, 1), cols(GV, 1), shift, ALU.subtract))
                link(v.tensor_tensor(cols(NC_ + 3, 1), cols(GV, 1), cols(NC_, 1), ALU.mult))
                v.tensor_tensor(cols(NC_ + 1, 1), beta, cols(NC_ + 3, 1), ALU.subtract).then_inc(s_coef, 1)

            dve.wait_ge(s_x, 16)
            channel_stats(0, XIN, None)
            dve.wait_ge(s_const, 16)
            dve.wait_ge(s_vec, 16)
            dve.wait_ge(s_wrep, 16)

            def by_image(at, name, width):
                o, _ = CONST["same_image"]
                return v.tensor_tensor(ap(at, [[width, B], [1, width]]),
                                       ap(WR + WREP[name][0], [[0, B], [1, width]]),
                                       ap(CON + o, [[C, B], [0, width]]), ALU.mult)

            by_image(W_GATE, "gate", C).then_inc(s_w0, 1)
            by_image(W_UPD, "upd", C).then_inc(s_w0, 1)
            norm_coefficients(0, 2, vec("gn_w"), vec("gn_b"))
            by_image(W_HID, "w1", HID).then_inc(s_w1, 1)

            v.tensor_scalar(cols(BV, NT), vec("v1", 0, NT), EPS, None, ALU.add)
            v.tensor_scalar(cols(BV + NT, NT), vec("v2", 0, NT), EPS, None, ALU.add)
            v.tensor_scalar(cols(BV + 2 * NT, 1), vec("v3"), EPS, None, ALU.add).then_inc(s_bn, 1)

            for ch in range(NCH):
                dve.wait_ge(s_g_act, ch + 1)
                link(v.tensor_scalar(cols(T3 + ch * CH, CH), cols(T1 + ch * CH, CH), -1.0, 1.0, ALU.mult, ALU.add))
                dve.wait_ge(s_upd, ch + 1)
                v.scalar_tensor_tensor(cols(T0 + ch * CH, CH), ps(4 + ch % 4, 0, CH), vec("upd_b"),
                                       cols(T3 + ch * CH, CH), ALU.add, ALU.mult).then_inc(s_blend, 1)
            dve.wait_ge(s_blend, NCH)
            link(v.memset(ap(T1, [[W, H]]), 0.0))
            link(v.tensor_tensor_scan(cols(T4, N), cols(T1, N), cols(T0, N), 0.0, ALU.mult, ALU.add))
            link(v.tensor_tensor(ap(T5, [[H, W], [1, H]]), ap(T3, [[1, W], [W, H]]), ap(T4, [[1, W], [W, H]]),
                                 ALU.mult))
            dve.wait_ge(s_a, NCH)
            link(v.memset(ap(T2, [[H, W]]), 0.0))
            link(v.tensor_tensor_scan(cols(T1, N), cols(T2, N), cols(T5, N), 0.0, ALU.mult, ALU.add))
            v.tensor_tensor(ap(XIN, [[W, H], [1, W]]), ap(XIN, [[W, H], [1, W]]), ap(T1, [[1, H], [H, W]]),
                            ALU.add).then_inc(s_xsum, 1)

            dve.wait_ge(s_xsum, 1)
            link(v.tensor_reduce(cols(XS, 1), cols(XIN, N), AX.X, ALU.add))
            o = CONST["same_image"][0]
            v.tensor_scalar(ap(W_OUT, [[HID, B], [1, HID]]), ap(CON + o, [[C, B], [0, HID]]), cols(XS, 1), None,
                            ALU.mult).then_inc(s_pool_w, 1)
            dve.wait_ge(s_bnstd, 1)
            link(v.reciprocal(cols(BV, 2 * NT + 1), cols(BV, 2 * NT + 1)))
            link(v.tensor_tensor(cols(BN, NT), cols(BV, NT), vec("g1", 0, NT), ALU.mult))
            link(v.tensor_tensor(cols(BN + 2 * NT, NT), cols(BV + NT, NT), vec("g2", 0, NT), ALU.mult))
            link(v.tensor_tensor(cols(S3, 1), cols(BV + 2 * NT, 1), vec("g3"), ALU.mult))
            link(v.tensor_tensor(cols(BN + NT, NT), vec("m1", 0, NT), cols(BN, NT), ALU.mult))
            link(v.tensor_tensor(cols(BN + 3 * NT, NT), vec("m2", 0, NT), cols(BN + 2 * NT, NT), ALU.mult))
            link(v.tensor_tensor(cols(B3, 1), vec("m3"), cols(S3, 1), ALU.mult))
            link(v.tensor_tensor(cols(BN + NT, NT), vec("b1", 0, NT), cols(BN + NT, NT), ALU.subtract))
            link(v.tensor_tensor(cols(BN + 3 * NT, NT), vec("b2", 0, NT), cols(BN + 3 * NT, NT), ALU.subtract))
            link(v.tensor_tensor(cols(B3, 1), vec("b3"), cols(B3, 1), ALU.subtract))
            v.tensor_tensor(ap(WDS, [[K, NT], [1, K]]), ap(VE + VEC["wd"][0], [[K, NT], [1, K]]),
                            ap(BN + 2 * NT, [[1, NT], [0, K]]), ALU.mult).then_inc(s_bnc, 1)
            dve.wait_ge(s_bnc, 1)

            def diagonals(t):
                v.tensor_tensor(ap(W_DIAG, [[P, K], [1, P]]), ap(CON + CONST["ident"][0], [[0, K], [1, P]]),
                                ap(WDS + t * K, [[1, K], [0, P]]), ALU.mult).then_inc(s_diag, 1)

            diagonals(BY_TENSOR[0])
            dve.wait_ge(s_route, 1)
            v.scalar_tensor_tensor(ap(ROUTL, [[E, NT], [1, E]]), ap_ps(7, [[E, NT], [1, E]]), 1.0 / N,
                                   ap(VE + VEC["br"][0], [[0, NT], [1, E]]), ALU.mult, ALU.add).then_inc(s_rl, 1)
            dve.wait_ge(s_rsig, 1)

            def mix_experts():
                link(v.tensor_tensor(ap(W_OUT, [[E * C, NT], [C, E], [1, C]]),
                                     ap(WR + WREP["we"][0], [[E * C, NT], [C, E], [1, C]]),
                                     ap(ROUT, [[E, NT], [1, E], [0, C]]), ALU.mult))
                link(v.tensor_reduce(ap(KO, [[C, NT], [1, C]]), ap(W_OUT, [[E * C, NT], [1, C], [C, E]]), AX.X,
                                     ALU.add))
                link(v.memset(cols(W_OUT, NT * P), 0.0))
                for t in range(NT):
                    for p0 in range(0, P, 32):
                        b = (t * P + p0) // HID
                        ins = v.tensor_copy(ap(W_OUT + t * P + b * C, [[1, C]], p0, 32),
                                            ap(KO + t * C, [[1, C]], p0, 32))
                ins.then_inc(s_wo, 1)

            mix_experts()

            def depthwise(eng, link_, t, clip=True):
                src, dst = T_PAD[PADBUF[t]], T_HID[t]
                whole = lambda at, dy, dx: ap(at + dy * PW + dx, [[PW, H], [1, W]])
                full = ap(dst, [[W, H], [1, W]])
                link_(eng.tensor_scalar(full, whole(src, 0, 0), cols(WDS + t * K, 1), cols(BN + 3 * NT + t, 1),
                                        ALU.mult, ALU.add))
                for k in range(1, K):
                    link_(eng.scalar_tensor_tensor(full, whole(src, k // 3, k % 3), cols(WDS + t * K + k, 1), full,
                                                   ALU.mult, ALU.add))
                return eng.tensor_scalar(cols(dst, N), cols(dst, N), 0.0, 6.0, ALU.max, ALU.min)

            for i, t in enumerate(BY_VECTOR):
                dve.wait_ge(s_relu, NCH * (ORDER.index(t) + 1))
                link(v.tensor_scalar(cols(T_PAD[PADBUF[t]], PADN), cols(T_PAD[PADBUF[t]], PADN), 6.0, None, ALU.min))
                depthwise(v, link, t).then_inc(s_dwv, 1)
                if i == 0:
                    dve.wait_ge(s_dw, NCH)
                    diagonals(BY_TENSOR[1])
            dve.wait_ge(s_dwv, len(BY_VECTOR))
            link(v.memset(cols(XA, XN), 0.0))
            for i, t in enumerate(BY_TENSOR):
                dve.wait_ge(s_dwa, NCH * (i + 1))
                v.tensor_scalar(cols(T_HID[t], N), cols(T_HID[t], N), 6.0, None, ALU.min).then_inc(s_hid, 1)
            for ch in range(NCH):
                dve.wait_ge(s_proj, ch + 1)
                v.tensor_scalar(cols(T_PAD[2] + (ch % 2) * CH, CH), ps(ch % 4, 0, CH), cols(S3, 1), cols(B3, 1),
                                ALU.mult, ALU.add).then_inc(s_proj_free, 1)
                dve.wait_ge(s_proj_free, ch + 1)
                v.tensor_tensor(xa_rows(ch), ap(T_PAD[2] + (ch % 2) * CH, [[W, CR], [1, W]]),
                                ap(XIN + ch * CH, [[W, CR], [1, W]]), ALU.add).then_inc(s_xa, 1)

            def sample_weights(L):
                if L == 0:
                    v.memset(cols(ZERO, P), 0.0).then_inc(s_z, 1)
                v.tensor_tensor(ap(W_OFF, [[K * B, 2 * K], [B, K], [1, B]]),
                                ap(WR + WREP[f"ow{L}"][0], [[K, 2 * K], [1, K], [0, B]]),
                                ap(CON + CONST["same_image"][0], [[0, 2 * K], [0, K], [C, B]]),
                                ALU.mult).then_inc(s_ow, 1)
                v.tensor_tensor(ap(W_SAMP, [[8, K * C], [1, 8]]),
                                ap(WR + WREP[f"sw{L}"][0], [[1, K * C], [0, 8]]),
                                ap(CON + CONST["px8"][0], [[0, K * C], [1, 8]]), ALU.mult).then_inc(s_sw, 1)

            def reach(L):
                dve.wait_ge(s_ob, 16 * (L + 1))
                link(v.tensor_reduce(cols(FMAX, 2 * K), ap(OFFB, [[BPX, 2 * K], [1, BPX]]), AX.X, ALU.max,
                                     apply_absolute_value=True))
                v.tensor_tensor(cols(FMAX, K), cols(FMAX, K), cols(FMAX + K, K), ALU.max).then_inc(s_am, 1)
                dve.wait_ge(s_amt, L + 1)
                link(v.tensor_reduce(cols(FLAG, BLK, 0, K), bass.AP(psum, 0, [[8 * CH, K], [1, BLK], [BLK, B]]),
                                     AX.X, ALU.max))
                link(v.tensor_scalar(cols(FMAX, BLK, 0, K), cols(FLAG, BLK, 0, K), REACH - 1.0, 1.0, ALU.min,
                                     ALU.add))
                link(v.scalar_tensor_tensor(cols(FMAX, BLK, 0, K), cols(FLAG, BLK, 0, K), 1.0,
                                            cols(FMAX, BLK, 0, K), ALU.is_gt, ALU.mult))
                v.tensor_copy(cols(FLAG, BLK, 0, K).bitcast(I32), cols(FMAX, BLK, 0, K)).then_inc(s_fl, 1)

            def grp(dx, g):
                return ap(GRP + (dx * NG + g) * GN_, [[W, C], [1, W]])

            def tents(L, at):
                plane = lambda step: ap(TXY + step * K * W, [[3 * K * W, 2], [1, K * W]])
                wide = lambda step: ap(TXY + step * K * W, [[3 * K * W, 2], [W, K], [1, W]])
                off4 = ap(OFFB + at, [[K * BPX, 2], [BPX, K], [1, W]])
                v.tensor_scalar(wide(0), off4, -1.0, 0.0, ALU.mult, ALU.max)
                link(v.tensor_scalar(wide(2), off4, 0.0, None, ALU.max))
                link(v.tensor_tensor(plane(1), plane(0), plane(2), ALU.max))
                near = cols(TMP, K * W)
                link(v.tensor_tensor(near, cols(TXY + K * W, K * W), cols(TXY + 4 * K * W, K * W), ALU.max))
                link(v.tensor_scalar(near, near, 1.0, None, ALU.is_le))
                link(v.tensor_scalar(plane(1), plane(1), -1.0, 1.0, ALU.mult, ALU.add))
                count[0] += 1
                v.tensor_tensor(ap(TXY, [[K * W, 3], [1, K * W]]), ap(TXY, [[K * W, 3], [1, K * W]]),
                                ap(TMP, [[0, 3], [1, K * W]]), ALU.mult).then_inc(s_v, 1)
                dve.wait_ge(s_v, count[0])
                dve.sem_inc(s_held, 1)

            def sample_row(L, r):
                base = count[0]
                count[0] = base + r * ROW_LINKS
                tents(L, r * W)
                row_start = count[0]
                with dve.Fori(0, 3) as dy:
                    count[0] = row_start + dy * DY_LINKS
                    n = r * 3 + dy
                    for dx in range(3):
                        step = n * 3 + (dx + STEPS * L)
                        dve.wait_ge(s_gp, step + 1)
                        v.tensor_tensor(
                            ap(TT + dx * 9 * W, [[3 * W, 3], [W, 3], [1, W]]),
                            ap(TXY + dx * W + dy * (3 * W), [[K * W, 3], [0, 3], [1, W]]),
                            ap(TXY + 3 * K * W + dx * W + dy * (3 * W), [[0, 3], [K * W, 3], [1, W]]),
                            ALU.mult).then_inc(s_t, 1)
                        dve.wait_ge(s_t, step + 1)
                        dve.wait_ge(s_tr, step + 1)

                        def product(m, dst):
                            j, i = divmod(m, 3)
                            return v.tensor_tensor(dst, neighbours(r + dy, dx, j, i), tent(dx, m), ALU.mult)

                        t0, t1 = ap(TMP, [[W, C], [1, W]]), ap(TMP + GN_, [[W, C], [1, W]])
                        product(0, grp(dx, 0))
                        product(1, t0)
                        product(2, grp(dx, 1))
                        product(3, t1)
                        link(product(4, grp(dx, 2)))
                        v.tensor_tensor(grp(dx, 0), grp(dx, 0), t0, ALU.add)
                        link(v.tensor_tensor(grp(dx, 1), grp(dx, 1), t1, ALU.add))
                        link(product(5, t0))
                        v.tensor_tensor(grp(dx, 2), grp(dx, 2), t0, ALU.add).then_inc(s_gv, 1)
                count[0] = base

            ROW_LINKS, DY_LINKS = 6 + 3 * 9, 9

            def far_link(ins, last=False):
                ins.then_inc(s_fc, 1)
                if last:
                    dve.wait_ge(s_fc, dve.snap(far_chain) + 1)
                dve.reg_add(far_chain, far_chain, 1)
                if not last:
                    dve.wait_ge(s_fc, dve.snap(far_chain))

            far_chain = dve.alloc_register("far_chain")
            far_done = dve.alloc_register("far_done_by_vector")
            dve.reg_mov(far_chain, 0)
            dve.reg_mov(far_done, 0)

            def far_block(L, ky, kx, blk, far):
                rows = ap(CON + CONST["rows"][0], [[1, BR], [0, W]])
                columns = ap(CON + CONST["columns"][0], [[0, BR], [1, W]])
                step_at = lambda i: cols(CON + CONST["steps"][0] + i, 1)
                img = lambda at: ap(at, [[W, BR], [1, W]])
                v.tensor_scalar(cols(FSEL, P), con("same_image"), cols(CON + CONST["blkhot"][0] + blk, 1), None,
                                ALU.mult)
                v.tensor_tensor(ap(FW, [[C, B], [1, C]]),
                                ap(WR + WREP[f"cw{L}"][0] + kx * C + ky * (3 * C), [[0, B], [1, C]]),
                                ap(CON + CONST["same_image"][0], [[C, B], [0, C]]), ALU.mult).then_inc(s_rw, 1)
                dve.reg_add(far_done, far_done, 1)
                dve.wait_ge(s_ro, dve.snap(far_done))
                far_link(v.tensor_copy(cols(FO, 2 * BPX), ps(0, 0, 2 * BPX)))
                far_link(v.scalar_tensor_tensor(cols(FE, 2 * BPX), cols(FO, 2 * BPX), -1.0, cols(FO, 2 * BPX),
                                                ALU.mult, ALU.max))
                far_link(v.tensor_tensor(cols(FMASK, BPX), cols(FE, BPX), cols(FE + BPX, BPX), ALU.max))
                far_link(v.tensor_scalar(cols(FMASK, BPX), cols(FMASK, BPX), 1.0, None, ALU.is_gt))
                for off, at, plane, size in ((FO, step_at(blk * BR + ky + (REACH - 1)), rows, H),
                                             (FO + BPX, step_at(kx + (REACH - 1)), columns, W)):
                    far_link(v.tensor_scalar(cols(off, BPX), cols(off, BPX), at, None, ALU.add))
                    far_link(v.tensor_tensor(img(off), img(off), plane, ALU.add))
                    far_link(v.tensor_scalar(cols(off, BPX), cols(off, BPX), -1.0, float(size), ALU.max, ALU.min))
                    far_link(v.tensor_tensor(img(off), img(off), plane, ALU.subtract))
                    far_link(v.tensor_scalar(cols(off, BPX), cols(off, BPX), at, None, ALU.subtract))

                def tent_before_relu(dst, off, i):
                    far_link(v.tensor_scalar(cols(dst, BPX), cols(off, BPX), step_at(i), None, ALU.subtract))
                    far_link(v.scalar_tensor_tensor(cols(dst, BPX), cols(dst, BPX), -1.0, cols(dst, BPX), ALU.mult,
                                                    ALU.max))
                    far_link(v.tensor_scalar(cols(dst, BPX), cols(dst, BPX), -1.0, 1.0, ALU.mult, ALU.add))

                far_link(v.memset(cols(FACC, BPX), 0.0), last=True)
                with dve.Fori(REACH - far, REACH + far + 1) as j:
                    tent_before_relu(FTY, FO, j)
                    far_link(v.scalar_tensor_tensor(cols(FTY, BPX), cols(FTY, BPX), 0.0, cols(FMASK, BPX), ALU.max,
                                                    ALU.mult))
                    far_link(v.memset(cols(FROW, BPX), 0.0), last=True)
                    with dve.Fori(REACH - far, REACH + far + 1) as i:
                        tent_before_relu(FTX, FO + BPX, i)
                        at = (blk * BR + ky + j + (1 - REACH)) * XW + kx + i + (1 - REACH)
                        far_link(v.scalar_tensor_tensor(img(FTX), img(FTX), 0.0, ap(XA + at, [[XW, BR], [1, W]]),
                                                        ALU.max, ALU.mult))
                        far_link(v.tensor_tensor(cols(FROW, BPX), cols(FROW, BPX), cols(FTX, BPX), ALU.add), last=True)
                    far_link(v.tensor_tensor(cols(FROW, BPX), cols(FROW, BPX), cols(FTY, BPX), ALU.mult))
                    far_link(v.tensor_tensor(cols(FACC, BPX), cols(FACC, BPX), cols(FROW, BPX), ALU.add), last=True)
                dve.sem_inc(s_rs, 1)
                dve.wait_ge(s_rp, dve.snap(far_done))
                far_link(v.tensor_tensor(cols(YA + blk * BPX, BPX), cols(YA + blk * BPX, BPX), ps(1, 0, BPX),
                                         ALU.add), last=True)

            def far_samples(L):
                dve.wait_ge(s_fb, 16 * (L + 1))
                v.tensor_reduce(cols(FLAG1 + K * BLK, 1, 0, 1).bitcast(I32), cols(FLAG1, K * BLK, 0, 1).bitcast(I32),
                                AX.X, ALU.max).then_inc(s_any, 1)
                dve.wait_ge(s_any, L + 1)
                for_far(dve, L, lambda *a: far_block(L, *a))

            def layer2(L):
                sample_weights(L)
                dve.wait_ge(s_sw, L + 1)
                reach(L)
                dve.wait_ge(s_xb, 16 * B * (L + 1))
                dve.wait_ge(s_od, 16 * (L + 1))
                with dve.Fori(0, BR) as r:
                    sample_row(L, r)
                count[0] = count[0] + BR * ROW_LINKS
                dve.wait_ge(s_ya, 16 * (L + 1))
                far_samples(L)
                channel_stats(1 + L, YA, None, vec(f"db{L}"))
                norm_coefficients(1 + L, C, vec(f"dg{L}"), vec(f"dbe{L}"), vec(f"db{L}"))
                for ch in range(NCH):
                    dve.wait_ge(s_nrm, NCH * L + ch + 1)
                    v.tensor_tensor(xa_rows(ch), xa_rows(ch), ap(YA + ch * CH, [[W, CR], [1, W]]),
                                    ALU.add).then_inc(s_xa, 1)

            dve.wait_ge(s_proj, NCH)
            for L in range(2):
                layer2(L)

            def distance(L):
                src = XA if L == 0 else XP3
                o = WR + WREP[f"dt{L}"][0]
                link(v.tensor_scalar(cols(o, K * C), cols(o, K * C), -2.0, None, ALU.mult))
                v.tensor_tensor(ap(W_DT, [[P, K], [C, B], [1, C]]), ap(o, [[C, K], [0, B], [1, C]]),
                                ap(CON + CONST["same_image"][0], [[0, K], [C, B], [0, C]]),
                                ALU.mult).then_inc(s_dw3, 1)
                link(v.tensor_tensor_reduce(cols(V3, K * C), cols(WR + WREP[f"cn{L}"][0], K * C),
                                            cols(WR + WREP[f"cn{L}"][0], K * C), 1.0, 0.0, ALU.mult, ALU.add,
                                            cols(C2, 1)))
                dve.wait_ge(s_sq, L + 1)
                sq = lambda dx: ap(SQ3 + XW + 1 + dx, [[XW, PW], [1, W]])
                hs = ap(HS3, [[W, PW], [1, W]])
                link(v.tensor_tensor(hs, sq(0), sq(1), ALU.add))
                link(v.tensor_tensor(hs, hs, sq(2), ALU.add))
                link(v.tensor_tensor(cols(V3, N), cols(HS3, N), cols(HS3 + W, N), ALU.add))
                v.tensor_tensor(cols(V3, N), cols(V3, N), cols(HS3 + 2 * W, N), ALU.add).then_inc(s_box, 1)
                for ch in range(NCH):
                    dve.wait_ge(s_dp, NCH * L + ch + 1)
                    v.tensor_scalar(cols(D3 + ch * CH, CH), ps(ch % 8, 0, CH), cols(C2, 1), D2_EPS, ALU.add,
                                    ALU.max).then_inc(s_d2, 1)
                for ch in range(NCH):
                    dve.wait_ge(s_dist, NCH * L + ch + 1)
                    ins = v.bn_stats(cols(STAT + 6 * ch, 6), cols(D3 + ch * CH, CH))
                link(ins)
                link(v.bn_aggr(cols(MV, 2), cols(STAT, 6 * NCH)))
                v.scalar_tensor_tensor(cols(MV + 1, 1), cols(MV, 1), cols(MV, 1), cols(MV + 1, 1), ALU.mult,
                                       ALU.add).then_inc(s_stat, 1)
                norm_coefficients(3 + L, B, vec(f"gamma{L}"), vec(f"beta{L}"))

            dve.wait_ge(s_xa, 3 * NCH)
            distance(0)
            distance(1)
            dve.wait_ge(s_coef, 5)
            for ch in range(NCH):
                v.scalar_tensor_tensor(ap(D3 + ch * CH, [[W, CR], [1, W]]), ap(D3 + ch * CH, [[W, CR], [1, W]]),
                                       cols(NC_, 1), xa_rows(ch), ALU.mult, ALU.add).then_inc(s_fin, 1)

        @block.scalar
        def _(act):
            a = nc.scalar

            def deviation(n):
                act.wait_ge(s_var, n + 1)
                a.activation(cols(GV + 3, 1), cols(GV + 2, 1), ACT.Sqrt).then_inc(s_std, 1)

            deviation(0)
            act.wait_ge(s_bn, 1)
            a.activation(cols(BV, 2 * NT + 1), cols(BV, 2 * NT + 1), ACT.Sqrt).then_inc(s_bnstd, 1)
            act.wait_ge(s_coef, 1)
            for ch in range(NCH):
                a.activation(cols(T0 + ch * CH, CH), cols(XIN + ch * CH, CH), ACT.Identity, bias=cols(NC_ + 1, 1),
                             scale=cols(NC_, 1)).then_inc(s_hn, 1)
            for ch in range(NCH):
                act.wait_ge(s_gate, ch + 1)
                a.activation(cols(T1 + ch * CH, CH), ps(ch % 4, 0, CH), ACT.Sigmoid,
                             bias=vec("gate_b")).then_inc(s_g_act, 1)
                a.activation(ap(T2 + ch * CR, [[1, CR], [H, W]]), ap_ps(ch % 4, [[W, CR], [1, W]]), ACT.Sigmoid,
                             bias=vec("gate_b")).then_inc(s_a, 1)

            act.wait_ge(s_rl, 1)
            a.activation(cols(ROUT, NT * E), cols(ROUTL, NT * E), ACT.Sigmoid).then_inc(s_rsig, 1)
            act.wait_ge(s_bnc, 1)
            act.wait_ge(s_padz, 1)

            def hidden(q):
                t = ORDER[q]
                if t == 3:
                    act.wait_ge(s_dwv, 1)
                if t == 5:
                    act.wait_ge(s_dw, NCH)
                for ch in range(NCH):
                    act.wait_ge(s_c1, NCH * q + ch + 1)
                    a.activation(pad_rows(T_PAD[PADBUF[t]], ch * CR + 1, 1), ap_ps(ch % 4, [[W, CR], [1, W]]),
                                 ACT.Relu, bias=cols(BN + NT + t, 1), scale=cols(BN + t, 1)).then_inc(s_relu, 1)

            def depthwise_relu(i):
                t = BY_TENSOR[i]
                for ch in range(NCH):
                    act.wait_ge(s_dw, NCH * i + ch + 1)
                    a.activation(cols(T_HID[t] + ch * CH, CH), ps(4 + ch % 4, 0, CH), ACT.Relu,
                                 bias=cols(BN + 3 * NT + t, 1)).then_inc(s_dwa, 1)

            for q in range(4):
                hidden(q)
            depthwise_relu(0)
            hidden(4)
            hidden(5)
            depthwise_relu(1)

            a.sem_inc(s_st, AHEAD)
            a.sem_inc(s_oe, 1)
            a.sem_inc(s_yb, 1)
            for L in range(2):
                with act.Fori(0, NCH // 2) as i:
                    for u in range(2):
                        for ax in range(2):
                            act.wait_ge(s_oc, i * 4 + (2 * u + ax + 1 + 2 * NCH * L))
                            a.activation(ap(OFFA + ax * N + u * CH + i * (2 * CH), [[1, CH]], 0, K * B),
                                         ps(2 * u + ax, 0, CH, K * B), ACT.Identity,
                                         bias=vec("obyx"[:2] + "yx"[ax] + str(L), 0, 1, K * B)).then_inc(s_oe, 1)
                with act.Fori(0, BR) as r:
                    with act.Fori(0, 3) as dy:
                        for dx in range(3):
                            step = r * 9 + dy * 3 + (dx + STEPS * L)
                            act.wait_ge(s_tr, step + 1 + AHEAD)
                            act.wait_ge(s_cn, step + 1)
                            a.activation(cols(ST + dx * GN_, GN_), ap_ps(2 * dx, [[1, GN_]]),
                                         ACT.Copy).then_inc(s_st, 1)
                    act.wait_ge(s_acc, r + (BR * L + 1))
                    act.wait_ge(s_ys, r * 16 + (16 * BR * L + 16))
                    a.activation(ap(YB, [[1, 8], [W, C], [8, 8]]), ap_ps(6, [[P, 8], [8, C], [1, 8]]),
                                 ACT.Copy).then_inc(s_yb, 1)
                deviation(1 + L)
                act.wait_ge(s_coef, 2 + L)
                for ch in range(NCH):
                    a.activation(cols(YA + ch * CH, CH), cols(YA + ch * CH, CH), ACT.Relu, bias=cols(NC_ + 1, 1),
                                 scale=cols(NC_, 1)).then_inc(s_nrm, 1)

            for L in range(2):
                if L == 0:
                    act.wait_ge(s_xa, 3 * NCH)
                    a.activation(cols(SQ3, XN), cols(XA, XN), ACT.Square).then_inc(s_sq, 1)
                else:
                    act.wait_ge(s_x3, NCH)
                    a.activation(cols(SQ3, XN), cols(XP3, XN), ACT.Square).then_inc(s_sq, 1)
                for ch in range(NCH):
                    act.wait_ge(s_d2, NCH * L + ch + 1)
                    a.activation(cols(D3 + ch * CH, CH), cols(D3 + ch * CH, CH), ACT.Sqrt).then_inc(s_dist, 1)
                deviation(3 + L)
                act.wait_ge(s_coef, 4 + L)
                if L == 0:
                    act.wait_ge(s_cz, 1)
                    for ch in range(NCH):
                        a.activation(ap(XP3 + (ch * CR + 2) * XW + 2, [[XW, CR], [1, W]]),
                                     ap(D3 + ch * CH, [[W, CR], [1, W]]), ACT.Relu, bias=cols(NC_ + 1, 1),
                                     scale=cols(NC_, 1)).then_inc(s_x3, 1)
                else:
                    for ch in range(NCH):
                        act.wait_ge(s_fin, ch + 1)
                        a.activation(cols(OUT3 + ch * CH, CH), cols(D3 + ch * CH, CH), ACT.Relu,
                                     bias=cols(NC_ + 1, 1)).then_inc(s_res, 1)

        @block.tensor
        def _(pe):
            t_ = nc.tensor

            def group_sums(n, mask):
                pe.wait_ge(s_stat, n + 1)
                t_.matmul(ps(0, 0, 2), con(mask), cols(MV, 2), start=True, stop=True).then_inc(s_grp, 1)

            pe.wait_ge(s_const, 16)
            group_sums(0, "same_pair")
            pe.wait_ge(s_w0, 2)
            for ch in range(NCH):
                pe.wait_ge(s_hn, ch + 1)
                if ch >= 4:
                    pe.wait_ge(s_a, ch - 3)
                else:
                    pe.wait_ge(s_coef, 1)
                t_.matmul(ps(ch % 4, 0, CH), cols(W_GATE, P), cols(T0 + ch * CH, CH), start=True,
                          stop=True).then_inc(s_gate, 1)
                if ch >= 4:
                    pe.wait_ge(s_blend, ch - 3)
                t_.matmul(ps(4 + ch % 4, 0, CH), cols(W_UPD, P), cols(T0 + ch * CH, CH), start=True,
                          stop=True).then_inc(s_upd, 1)

            pe.wait_ge(s_pool_w, 1)
            pe.wait_ge(s_blend, NCH)
            for t in range(NT):
                ins = t_.matmul(ps(7, t * E, E), cols(W_OUT + t * P, P), cols(WR + WREP["wr"][0], E),
                                start=(t == 0), stop=True, skip_group_check=True)
            ins.then_inc(s_route, 1)
            pe.wait_ge(s_w1, 1)
            pe.wait_ge(s_xsum, 1)
            pe.wait_ge(s_a, NCH)

            def hidden(q):
                t = ORDER[q]
                for ch in range(NCH):
                    n = NCH * q + ch
                    if n >= 4:
                        pe.wait_ge(s_relu, n - 3)
                    t_.matmul(ps(ch % 4, 0, CH), cols(W_HID + t * P, P), cols(XIN + ch * CH, CH), start=True,
                              stop=True).then_inc(s_c1, 1)

            def depthwise(i):
                t = BY_TENSOR[i]
                pe.wait_ge(s_diag, i + 1)
                pe.wait_ge(s_clip_g, i + 1)
                if i == 0:
                    pe.wait_ge(s_rl, 1)
                for ch in range(NCH):
                    n = NCH * i + ch
                    if n >= 4:
                        pe.wait_ge(s_dwa, n - 3)
                    for k in range(K):
                        ins = t_.matmul(ps(4 + ch % 4, 0, CH), cols(W_DIAG + k * P, P),
                                        pad_rows(T_PAD[PADBUF[t]], ch * CR + k // 3, k % 3), start=(k == 0),
                                        stop=(k == K - 1))
                    ins.then_inc(s_dw, 1)

            for q in range(4):
                hidden(q)
            depthwise(0)
            hidden(4)
            hidden(5)
            depthwise(1)
            pe.wait_ge(s_wo, 1)
            pe.wait_ge(s_dwv, len(BY_VECTOR))
            pe.wait_ge(s_hid, 2)
            pe.wait_ge(s_relu, NCH * NT)
            for ch in range(NCH):
                if ch >= 4:
                    pe.wait_ge(s_proj_free, ch - 3)
                for t in range(NT):
                    ins = t_.matmul(ps(ch % 4, 0, CH), cols(W_OUT + t * P, P), cols(T_HID[t] + ch * CH, CH),
                                    start=(t == 0), stop=(t == NT - 1))
                ins.then_inc(s_proj, 1)

            pe.wait_ge(s_z, 1)
            far_done = pe.alloc_register("far_done_by_tensor")
            pe.reg_mov(far_done, 0)
            t_.sem_inc(s_tr, AHEAD)
            t_.sem_inc(s_cn, AHEAD)
            for L in range(2):
                pe.wait_ge(s_xa, NCH * (L + 1))
                pe.wait_ge(s_ow, L + 1)
                with pe.Fori(0, NCH // 2) as i:
                    pe.wait_ge(s_oe, i * 4 + (2 * NCH * L + 1))
                    for u in range(2):
                        for ax in range(2):
                            for k in range(K):
                                row = i * (2 * CR * XW) + ((u * CR + 1 + k // 3) * XW + 1 + k % 3)
                                ins = t_.matmul(ps(2 * u + ax, 0, CH, K * B),
                                                cols(W_OFF + (k * 2 + ax) * K * B, K * B),
                                                ap(XA + row, [[XW, CR], [1, W]]), start=(k == 0),
                                                stop=(k == K - 1))
                            ins.then_inc(s_oc, 1)
                pe.wait_ge(s_am, L + 1)
                pe.wait_ge(s_oe, 2 * NCH * (L + 1) + 1)
                t_.matmul(ps(0, 0, P, K), cols(FMAX, K), con("ident"), start=True, stop=True).then_inc(s_amt, 1)
                pe.wait_ge(s_sw, L + 1)
                pe.wait_ge(s_fl, L + 1)
                with pe.Fori(0, BR) as r:
                    pe.wait_ge(s_yb, r + (BR * L + 1))
                    for h in range(2):
                        t_.matmul(ps(6 + h, 0, CH), cols(ZERO, P), ap(ZERO, [[0, CH // P], [1, P]]), start=True, stop=False,
                                  skip_group_check=True)
                    with pe.Fori(0, 3) as dy:
                        def turn(dx):
                            step = r * 9 + dy * 3 + (dx + STEPS * L)
                            pe.wait_ge(s_gv, step + 1)
                            pe.wait_ge(s_gp, step + 1 + AHEAD)
                            pe.wait_ge(s_st, step + 1)
                            for s_ in range(8):
                                for g in range(NG):
                                    ins = t_.matmul(ps(2 * dx + s_ // 4, (s_ % 4) * P, P),
                                                    ap(GRP + (dx * NG + g) * GN_ + s_, [[8, P]]),
                                                    con("ident"), start=(g == 0 and s_ % 4 == 0),
                                                    stop=(g == NG - 1), skip_group_check=True)
                            ins.then_inc(s_tr, 1)

                        def contract(dx):
                            step = r * 9 + dy * 3 + (dx + STEPS * L)
                            pe.wait_ge(s_st, step + 1 + AHEAD)
                            for s_ in range(8):
                                ins = t_.matmul(ps(6 + s_ // 4, (s_ % 4) * P, P), cols(ST + dx * GN_ + s_ * P, P),
                                                cols(W_SAMP + dx * P + dy * (3 * P), P), start=False, stop=False,
                                                skip_group_check=True)
                            ins.then_inc(s_cn, 1)

                        turn(0)
                        turn(1)
                        contract(0)
                        turn(2)
                        contract(1)
                        contract(2)
                    for h in range(2):
                        ins = t_.matmul(ps(6 + h, 0, CH), cols(ZERO, P), ap(ZERO, [[0, CH // P], [1, P]]), start=False, stop=True,
                                        skip_group_check=True)
                    ins.then_inc(s_acc, 1)

                def far_block(ky, kx, blk, far):
                    pe.reg_add(far_done, far_done, 1)
                    pe.wait_ge(s_rw, pe.snap(far_done))
                    for ax in range(2):
                        ins = t_.matmul(ps(0, ax * BPX, BPX), cols(FSEL, P),
                                        cols(OFFB + ax * K * BPX + kx * BPX + ky * (3 * BPX), BPX), start=(ax == 0),
                                        stop=True, skip_group_check=True)
                    ins.then_inc(s_ro, 1)
                    pe.wait_ge(s_rs, pe.snap(far_done))
                    t_.matmul(ps(1, 0, BPX), cols(FW, P), cols(FACC, BPX), start=True, stop=True).then_inc(s_rp, 1)

                pe.wait_ge(s_any, L + 1)
                pe.wait_ge(s_yb, BR * (L + 1) + 1)
                for_far(pe, L, far_block)
                group_sums(1 + L, "same_image")

            for L in range(2):
                src = XA if L == 0 else XP3
                if L == 0:
                    pe.wait_ge(s_xa, 3 * NCH)
                else:
                    pe.wait_ge(s_x3, NCH)
                pe.wait_ge(s_dw3, L + 1)
                for ch in range(NCH):
                    for k in range(K):
                        t_.matmul(ps(ch, 0, CH), cols(W_DT + k * P, P),
                                  ap(src + (ch * CR + 1 + k // 3) * XW + 1 + k % 3, [[XW, CR], [1, W]]),
                                  start=(k == 0), stop=False)
                    if ch == 0:
                        pe.wait_ge(s_box, L + 1)
                    t_.matmul(ps(ch, 0, CH), con("same_image"), cols(V3 + ch * CH, CH), start=False,
                              stop=True).then_inc(s_dp, 1)
                pe.wait_ge(s_d2, NCH * (L + 1))
                group_sums(3 + L, "same_channel")

        @block.gpsimd
        def _(pool):
            g = nc.gpsimd
            count = [0]

            def link(ins):
                count[0] += 1
                ins.then_inc(s_g, 1)
                pool.wait_ge(s_g, count[0])

            for buf in T_PAD[:3]:
                g.memset(cols(buf, PADN), 0.0)
            g.memset(cols(T_PAD[3], PADN), 0.0).then_inc(s_padz, 1)

            def clip(t, at):
                pool.wait_ge(s_relu, NCH * (ORDER.index(t) + 1))
                return g.tensor_scalar(cols(T_PAD[PADBUF[t]], PADN), cols(T_PAD[PADBUF[t]], PADN), 6.0, None, ALU.min)

            pool.wait_ge(s_padz, 1)
            for t in BY_TENSOR:
                clip(t, 0).then_inc(s_clip_g, 1)

            g.sem_inc(s_gp, AHEAD)
            for L in range(2):
                pool.wait_ge(s_xb, 16 * B * (L + 1))
                pool.wait_ge(s_od, 16 * (L + 1))
                with pool.Fori(0, BR) as r:
                    with pool.Fori(0, 3) as dy:
                        n = r * 3 + dy
                        for dx in range(3):
                            after = n * 3 + (dx + STEPS * L + 1)
                            pool.wait_ge(s_t, after)
                            pool.wait_ge(s_tr, after)
                            pool.wait_ge(s_gp, n * 3 + (dx + STEPS * L + AHEAD))
                            pool.sem_inc(s_held, 1)
                            grp = lambda q: ap(GRP + (dx * NG + q) * GN_, [[W, C], [1, W]])
                            t2 = ap(TMP + 2 * GN_, [[W, C], [1, W]])
                            for m, dst in ((6, grp(3)), (7, t2), (8, grp(4))):
                                ins = g.tensor_tensor(dst, neighbours(r + dy, dx, m // 3, m % 3), tent(dx, m),
                                                      ALU.mult)
                            ins.then_inc(s_gc, 1)
                            pool.wait_ge(s_gc, after)
                            g.tensor_tensor(grp(3), grp(3), t2, ALU.add).then_inc(s_gp, 1)

            pool.wait_ge(s_xa, 3 * NCH)
            g.memset(cols(XP3, XN), 0.0).then_inc(s_cz, 1)

def layout(i):
    f = lambda a: np.ascontiguousarray(np.asarray(a), dtype=np.float32)
    vectors = np.zeros((P, NVEC), np.float32)
    weights = np.zeros((P, NWREP), np.float32)

    def vec(name, value):
        o, w = VEC[name]
        vectors[:, o:o + w] = value.reshape(P, w)

    def wrep(name, value):
        o, w = WREP[name]
        weights[:, o:o + w] = value.reshape(P, w)

    per_channel = lambda a: np.tile(f(a), B)
    for name, key in [("gn_w", "L0_conv_gn_w"), ("gn_b", "L0_conv_gn_b"), ("gate_b", "L0_conv_gate_b"),
                      ("upd_b", "L0_conv_upd_b"), ("g3", "L1_conv_g3"), ("b3", "L1_conv_b3"), ("m3", "L1_conv_m3"),
                      ("v3", "L1_conv_v3"), ("dg0", "L2_conv_g1"), ("dbe0", "L2_conv_be1"), ("db0", "L2_conv_b1"),
                      ("dg1", "L2_conv_g2"), ("dbe1", "L2_conv_be2"), ("db1", "L2_conv_b2"),
                      ("gamma0", "L3_conv_gamma1"), ("beta0", "L3_conv_beta1"), ("gamma1", "L3_conv_gamma2"),
                      ("beta1", "L3_conv_beta2")]:
        vec(name, per_channel(i[key]))
    by_tile = lambda a: np.tile(f(a), (B,) + (1,) * (f(a).ndim - 1)).reshape(NT, P, -1).transpose(1, 0, 2)
    for name in ("g1", "b1", "m1", "v1", "g2", "b2", "m2", "v2"):
        vec(name, by_tile(i["L1_conv_" + name]))
    vec("wd", by_tile(f(i["L1_conv_wd"]).reshape(HID, K)))
    vec("br", np.tile(f(i["L1_conv_br"]), (P, 1)))
    for n in (0, 1):
        ob = f(i[f"L2_conv_ob{n + 1}"]).reshape(K, 2)
        for name, a in (("oby", ob[:, 0]), ("obx", ob[:, 1])):
            col = np.zeros(P, np.float32)
            col[:B * K] = np.repeat(a, B)
            vec(f"{name}{n}", col)

    per_image = lambda a: np.tile(f(a), (B, 1))
    wrep("gate", per_image(f(i["L0_conv_gate_w"]).T))
    wrep("upd", per_image(f(i["L0_conv_upd_w"]).T))
    wrep("w1", per_image(f(i["L1_conv_w1"]).T))
    wrep("wr", per_image(f(i["L1_conv_wr"]).T))
    wrep("we", by_tile(f(i["L1_conv_we"]).transpose(2, 0, 1).reshape(HID, E * C)))
    for n in (0, 1):
        ow = f(i[f"L2_conv_ow{n + 1}"]).reshape(K, 2, C, K)
        wrep(f"ow{n}", per_image(ow.transpose(2, 3, 1, 0).reshape(C, -1)))
        w = f(i[f"L2_conv_w{n + 1}"]).reshape(C, C, K)
        wt = w.transpose(1, 2, 0).reshape(C, -1)
        wrep(f"cw{n}", per_image(wt))
        wrep(f"sw{n}", np.repeat(wt, B, axis=0))
        cen = f(i[f"L3_conv_centers{n + 1}"])
        wrep(f"dt{n}", per_image(cen.reshape(C, C, K).transpose(1, 2, 0).reshape(C, -1)))
        wrep(f"cn{n}", per_image(cen))
    return vectors, weights


def kernel(**inputs):
    import concourse.bacc as _bacc
    from concourse.bass_utils import run_bass_kernel_spmd as _run

    nc = _bacc.Bacc("TRN2", target_bir_lowering=False, num_devices=1)
    vectors, weights = layout(inputs)
    arrays = {"in_x": np.ascontiguousarray(inputs["x"]), "in_const": constants(), "in_vectors": vectors,
              "in_weights": weights}
    args = [nc.dram_tensor(k, a.shape, F32, kind="ExternalInput").ap() for k, a in arrays.items()]
    args.append(nc.dram_tensor("out_0", (B, C, H, W), F32, kind="ExternalOutput").ap())
    build(nc, *args)
    r = _run(nc, [arrays], core_ids=[0])
    return r.results[0]["out_0"]
```

```python
from contextlib import ExitStack

import numpy as np
import concourse.bass as bass
from concourse import mybir

F32 = mybir.dt.float32
I32 = mybir.dt.int32
ALU = mybir.AluOpType
ACT = mybir.ActivationFunctionType
AX = mybir.AxisListType

P = 128
B, C, H, W = 8, 16, 64, 64
N = H * W
CH = 512
NCH = N // CH
CR = CH // W
HID, NT = 96, B * 96 // P
E = 8
K = 9
PW = W + 2
PADN = PW * PW
XW = W + 4
XN = XW * XW
BLK = 16
BR = H // BLK
BPX = BR * W
HR = BR + 4
HB = HR * XW
OM = BR * 2 * K
OK = (BR + 2) * C
EPS = 1e-5
D2_EPS = 1e-12
REACH = 67
SPAN = REACH + 1
NG = 5

VEC = {}
for name, width in [("gn_w", 1), ("gn_b", 1), ("gate_b", 1), ("upd_b", 1), ("g3", 1), ("b3", 1), ("m3", 1),
                    ("v3", 1), ("dg0", 1), ("dbe0", 1), ("db0", 1), ("dg1", 1), ("dbe1", 1), ("db1", 1),
                    ("gamma0", 1), ("beta0", 1), ("gamma1", 1), ("beta1", 1),
                    ("g1", NT), ("b1", NT), ("m1", NT), ("v1", NT), ("g2", NT), ("b2", NT), ("m2", NT),
                    ("v2", NT), ("wd", NT * K), ("br", E), ("ob0", 1), ("ob1", 1)]:
    VEC[name] = (sum(w for _, w in VEC.values()), width)
NVEC = sum(w for _, w in VEC.values())

WREP = {}
for name, width in [("gate", C), ("upd", C), ("w1", HID), ("wr", E), ("ow0", 3 * OM), ("ow1", 3 * OM),
                    ("cw0", K * C), ("cw1", K * C), ("sw0", K * C), ("sw1", K * C), ("dt0", K * C),
                    ("dt1", K * C), ("cn0", K * C), ("cn1", K * C), ("we", NT * E * C)]:
    WREP[name] = (sum(w for _, w in WREP.values()), width)
NWREP = sum(w for _, w in WREP.values())

CONST = {}
for name, width in [("ident", P), ("same_image", P), ("same_channel", P), ("same_pair", P), ("px8", 8),
                    ("blkhot", BLK), ("steps", 2 * SPAN + 1), ("rows", BR), ("columns", W)]:
    CONST[name] = (sum(w for _, w in CONST.values()), width)
NCONST = sum(w for _, w in CONST.values())


def constants():
    c = np.zeros((P, NCONST), np.float32)
    p = np.arange(P)

    def put(name, value):
        o, w = CONST[name]
        c[:, o:o + w] = value

    put("ident", p[:, None] == p[None, :])
    put("same_image", p[:, None] // C == p[None, :] // C)
    put("same_channel", p[:, None] % C == p[None, :] % C)
    put("same_pair", p[:, None] // 2 == p[None, :] // 2)
    put("px8", p[:, None] % 8 == np.arange(8)[None, :])
    put("blkhot", p[:, None] % BLK == np.arange(BLK)[None, :])
    put("steps", np.arange(-SPAN, SPAN + 1)[None, :])
    put("rows", np.arange(BR)[None, :])
    put("columns", np.arange(W)[None, :])
    e = np.arange(K * BLK)
    entries = np.stack([e + 1, e // BLK, e // BLK // 3, e // BLK % 3, e % BLK]).astype(np.float32)
    return c, entries


def build(nc, x, const, entries, vectors, weights, out):
    with ExitStack() as ctx:
        SIZE = 53200
        arena = ctx.enter_context(nc.sbuf_tensor("arena", [P, SIZE], F32))
        taken = [0]

        def place(width, at=None):
            if at is None:
                at = taken[0]
                taken[0] += width
            assert at + width <= SIZE, (at, width)
            return at

        def ap(at, dims, p0=0, pn=P):
            return bass.AP(arena, at + p0 * SIZE, [[SIZE, pn]] + [list(d) for d in dims])

        def cols(at, n, p0=0, pn=P):
            return ap(at, [[1, n]], p0, pn)

        CON = place(NCONST)
        VE = place(NVEC)
        WR = place(NWREP)

        def con(name, i=0, n=None):
            o, w = CONST[name]
            return cols(CON + o + i, w if n is None else n)

        def vec(name, i=0, n=1, pn=P):
            o, _ = VEC[name]
            return cols(VE + o + i, n, 0, pn)

        SMALL = place(720)
        small_at = [SMALL]

        def small(n):
            small_at[0] += n
            assert small_at[0] <= SMALL + 720
            return small_at[0] - n

        MATS = place(2 * P + 2 * NT * P + K * P)
        W_GATE, W_UPD, W_HID = MATS, MATS + P, MATS + 2 * P
        W_OUT = W_HID + NT * P
        W_DIAG = W_OUT + NT * P
        W_SAMP = place(K * P, MATS)
        ZERO = place(P, W_SAMP + K * P)
        W_DT = place(K * P, MATS)

        BIG = taken[0]
        T_HID = [place(N) for _ in range(NT)]
        T_PAD = [place(PADN) for _ in range(4)]
        XIN = place(N)

        XA = T_PAD[0]
        XB = BIG
        GRP = BIG + C * HB
        GN_ = C * W
        OFFC = GRP
        YA = BIG
        OFFB = XA + XN
        XC = OFFB
        TXY = OFFB + 2 * K * BPX
        TT = TXY + 6 * K * W
        TMP = TT + 3 * 9 * W
        ST = TMP + 3 * GN_
        YB = ST + 3 * GN_
        place(0, YB + GN_)

        xa_d = nc.dram_tensor("padded_image", [B, C, XN], F32, kind="Internal").ap()
        rows_d = nc.dram_tensor("padded_image_by_rows", [XW, C, B, XW], F32, kind="Internal").ap()
        off_d = nc.dram_tensor("offsets", [BLK, B, OM, W], F32, kind="Internal").ap()
        y_d = nc.dram_tensor("sampled", [C, B * BLK, BPX], F32, kind="Internal").ap()
        flag_d = nc.dram_tensor("reach", [2 * K, BLK], F32, kind="Internal").ap()

        psum = ctx.enter_context(nc.psum_tensor("psum", [P, 8, CH], F32))

        def ps(bank, off, n, pn=P):
            return psum[0:pn, bank, off:off + n]

        def ap_ps(bank, dims):
            return bass.AP(psum, bank * CH, [[8 * CH, P]] + [list(d) for d in dims])

        def sem(name):
            return ctx.enter_context(nc.semaphore(name))

        s_const, s_vec, s_wrep, s_x = sem("const_loaded"), sem("vec_loaded"), sem("weights_loaded"), sem("x_loaded")
        s_out = sem("out_stored")
        s_v, s_a, s_g = sem("vector_chain"), sem("scalar_chain"), sem("gpsimd_chain")
        s_stat, s_grp, s_var, s_std, s_coef = (sem("stats_ready"), sem("group_sums_ready"), sem("variance_ready"),
                                               sem("deviation_ready"), sem("coefficients_ready"))
        s_w0, s_w1, s_wo = sem("gate_weights_ready"), sem("hidden_weights_ready"), sem("out_weights_ready")
        s_hn = sem("normed_ready")
        s_gate, s_upd = sem("gate_products_ready"), sem("update_products_ready")
        s_g_act, s_blend = sem("gate_chunks_ready"), sem("update_chunks_ready")
        s_xsum, s_pool_w, s_route, s_rsig = (sem("layer0_ready"), sem("pooled_weights_ready"),
                                             sem("routing_logits_ready"), sem("routing_ready"))
        s_rl = sem("routing_biased")
        s_bn, s_bnstd = sem("bn_variance_ready"), sem("bn_deviation_ready")
        s_bnc = sem("bn_coefficients_ready")
        s_padz = sem("hidden_padding_cleared")
        s_c1, s_c1_free = sem("hidden_products_ready"), sem("hidden_banks_free")
        s_relu = sem("hidden_chunks_written")
        s_clip_g = sem("hidden_clipped_by_gpsimd")
        s_dwv, s_dwa = sem("depthwise_by_vector"), sem("depthwise_by_tensor")
        s_dw, s_dw_free = sem("depthwise_products_ready"), sem("depthwise_banks_free")
        s_diag = sem("diagonals_ready")
        s_hid = sem("hidden_tiles_finished")
        s_proj, s_proj_free = sem("projection_ready"), sem("projection_banks_free")
        s_xa = sem("layer_result_in_padded_image")

        s_sw = sem("sample_weights_ready")
        s_rd = sem("padded_rows_stored")
        s_xc = [sem(f"rows_image_loaded_{h}") for h in range(2)]
        s_oc, s_oe = sem("offset_products_ready"), sem("offsets_written")
        s_xd, s_xb, s_od, s_ob = (sem("padded_image_stored"), sem("block_image_loaded"), sem("offsets_stored"),
                                  sem("block_offsets_loaded"))
        s_am, s_amt, s_fl = sem("block_maxima_ready"), sem("block_maxima_turned"), sem("reach_ready")
        s_fd, s_fb = sem("reach_stored"), sem("reach_loaded")
        s_t = sem("tents_ready")
        s_gv, s_gp = sem("vector_groups_ready"), sem("gpsimd_groups_ready")
        s_tr, s_st, s_cn = sem("samples_turned"), sem("turned_samples_copied"), sem("samples_contracted")
        s_acc, s_yb, s_ys, s_ya = (sem("row_accumulated"), sem("row_copied"), sem("row_stored"),
                                   sem("convolution_loaded"))
        s_rw, s_ro, s_rs, s_rp = (sem("far_weights_ready"), sem("far_offsets_spread"), sem("far_samples_ready"),
                                  sem("far_products_ready"))
        s_any, s_fc = sem("farthest_known"), sem("far_chain")
        s_gc = sem("gpsimd_products_ready")
        s_z = sem("zeros_ready")
        s_held = sem("held")
        s_nrm = sem("normed_relu_ready")
        s_dw3, s_cz = sem("distance_weights_ready"), sem("second_padding_cleared")
        s_sq, s_box = sem("squares_ready"), sem("box_sums_ready")
        s_dp, s_d2, s_dist = sem("distance_products_ready"), sem("squared_distances_ready"), sem("distances_ready")
        s_x3, s_fin, s_res = sem("second_input_ready"), sem("final_sums_ready"), sem("results_ready")

        AHEAD = 3
        STEPS = BR * K

        block = ctx.enter_context(nc.Block())

        ORDER = [0, 4, 1, 2, 5, 3]
        PADBUF = {0: 0, 4: 3, 1: 1, 2: 2, 5: 3, 3: 0}
        BY_VECTOR, BY_TENSOR = [0, 1, 2, 3], [4, 5]

        STAT, MV, GV, NC_ = small(6 * NCH), small(4), small(4), small(4)
        ROUT, ROUTL = small(NT * E), small(NT * E)
        KO = small(NT * C)
        BN = small(4 * NT)
        BV = small(2 * NT + 1)
        S3, B3 = small(1), small(1)
        WDS = small(NT * K)
        XS = small(1)

        FMAX, FLAG = small(2 * K), small(BLK)
        COUNT = small(1)
        ENTRY = small(6)
        LAST = small(1)
        C2 = small(1)

        T0, T1, T2, T3, T4, T5 = T_HID

        FSEL, FW = GRP, GRP + P
        FO, FE = FW + P, FW + P + 2 * BPX
        FMASK, FTY, FTX, FROW, FACC = (FE + 2 * BPX + i * BPX for i in range(5))
        FKEY = FACC + BPX
        FHIT = FKEY + K * BLK
        FATTR = FHIT + K * BLK
        FREACH = FATTR + 6 * K * BLK
        FNUMBER = FREACH + 2 * K * BLK
        FTAP = FNUMBER + K * BLK

        SQ3 = BIG
        HS3 = SQ3 + XN
        V3 = HS3 + PW * W
        D3 = V3 + N
        XP3 = D3 + N
        OUT3 = V3
        assert XP3 + XN <= XA and OFFB == XA + XN
        def xa_rows(ch):
            return ap(XA + (ch * CR + 2) * XW + 2, [[XW, CR], [1, W]])

        def pad_rows(buf, row, col):
            return ap(buf + row * PW + col, [[PW, CR], [1, W]])

        def loaded(eng, at, low, high):
            return eng.value_load(cols(at, 1, 0, 1).bitcast(I32), min_val=low, max_val=high)

        def neighbours(row, dx, j, i):
            return ap(XB + (j * XW + dx + i) + row * XW, [[HB, C], [1, W]])

        def tent(dx, m):
            return ap(TT + (dx * 9 + m) * W, [[0, C], [1, W]])

        @block.sync
        def _(sp):
            sp.dma_start(cols(XIN, N), x.rearrange("b c h w -> (b c) (h w)")).then_inc(s_x, 16)
            sp.dma_start(cols(CON, NCONST), const).then_inc(s_const, 16)
            sp.dma_start(cols(VE, NVEC), vectors).then_inc(s_vec, 16)
            sp.dma_start(cols(WR, NWREP), weights).then_inc(s_wrep, 16)
            sp.sem_inc(s_ys, 16)
            for L in range(2):
                for h, (ready, row, end) in enumerate(((5, 0, 5 * CR + 2), (NCH, 5 * CR + 2, XW))):
                    sp.wait_ge(s_xa, NCH * L + ready)
                    for b in range(B):
                        sp.dma_start(rows_d[row:end, :, b, :].rearrange("h c x -> c h x"),
                                     ap(XA + row * XW, [[XW, end - row], [1, XW]], b * C, C)).then_inc(s_rd, 16)
                    sp.wait_ge(s_rd, 16 * B * (2 * L + h + 1))
                    sp.dma_start(ap(XC + h * BLK // 2 * B * XW, [[B * XW, BLK // 2], [1, B * XW]], 0, OK),
                                 bass.AP(rows_d.tensor, (h * BLK // 2 * BR + 1) * C * B * XW,
                                         [[B * XW, OK], [BR * C * B * XW, BLK // 2], [1, B * XW]])
                                 ).then_inc(s_xc[h], 16)
                sp.dma_start(xa_d.rearrange("b c n -> (b c) n"), cols(XA, XN)).then_inc(s_xd, 16)
                sp.wait_ge(s_xd, 16 * (L + 1))
                for b in range(B):
                    sp.dma_start(ap(XB, [[HB, C], [1, HB]], b * BLK, BLK),
                                 bass.AP(xa_d.tensor, b * C * XN, [[BR * XW, BLK], [XN, C], [1, HB]])
                                 ).then_inc(s_xb, 16)
                for q in range(4):
                    sp.wait_ge(s_oe, BLK * L + 4 * q + 8)
                    sp.dma_start(bass.AP(off_d.tensor, q * 4 * B * OM * W,
                                         [[W, OM], [OM * W, 4 * B], [1, W]]),
                                 ap(OFFC + q * 4 * CH, [[W, 4 * B], [1, W]], 0, OM)).then_inc(s_od, 16)
                sp.wait_ge(s_od, 64 * (L + 1))
                for b in range(B):
                    sp.dma_start(cols(OFFB, OM * W, b * BLK, BLK),
                                 off_d[:, b].rearrange("q m x -> q (m x)")).then_inc(s_ob, 16)
                sp.wait_ge(s_fl, L + 1)
                sp.dma_start(flag_d, cols(FLAG, BLK, 0, 2 * K)).then_inc(s_fd, 16)
                sp.wait_ge(s_fd, 16 * (L + 1))
                with sp.Fori(0, BR) as r:
                    sp.wait_ge(s_yb, r + (BR * L + 2))
                    sp.dma_start(y_d.rearrange("o p n -> p o n")[:, :, bass.ds(r * W, W)],
                                 ap(YB, [[W, C], [1, W]])).then_inc(s_ys, 16)
                sp.wait_ge(s_acc, BR * (L + 1))
                sp.dma_start(cols(FREACH, 2 * K * BLK, 0, 1),
                             flag_d.rearrange("k q -> (k q)").unsqueeze(0)).then_inc(s_fb, 16)
                sp.dma_start(cols(FNUMBER, 5 * K * BLK, 0, 1),
                             entries.rearrange("k q -> (k q)").unsqueeze(0)).then_inc(s_fb, 16)
                sp.wait_ge(s_ys, 16 * BR * (L + 1) + 16)
                sp.dma_start(cols(YA, N),
                             y_d.rearrange("o (b q) n -> b o (q n)", b=B)).then_inc(s_ya, 16)
            for ch in range(NCH):
                sp.wait_ge(s_res, ch + 1)
                sp.dma_start(out.rearrange("b c h w -> (b c) (h w)")[:, ch * CH:(ch + 1) * CH],
                             cols(OUT3 + ch * CH, CH)).then_inc(s_out, 16)
            sp.wait_ge(s_out, 16 * NCH)
            sp.wait_ge(s_held, 2 * STEPS + 2 * BR)

        @block.vector
        def _(dve):
            v = nc.vector
            count = [0]

            def link(ins):
                count[0] += 1
                ins.then_inc(s_v, 1)
                dve.wait_ge(s_v, count[0])

            def channel_stats(n, src, mask_cols, shift=None):
                for ch in range(NCH):
                    ins = v.bn_stats(cols(STAT + 6 * ch, 6), cols(src + ch * CH, CH))
                link(ins)
                link(v.bn_aggr(cols(MV, 2), cols(STAT, 6 * NCH)))
                if shift is not None:
                    link(v.tensor_tensor(cols(MV, 1), cols(MV, 1), shift, ALU.add))
                v.scalar_tensor_tensor(cols(MV + 1, 1), cols(MV, 1), cols(MV, 1), cols(MV + 1, 1), ALU.mult,
                                       ALU.add).then_inc(s_stat, 1)

            def norm_coefficients(n, count_, gamma, beta, shift=None):
                dve.wait_ge(s_grp, n + 1)
                link(v.tensor_scalar(cols(GV, 2), ps(0, 0, 2), 1.0 / count_, None, ALU.mult))
                link(v.tensor_tensor(cols(GV + 2, 1), cols(GV, 1), cols(GV, 1), ALU.mult))
                link(v.tensor_tensor(cols(GV + 2, 1), cols(GV + 1, 1), cols(GV + 2, 1), ALU.subtract))
                v.tensor_scalar(cols(GV + 2, 1), cols(GV + 2, 1), EPS, None, ALU.add).then_inc(s_var, 1)
                dve.wait_ge(s_std, n + 1)
                link(v.reciprocal(cols(NC_ + 2, 1), cols(GV + 3, 1)))
                link(v.tensor_tensor(cols(NC_, 1), cols(NC_ + 2, 1), gamma, ALU.mult))
                if shift is not None:
                    link(v.tensor_tensor(cols(GV, 1), cols(GV, 1), shift, ALU.subtract))
                link(v.tensor_tensor(cols(NC_ + 3, 1), cols(GV, 1), cols(NC_, 1), ALU.mult))
                v.tensor_tensor(cols(NC_ + 1, 1), beta, cols(NC_ + 3, 1), ALU.subtract).then_inc(s_coef, 1)

            dve.wait_ge(s_x, 16)
            channel_stats(0, XIN, None)
            dve.wait_ge(s_const, 16)
            dve.wait_ge(s_vec, 16)
            dve.wait_ge(s_wrep, 16)

            def by_image(at, name, width):
                o, _ = CONST["same_image"]
                return v.tensor_tensor(ap(at, [[width, B], [1, width]]),
                                       ap(WR + WREP[name][0], [[0, B], [1, width]]),
                                       ap(CON + o, [[C, B], [0, width]]), ALU.mult)

            by_image(W_GATE, "gate", C).then_inc(s_w0, 1)
            by_image(W_UPD, "upd", C).then_inc(s_w0, 1)
            norm_coefficients(0, 2, vec("gn_w"), vec("gn_b"))
            by_image(W_HID, "w1", HID).then_inc(s_w1, 1)

            v.tensor_scalar(cols(BV, NT), vec("v1", 0, NT), EPS, None, ALU.add)
            v.tensor_scalar(cols(BV + NT, NT), vec("v2", 0, NT), EPS, None, ALU.add)
            v.tensor_scalar(cols(BV + 2 * NT, 1), vec("v3"), EPS, None, ALU.add).then_inc(s_bn, 1)

            for ch in range(NCH):
                dve.wait_ge(s_g_act, ch + 1)
                link(v.tensor_scalar(cols(T3 + ch * CH, CH), cols(T1 + ch * CH, CH), -1.0, 1.0, ALU.mult, ALU.add))
                dve.wait_ge(s_upd, ch + 1)
                v.scalar_tensor_tensor(cols(T0 + ch * CH, CH), ps(4 + ch % 4, 0, CH), vec("upd_b"),
                                       cols(T3 + ch * CH, CH), ALU.add, ALU.mult).then_inc(s_blend, 1)
            dve.wait_ge(s_blend, NCH)
            link(v.memset(ap(T1, [[W, H]]), 0.0))
            link(v.tensor_tensor_scan(cols(T4, N), cols(T1, N), cols(T0, N), 0.0, ALU.mult, ALU.add))
            link(v.tensor_tensor(ap(T5, [[H, W], [1, H]]), ap(T3, [[1, W], [W, H]]), ap(T4, [[1, W], [W, H]]),
                                 ALU.mult))
            dve.wait_ge(s_a, NCH)
            link(v.memset(ap(T2, [[H, W]]), 0.0))
            link(v.tensor_tensor_scan(cols(T1, N), cols(T2, N), cols(T5, N), 0.0, ALU.mult, ALU.add))
            v.tensor_tensor(ap(XIN, [[W, H], [1, W]]), ap(XIN, [[W, H], [1, W]]), ap(T1, [[1, H], [H, W]]),
                            ALU.add).then_inc(s_xsum, 1)

            dve.wait_ge(s_xsum, 1)
            link(v.tensor_reduce(cols(XS, 1), cols(XIN, N), AX.X, ALU.add))
            o = CONST["same_image"][0]
            v.tensor_scalar(ap(W_OUT, [[HID, B], [1, HID]]), ap(CON + o, [[C, B], [0, HID]]), cols(XS, 1), None,
                            ALU.mult).then_inc(s_pool_w, 1)
            dve.wait_ge(s_bnstd, 1)
            link(v.reciprocal(cols(BV, 2 * NT + 1), cols(BV, 2 * NT + 1)))
            link(v.tensor_tensor(cols(BN, NT), cols(BV, NT), vec("g1", 0, NT), ALU.mult))
            link(v.tensor_tensor(cols(BN + 2 * NT, NT), cols(BV + NT, NT), vec("g2", 0, NT), ALU.mult))
            link(v.tensor_tensor(cols(S3, 1), cols(BV + 2 * NT, 1), vec("g3"), ALU.mult))
            link(v.tensor_tensor(cols(BN + NT, NT), vec("m1", 0, NT), cols(BN, NT), ALU.mult))
            link(v.tensor_tensor(cols(BN + 3 * NT, NT), vec("m2", 0, NT), cols(BN + 2 * NT, NT), ALU.mult))
            link(v.tensor_tensor(cols(B3, 1), vec("m3"), cols(S3, 1), ALU.mult))
            link(v.tensor_tensor(cols(BN + NT, NT), vec("b1", 0, NT), cols(BN + NT, NT), ALU.subtract))
            link(v.tensor_tensor(cols(BN + 3 * NT, NT), vec("b2", 0, NT), cols(BN + 3 * NT, NT), ALU.subtract))
            link(v.tensor_tensor(cols(B3, 1), vec("b3"), cols(B3, 1), ALU.subtract))
            v.tensor_tensor(ap(WDS, [[K, NT], [1, K]]), ap(VE + VEC["wd"][0], [[K, NT], [1, K]]),
                            ap(BN + 2 * NT, [[1, NT], [0, K]]), ALU.mult).then_inc(s_bnc, 1)
            dve.wait_ge(s_bnc, 1)

            def diagonals(t):
                v.tensor_tensor(ap(W_DIAG, [[P, K], [1, P]]), ap(CON + CONST["ident"][0], [[0, K], [1, P]]),
                                ap(WDS + t * K, [[1, K], [0, P]]), ALU.mult).then_inc(s_diag, 1)

            diagonals(BY_TENSOR[0])
            dve.wait_ge(s_route, 1)
            v.scalar_tensor_tensor(ap(ROUTL, [[E, NT], [1, E]]), ap_ps(7, [[E, NT], [1, E]]), 1.0 / N,
                                   ap(VE + VEC["br"][0], [[0, NT], [1, E]]), ALU.mult, ALU.add).then_inc(s_rl, 1)
            dve.wait_ge(s_rsig, 1)

            def mix_experts():
                link(v.tensor_tensor(ap(W_OUT, [[E * C, NT], [C, E], [1, C]]),
                                     ap(WR + WREP["we"][0], [[E * C, NT], [C, E], [1, C]]),
                                     ap(ROUT, [[E, NT], [1, E], [0, C]]), ALU.mult))
                link(v.tensor_reduce(ap(KO, [[C, NT], [1, C]]), ap(W_OUT, [[E * C, NT], [1, C], [C, E]]), AX.X,
                                     ALU.add))
                link(v.memset(cols(W_OUT, NT * P), 0.0))
                for t in range(NT):
                    for p0 in range(0, P, 32):
                        b = (t * P + p0) // HID
                        ins = v.tensor_copy(ap(W_OUT + t * P + b * C, [[1, C]], p0, 32),
                                            ap(KO + t * C, [[1, C]], p0, 32))
                ins.then_inc(s_wo, 1)

            mix_experts()

            def depthwise(eng, link_, t, clip=True):
                src, dst = T_PAD[PADBUF[t]], T_HID[t]
                whole = lambda at, dy, dx: ap(at + dy * PW + dx, [[PW, H], [1, W]])
                full = ap(dst, [[W, H], [1, W]])
                link_(eng.tensor_scalar(full, whole(src, 0, 0), cols(WDS + t * K, 1), cols(BN + 3 * NT + t, 1),
                                        ALU.mult, ALU.add))
                for k in range(1, K):
                    link_(eng.scalar_tensor_tensor(full, whole(src, k // 3, k % 3), cols(WDS + t * K + k, 1), full,
                                                   ALU.mult, ALU.add))
                return eng.tensor_scalar(cols(dst, N), cols(dst, N), 0.0, 6.0, ALU.max, ALU.min)

            for i, t in enumerate(BY_VECTOR):
                dve.wait_ge(s_relu, NCH * (ORDER.index(t) + 1))
                link(v.tensor_scalar(cols(T_PAD[PADBUF[t]], PADN), cols(T_PAD[PADBUF[t]], PADN), 6.0, None, ALU.min))
                depthwise(v, link, t).then_inc(s_dwv, 1)
                if i == 0:
                    dve.wait_ge(s_dw, NCH)
                    diagonals(BY_TENSOR[1])
            dve.wait_ge(s_dwv, len(BY_VECTOR))
            link(v.memset(cols(XA, XN), 0.0))
            for i, t in enumerate(BY_TENSOR):
                dve.wait_ge(s_dwa, NCH * (i + 1))
                v.tensor_scalar(cols(T_HID[t], N), cols(T_HID[t], N), 6.0, None, ALU.min).then_inc(s_hid, 1)
            PROJ = T_PAD[3] + PADN - 2 * CH
            for ch in range(NCH):
                dve.wait_ge(s_proj, ch + 1)
                v.tensor_scalar(cols(PROJ + (ch % 2) * CH, CH), ps(ch % 4, 0, CH), cols(S3, 1), cols(B3, 1),
                                ALU.mult, ALU.add).then_inc(s_proj_free, 1)
                dve.wait_ge(s_proj_free, ch + 1)
                v.tensor_tensor(xa_rows(ch), ap(PROJ + (ch % 2) * CH, [[W, CR], [1, W]]),
                                ap(XIN + ch * CH, [[W, CR], [1, W]]), ALU.add).then_inc(s_xa, 1)

            def sample_weights(L):
                if L == 0:
                    v.memset(cols(ZERO, P), 0.0).then_inc(s_z, 1)
                v.tensor_tensor(ap(W_SAMP, [[8, K * C], [1, 8]]),
                                ap(WR + WREP[f"sw{L}"][0], [[1, K * C], [0, 8]]),
                                ap(CON + CONST["px8"][0], [[0, K * C], [1, 8]]), ALU.mult).then_inc(s_sw, 1)

            def reach(L):
                dve.wait_ge(s_ob, 16 * B * (L + 1))
                v.tensor_reduce(cols(FMAX, 2 * K), ap(OFFB, [[W, 2 * K], [2 * K * W, BR], [1, W]]), AX.XY, ALU.max,
                                apply_absolute_value=True).then_inc(s_am, 1)
                dve.wait_ge(s_amt, L + 1)
                axis = lambda at: cols(at, BLK, 0, 2 * K)
                link(v.tensor_reduce(axis(FLAG), bass.AP(psum, 0, [[8 * CH, 2 * K], [1, BLK], [BLK, B]]), AX.X,
                                     ALU.max))
                link(v.tensor_scalar(axis(FMAX), axis(FLAG), REACH - 1.0, None, ALU.min))
                link(v.scalar_tensor_tensor(axis(FMAX), axis(FLAG), 1.0, axis(FMAX), ALU.is_gt, ALU.mult))
                v.tensor_scalar(axis(FLAG), axis(FMAX), 1.0, None, ALU.add).then_inc(s_fl, 1)

            def grp(dx, g):
                return ap(GRP + (dx * NG + g) * GN_, [[W, C], [1, W]])

            def tents(L, at):
                plane = lambda step: ap(TXY + step * K * W, [[3 * K * W, 2], [1, K * W]])
                wide = lambda step: ap(TXY + step * K * W, [[3 * K * W, 2], [W, K], [1, W]])
                off4 = ap(OFFB + at, [[K * W, 2], [W, K], [1, W]])
                v.tensor_scalar(wide(0), off4, -1.0, 0.0, ALU.mult, ALU.max)
                link(v.tensor_scalar(wide(2), off4, 0.0, None, ALU.max))
                link(v.tensor_tensor(plane(1), plane(0), plane(2), ALU.max))
                near = cols(TMP, K * W)
                link(v.tensor_tensor(near, cols(TXY + K * W, K * W), cols(TXY + 4 * K * W, K * W), ALU.max))
                link(v.tensor_scalar(near, near, 1.0, None, ALU.is_le))
                link(v.tensor_scalar(plane(1), plane(1), -1.0, 1.0, ALU.mult, ALU.add))
                count[0] += 1
                v.tensor_tensor(ap(TXY, [[K * W, 3], [1, K * W]]), ap(TXY, [[K * W, 3], [1, K * W]]),
                                ap(TMP, [[0, 3], [1, K * W]]), ALU.mult).then_inc(s_v, 1)
                dve.wait_ge(s_v, count[0])
                dve.sem_inc(s_held, 1)

            def sample_row(L, r):
                base = count[0]
                count[0] = base + r * ROW_LINKS
                tents(L, r * (2 * K * W))
                row_start = count[0]
                with dve.Fori(0, 3) as dy:
                    count[0] = row_start + dy * DY_LINKS
                    n = r * 3 + dy
                    for dx in range(3):
                        step = n * 3 + (dx + STEPS * L)
                        dve.wait_ge(s_gp, step + 1)
                        v.tensor_tensor(
                            ap(TT + dx * 9 * W, [[3 * W, 3], [W, 3], [1, W]]),
                            ap(TXY + dx * W + dy * (3 * W), [[K * W, 3], [0, 3], [1, W]]),
                            ap(TXY + 3 * K * W + dx * W + dy * (3 * W), [[0, 3], [K * W, 3], [1, W]]),
                            ALU.mult).then_inc(s_t, 1)
                        dve.wait_ge(s_t, step + 1)
                        dve.wait_ge(s_tr, step + 1)

                        def product(m, dst):
                            j, i = divmod(m, 3)
                            return v.tensor_tensor(dst, neighbours(r + dy, dx, j, i), tent(dx, m), ALU.mult)

                        t0, t1 = ap(TMP, [[W, C], [1, W]]), ap(TMP + GN_, [[W, C], [1, W]])
                        product(0, grp(dx, 0))
                        product(1, t0)
                        product(2, grp(dx, 1))
                        product(3, t1)
                        link(product(4, grp(dx, 2)))
                        v.tensor_tensor(grp(dx, 0), grp(dx, 0), t0, ALU.add)
                        link(v.tensor_tensor(grp(dx, 1), grp(dx, 1), t1, ALU.add))
                        link(product(5, t0))
                        v.tensor_tensor(grp(dx, 2), grp(dx, 2), t0, ALU.add).then_inc(s_gv, 1)
                count[0] = base

            ROW_LINKS, DY_LINKS = 6 + 3 * 9, 9

            def far_link(ins, last=False):
                ins.then_inc(s_fc, 1)
                if last:
                    dve.wait_ge(s_fc, dve.snap(far_chain) + 1)
                dve.reg_add(far_chain, far_chain, 1)
                if not last:
                    dve.wait_ge(s_fc, dve.snap(far_chain))

            far_chain = dve.alloc_register("far_chain")
            far_done = dve.alloc_register("far_done_by_vector")
            dve.reg_mov(far_chain, 0)
            dve.reg_mov(far_done, 0)

            def far_block(L):
                every = lambda at, n: ap(at, [[K * BLK, n], [1, K * BLK]], 0, 1)
                far_link(v.tensor_reduce(cols(LAST, 1, 0, 1), every(FKEY, 1), AX.X, ALU.max))
                far_link(v.tensor_scalar(every(FHIT, 1), every(FKEY, 1), cols(LAST, 1, 0, 1), None, ALU.is_equal))
                v.tensor_tensor(every(FATTR, 4), every(FTAP, 4),
                                ap(FHIT, [[0, 4], [1, K * BLK]], 0, 1), ALU.mult)
                far_link(v.tensor_tensor(every(FATTR + 4 * K * BLK, 2), every(FREACH, 2),
                                      ap(FHIT, [[0, 2], [1, K * BLK]], 0, 1), ALU.mult))
                far_link(v.tensor_reduce(cols(FATTR, 6, 0, 1), every(FATTR, 6), AX.X, ALU.add))
                far_link(v.tensor_copy(cols(ENTRY, 6, 0, 1).bitcast(I32), cols(FATTR, 6, 0, 1)))
                v.scalar_tensor_tensor(every(FKEY, 1), every(FHIT, 1), -float(K * BLK + 1), every(FKEY, 1),
                                       ALU.mult, ALU.add).then_inc(s_fc, 1)
                dve.reg_add(far_chain, far_chain, 1)
                ky, kx, blk = (loaded(dve, ENTRY + i, 0, h) for i, h in ((1, 2), (2, 2), (3, BLK - 1)))
                far_y, far_x = (loaded(dve, ENTRY + i, 1, REACH) for i in (4, 5))
                rows = ap(CON + CONST["rows"][0], [[1, BR], [0, W]])
                columns = ap(CON + CONST["columns"][0], [[0, BR], [1, W]])
                step_at = lambda i: cols(CON + CONST["steps"][0] + i, 1)
                img = lambda at: ap(at, [[W, BR], [1, W]])
                dve.wait_ge(s_fc, dve.snap(far_chain))
                v.tensor_scalar(cols(FSEL, P), con("same_image"), cols(CON + CONST["blkhot"][0] + blk, 1), None,
                                ALU.mult)
                v.tensor_tensor(ap(FW, [[C, B], [1, C]]),
                                ap(WR + WREP[f"cw{L}"][0] + kx * C + ky * (3 * C), [[0, B], [1, C]]),
                                ap(CON + CONST["same_image"][0], [[C, B], [0, C]]), ALU.mult).then_inc(s_rw, 1)
                dve.reg_add(far_done, far_done, 1)
                dve.wait_ge(s_ro, dve.snap(far_done))
                far_link(v.tensor_copy(cols(FO, 2 * BPX), ps(0, 0, 2 * BPX)))
                far_link(v.scalar_tensor_tensor(cols(FE, 2 * BPX), cols(FO, 2 * BPX), -1.0, cols(FO, 2 * BPX),
                                                ALU.mult, ALU.max))
                far_link(v.tensor_tensor(cols(FMASK, BPX), cols(FE, BPX), cols(FE + BPX, BPX), ALU.max))
                far_link(v.tensor_scalar(cols(FMASK, BPX), cols(FMASK, BPX), 1.0, None, ALU.is_gt))
                for off, at, plane, size in ((FO, step_at(blk * BR + ky + (SPAN - 1)), rows, H),
                                             (FO + BPX, step_at(kx + (SPAN - 1)), columns, W)):
                    far_link(v.tensor_scalar(cols(off, BPX), cols(off, BPX), at, None, ALU.add))
                    far_link(v.tensor_tensor(img(off), img(off), plane, ALU.add))
                    far_link(v.tensor_scalar(cols(off, BPX), cols(off, BPX), -1.0, float(size), ALU.max, ALU.min))
                    far_link(v.tensor_tensor(img(off), img(off), plane, ALU.subtract))
                    far_link(v.tensor_scalar(cols(off, BPX), cols(off, BPX), at, None, ALU.subtract))

                def tent_before_relu(dst, off, i):
                    far_link(v.tensor_scalar(cols(dst, BPX), cols(off, BPX), -1.0, step_at(i + 1), ALU.mult, ALU.add))
                    far_link(v.scalar_tensor_tensor(cols(dst, BPX), cols(off, BPX), step_at(i - 1), cols(dst, BPX),
                                                    ALU.subtract, ALU.min))

                far_link(v.memset(cols(FACC, BPX), 0.0), last=True)
                with dve.Fori(SPAN - far_y, SPAN + far_y + 1) as j:
                    tent_before_relu(FTY, FO, j)
                    far_link(v.scalar_tensor_tensor(cols(FTY, BPX), cols(FTY, BPX), 0.0, cols(FMASK, BPX), ALU.max,
                                                    ALU.mult))
                    far_link(v.memset(cols(FROW, BPX), 0.0), last=True)
                    with dve.Fori(SPAN - far_x, SPAN + far_x + 1) as i:
                        tent_before_relu(FTX, FO + BPX, i)
                        at = (blk * BR + ky + j + (1 - SPAN)) * XW + kx + i + (1 - SPAN)
                        far_link(v.scalar_tensor_tensor(img(FTX), img(FTX), 0.0, ap(XA + at, [[XW, BR], [1, W]]),
                                                        ALU.max, ALU.mult))
                        far_link(v.tensor_tensor(cols(FROW, BPX), cols(FROW, BPX), cols(FTX, BPX), ALU.add), last=True)
                    far_link(v.tensor_tensor(cols(FROW, BPX), cols(FROW, BPX), cols(FTY, BPX), ALU.mult))
                    far_link(v.tensor_tensor(cols(FACC, BPX), cols(FACC, BPX), cols(FROW, BPX), ALU.add), last=True)
                dve.sem_inc(s_rs, 1)
                dve.wait_ge(s_rp, dve.snap(far_done))
                far_link(v.tensor_tensor(cols(YA + blk * BPX, BPX), cols(YA + blk * BPX, BPX), ps(1, 0, BPX),
                                         ALU.add), last=True)

            def far_samples(L):
                dve.wait_ge(s_fb, 32 * (L + 1))
                flat = lambda at: cols(at, K * BLK, 0, 1)
                link(v.tensor_tensor(flat(FHIT), flat(FREACH), flat(FREACH + K * BLK), ALU.max))
                link(v.tensor_scalar(flat(FHIT), flat(FHIT), 1.0, None, ALU.is_gt))
                link(v.tensor_reduce(cols(LAST, 1, 0, 1), flat(FHIT), AX.X, ALU.add))
                v.tensor_tensor(flat(FKEY), flat(FHIT), flat(FNUMBER), ALU.mult)
                v.tensor_copy(cols(COUNT, 1, 0, 1).bitcast(I32), cols(LAST, 1, 0, 1)).then_inc(s_any, 1)
                dve.wait_ge(s_any, L + 1)
                many = loaded(dve, COUNT, 0, K * BLK)
                with dve.If(many > 0):
                    with dve.Fori(0, many):
                        far_block(L)

            def layer2(L):
                sample_weights(L)
                dve.wait_ge(s_sw, L + 1)
                reach(L)
                dve.wait_ge(s_xb, 16 * B * (L + 1))
                dve.wait_ge(s_od, 64 * (L + 1))
                with dve.Fori(0, BR) as r:
                    sample_row(L, r)
                count[0] = count[0] + BR * ROW_LINKS
                dve.wait_ge(s_ya, 16 * (L + 1))
                far_samples(L)
                channel_stats(1 + L, YA, None, vec(f"db{L}"))
                norm_coefficients(1 + L, C, vec(f"dg{L}"), vec(f"dbe{L}"), vec(f"db{L}"))
                for ch in range(NCH):
                    dve.wait_ge(s_nrm, NCH * L + ch + 1)
                    v.tensor_tensor(xa_rows(ch), xa_rows(ch), ap(YA + ch * CH, [[W, CR], [1, W]]),
                                    ALU.add).then_inc(s_xa, 1)

            dve.wait_ge(s_proj, NCH)
            for L in range(2):
                layer2(L)

            def distance(L):
                src = XA if L == 0 else XP3
                o = WR + WREP[f"dt{L}"][0]
                link(v.tensor_scalar(cols(o, K * C), cols(o, K * C), -2.0, None, ALU.mult))
                v.tensor_tensor(ap(W_DT, [[P, K], [C, B], [1, C]]), ap(o, [[C, K], [0, B], [1, C]]),
                                ap(CON + CONST["same_image"][0], [[0, K], [C, B], [0, C]]),
                                ALU.mult).then_inc(s_dw3, 1)
                link(v.tensor_tensor_reduce(cols(V3, K * C), cols(WR + WREP[f"cn{L}"][0], K * C),
                                            cols(WR + WREP[f"cn{L}"][0], K * C), 1.0, 0.0, ALU.mult, ALU.add,
                                            cols(C2, 1)))
                dve.wait_ge(s_sq, L + 1)
                sq = lambda dx: ap(SQ3 + XW + 1 + dx, [[XW, PW], [1, W]])
                hs = ap(HS3, [[W, PW], [1, W]])
                link(v.tensor_tensor(hs, sq(0), sq(1), ALU.add))
                link(v.tensor_tensor(hs, hs, sq(2), ALU.add))
                link(v.tensor_tensor(cols(V3, N), cols(HS3, N), cols(HS3 + W, N), ALU.add))
                v.tensor_tensor(cols(V3, N), cols(V3, N), cols(HS3 + 2 * W, N), ALU.add).then_inc(s_box, 1)
                for ch in range(NCH):
                    dve.wait_ge(s_dp, NCH * L + ch + 1)
                    v.tensor_scalar(cols(D3 + ch * CH, CH), ps(ch % 8, 0, CH), cols(C2, 1), D2_EPS, ALU.add,
                                    ALU.max).then_inc(s_d2, 1)
                for ch in range(NCH):
                    dve.wait_ge(s_dist, NCH * L + ch + 1)
                    ins = v.bn_stats(cols(STAT + 6 * ch, 6), cols(D3 + ch * CH, CH))
                link(ins)
                link(v.bn_aggr(cols(MV, 2), cols(STAT, 6 * NCH)))
                v.scalar_tensor_tensor(cols(MV + 1, 1), cols(MV, 1), cols(MV, 1), cols(MV + 1, 1), ALU.mult,
                                       ALU.add).then_inc(s_stat, 1)
                norm_coefficients(3 + L, B, vec(f"gamma{L}"), vec(f"beta{L}"))

            dve.wait_ge(s_xa, 3 * NCH)
            distance(0)
            distance(1)
            dve.wait_ge(s_coef, 5)
            for ch in range(NCH):
                v.scalar_tensor_tensor(ap(D3 + ch * CH, [[W, CR], [1, W]]), ap(D3 + ch * CH, [[W, CR], [1, W]]),
                                       cols(NC_, 1), xa_rows(ch), ALU.mult, ALU.add).then_inc(s_fin, 1)

        @block.scalar
        def _(act):
            a = nc.scalar

            def deviation(n):
                act.wait_ge(s_var, n + 1)
                a.activation(cols(GV + 3, 1), cols(GV + 2, 1), ACT.Sqrt).then_inc(s_std, 1)

            deviation(0)
            act.wait_ge(s_bn, 1)
            a.activation(cols(BV, 2 * NT + 1), cols(BV, 2 * NT + 1), ACT.Sqrt).then_inc(s_bnstd, 1)
            act.wait_ge(s_coef, 1)
            for ch in range(NCH):
                a.activation(cols(T0 + ch * CH, CH), cols(XIN + ch * CH, CH), ACT.Identity, bias=cols(NC_ + 1, 1),
                             scale=cols(NC_, 1)).then_inc(s_hn, 1)
            for ch in range(NCH):
                act.wait_ge(s_gate, ch + 1)
                a.activation(cols(T1 + ch * CH, CH), ps(ch % 4, 0, CH), ACT.Sigmoid,
                             bias=vec("gate_b")).then_inc(s_g_act, 1)
                a.activation(ap(T2 + ch * CR, [[1, CR], [H, W]]), ap_ps(ch % 4, [[W, CR], [1, W]]), ACT.Sigmoid,
                             bias=vec("gate_b")).then_inc(s_a, 1)

            act.wait_ge(s_rl, 1)
            a.activation(cols(ROUT, NT * E), cols(ROUTL, NT * E), ACT.Sigmoid).then_inc(s_rsig, 1)
            act.wait_ge(s_bnc, 1)
            act.wait_ge(s_padz, 1)

            def hidden(q):
                t = ORDER[q]
                if t == 3:
                    act.wait_ge(s_dwv, 1)
                if t == 5:
                    act.wait_ge(s_dw, NCH)
                for ch in range(NCH):
                    act.wait_ge(s_c1, NCH * q + ch + 1)
                    a.activation(pad_rows(T_PAD[PADBUF[t]], ch * CR + 1, 1), ap_ps(ch % 4, [[W, CR], [1, W]]),
                                 ACT.Relu, bias=cols(BN + NT + t, 1), scale=cols(BN + t, 1)).then_inc(s_relu, 1)

            def depthwise_relu(i):
                t = BY_TENSOR[i]
                for ch in range(NCH):
                    act.wait_ge(s_dw, NCH * i + ch + 1)
                    a.activation(cols(T_HID[t] + ch * CH, CH), ps(4 + ch % 4, 0, CH), ACT.Relu,
                                 bias=cols(BN + 3 * NT + t, 1)).then_inc(s_dwa, 1)

            for q in range(4):
                hidden(q)
            depthwise_relu(0)
            hidden(4)
            hidden(5)
            depthwise_relu(1)

            a.sem_inc(s_st, AHEAD)
            a.sem_inc(s_oe, 4)
            a.sem_inc(s_yb, 1)
            for L in range(2):
                with act.Fori(0, BLK // 4) as i:
                    for u in range(4):
                        act.wait_ge(s_oc, i * 4 + (u + 1 + BLK * L))
                        a.activation(ap(OFFC + u * CH + i * (4 * CH), [[1, CH]], 0, OM), ps(u, 0, CH, OM),
                                     ACT.Identity, bias=vec(f"ob{L}", 0, 1, OM)).then_inc(s_oe, 1)
                with act.Fori(0, BR) as r:
                    with act.Fori(0, 3) as dy:
                        for dx in range(3):
                            step = r * 9 + dy * 3 + (dx + STEPS * L)
                            act.wait_ge(s_tr, step + 1 + AHEAD)
                            act.wait_ge(s_cn, step + 1)
                            a.activation(cols(ST + dx * GN_, GN_), ap_ps(2 * dx, [[1, GN_]]),
                                         ACT.Copy).then_inc(s_st, 1)
                    act.wait_ge(s_acc, r + (BR * L + 1))
                    act.wait_ge(s_ys, r * 16 + (16 * BR * L + 16))
                    a.activation(ap(YB, [[1, 8], [W, C], [8, 8]]), ap_ps(6, [[P, 8], [8, C], [1, 8]]),
                                 ACT.Copy).then_inc(s_yb, 1)
                deviation(1 + L)
                act.wait_ge(s_coef, 2 + L)
                for ch in range(NCH):
                    a.activation(cols(YA + ch * CH, CH), cols(YA + ch * CH, CH), ACT.Relu, bias=cols(NC_ + 1, 1),
                                 scale=cols(NC_, 1)).then_inc(s_nrm, 1)

            for L in range(2):
                if L == 0:
                    act.wait_ge(s_xa, 3 * NCH)
                    a.activation(cols(SQ3, XN), cols(XA, XN), ACT.Square).then_inc(s_sq, 1)
                else:
                    act.wait_ge(s_x3, NCH)
                    a.activation(cols(SQ3, XN), cols(XP3, XN), ACT.Square).then_inc(s_sq, 1)
                for ch in range(NCH):
                    act.wait_ge(s_d2, NCH * L + ch + 1)
                    a.activation(cols(D3 + ch * CH, CH), cols(D3 + ch * CH, CH), ACT.Sqrt).then_inc(s_dist, 1)
                deviation(3 + L)
                act.wait_ge(s_coef, 4 + L)
                if L == 0:
                    act.wait_ge(s_cz, 1)
                    for ch in range(NCH):
                        a.activation(ap(XP3 + (ch * CR + 2) * XW + 2, [[XW, CR], [1, W]]),
                                     ap(D3 + ch * CH, [[W, CR], [1, W]]), ACT.Relu, bias=cols(NC_ + 1, 1),
                                     scale=cols(NC_, 1)).then_inc(s_x3, 1)
                else:
                    for ch in range(NCH):
                        act.wait_ge(s_fin, ch + 1)
                        a.activation(cols(OUT3 + ch * CH, CH), cols(D3 + ch * CH, CH), ACT.Relu,
                                     bias=cols(NC_ + 1, 1)).then_inc(s_res, 1)

        @block.tensor
        def _(pe):
            t_ = nc.tensor

            def group_sums(n, mask):
                pe.wait_ge(s_stat, n + 1)
                t_.matmul(ps(0, 0, 2), con(mask), cols(MV, 2), start=True, stop=True).then_inc(s_grp, 1)

            pe.wait_ge(s_const, 16)
            group_sums(0, "same_pair")
            pe.wait_ge(s_w0, 2)
            for ch in range(NCH):
                pe.wait_ge(s_hn, ch + 1)
                if ch >= 4:
                    pe.wait_ge(s_a, ch - 3)
                else:
                    pe.wait_ge(s_coef, 1)
                t_.matmul(ps(ch % 4, 0, CH), cols(W_GATE, P), cols(T0 + ch * CH, CH), start=True,
                          stop=True).then_inc(s_gate, 1)
                if ch >= 4:
                    pe.wait_ge(s_blend, ch - 3)
                t_.matmul(ps(4 + ch % 4, 0, CH), cols(W_UPD, P), cols(T0 + ch * CH, CH), start=True,
                          stop=True).then_inc(s_upd, 1)

            pe.wait_ge(s_pool_w, 1)
            pe.wait_ge(s_blend, NCH)
            for t in range(NT):
                ins = t_.matmul(ps(7, t * E, E), cols(W_OUT + t * P, P), cols(WR + WREP["wr"][0], E),
                                start=(t == 0), stop=True, skip_group_check=True)
            ins.then_inc(s_route, 1)
            pe.wait_ge(s_w1, 1)
            pe.wait_ge(s_xsum, 1)
            pe.wait_ge(s_a, NCH)

            def hidden(q):
                t = ORDER[q]
                for ch in range(NCH):
                    n = NCH * q + ch
                    if n >= 4:
                        pe.wait_ge(s_relu, n - 3)
                    t_.matmul(ps(ch % 4, 0, CH), cols(W_HID + t * P, P), cols(XIN + ch * CH, CH), start=True,
                              stop=True).then_inc(s_c1, 1)

            def depthwise(i):
                t = BY_TENSOR[i]
                pe.wait_ge(s_diag, i + 1)
                pe.wait_ge(s_clip_g, i + 1)
                if i == 0:
                    pe.wait_ge(s_rl, 1)
                for ch in range(NCH):
                    n = NCH * i + ch
                    if n >= 4:
                        pe.wait_ge(s_dwa, n - 3)
                    for k in range(K):
                        ins = t_.matmul(ps(4 + ch % 4, 0, CH), cols(W_DIAG + k * P, P),
                                        pad_rows(T_PAD[PADBUF[t]], ch * CR + k // 3, k % 3), start=(k == 0),
                                        stop=(k == K - 1))
                    ins.then_inc(s_dw, 1)

            for q in range(4):
                hidden(q)
            depthwise(0)
            hidden(4)
            hidden(5)
            depthwise(1)
            pe.wait_ge(s_wo, 1)
            pe.wait_ge(s_dwv, len(BY_VECTOR))
            pe.wait_ge(s_hid, 2)
            pe.wait_ge(s_relu, NCH * NT)
            for ch in range(NCH):
                if ch >= 4:
                    pe.wait_ge(s_proj_free, ch - 3)
                for t in range(NT):
                    ins = t_.matmul(ps(ch % 4, 0, CH), cols(W_OUT + t * P, P), cols(T_HID[t] + ch * CH, CH),
                                    start=(t == 0), stop=(t == NT - 1))
                ins.then_inc(s_proj, 1)

            pe.wait_ge(s_z, 1)
            far_done = pe.alloc_register("far_done_by_tensor")
            pe.reg_mov(far_done, 0)
            t_.sem_inc(s_tr, AHEAD)
            t_.sem_inc(s_cn, AHEAD)
            for L in range(2):
                for h in range(2):
                    pe.wait_ge(s_xc[h], 16 * (L + 1))
                    with pe.Fori(h * 2, h * 2 + 2) as i:
                        for u in range(4):
                            pe.wait_ge(s_oe, i * 4 + (u + 1 + BLK * L))
                            for dx in range(3):
                                ins = t_.matmul(ps(u, 0, CH, OM), cols(WR + WREP[f"ow{L}"][0] + dx * OM, OM, 0, OK),
                                                ap(XC + (u * B * XW + 1 + dx) + i * (4 * B * XW),
                                                   [[XW, B], [1, W]], 0, OK), start=(dx == 0), stop=(dx == 2))
                            ins.then_inc(s_oc, 1)
                pe.wait_ge(s_am, L + 1)
                pe.wait_ge(s_oe, BLK * (L + 1) + 4)
                t_.matmul(ps(0, 0, P, 2 * K), cols(FMAX, 2 * K), con("ident"), start=True, stop=True).then_inc(s_amt, 1)
                pe.wait_ge(s_sw, L + 1)
                pe.wait_ge(s_fl, L + 1)
                with pe.Fori(0, BR) as r:
                    pe.wait_ge(s_yb, r + (BR * L + 1))
                    for h in range(2):
                        t_.matmul(ps(6 + h, 0, CH), cols(ZERO, P), ap(ZERO, [[0, CH // P], [1, P]]), start=True, stop=False,
                                  skip_group_check=True)
                    with pe.Fori(0, 3) as dy:
                        def turn(dx):
                            step = r * 9 + dy * 3 + (dx + STEPS * L)
                            pe.wait_ge(s_gv, step + 1)
                            pe.wait_ge(s_gp, step + 1 + AHEAD)
                            pe.wait_ge(s_st, step + 1)
                            for s_ in range(8):
                                for g in range(NG):
                                    ins = t_.matmul(ps(2 * dx + s_ // 4, (s_ % 4) * P, P),
                                                    ap(GRP + (dx * NG + g) * GN_ + s_, [[8, P]]),
                                                    con("ident"), start=(g == 0 and s_ % 4 == 0),
                                                    stop=(g == NG - 1), skip_group_check=True)
                            ins.then_inc(s_tr, 1)

                        def contract(dx):
                            step = r * 9 + dy * 3 + (dx + STEPS * L)
                            pe.wait_ge(s_st, step + 1 + AHEAD)
                            for s_ in range(8):
                                ins = t_.matmul(ps(6 + s_ // 4, (s_ % 4) * P, P), cols(ST + dx * GN_ + s_ * P, P),
                                                cols(W_SAMP + dx * P + dy * (3 * P), P), start=False, stop=False,
                                                skip_group_check=True)
                            ins.then_inc(s_cn, 1)

                        turn(0)
                        turn(1)
                        contract(0)
                        turn(2)
                        contract(1)
                        contract(2)
                    for h in range(2):
                        ins = t_.matmul(ps(6 + h, 0, CH), cols(ZERO, P), ap(ZERO, [[0, CH // P], [1, P]]), start=False, stop=True,
                                        skip_group_check=True)
                    ins.then_inc(s_acc, 1)

                def far_block():
                    pe.wait_ge(s_rw, pe.snap(far_done) + 1)
                    pe.reg_add(far_done, far_done, 1)
                    tap = loaded(pe, ENTRY, 0, K - 1)
                    for ax in range(2):
                        ins = t_.matmul(ps(0, ax * BPX, BPX), cols(FSEL, P),
                                        ap(OFFB + ax * K * W + tap * W, [[2 * K * W, BR], [1, W]]), start=(ax == 0),
                                        stop=True, skip_group_check=True)
                    ins.then_inc(s_ro, 1)
                    pe.wait_ge(s_rs, pe.snap(far_done))
                    t_.matmul(ps(1, 0, BPX), cols(FW, P), cols(FACC, BPX), start=True, stop=True).then_inc(s_rp, 1)

                pe.wait_ge(s_any, L + 1)
                pe.wait_ge(s_yb, BR * (L + 1) + 1)
                many = loaded(pe, COUNT, 0, K * BLK)
                with pe.If(many > 0):
                    with pe.Fori(0, many):
                        far_block()
                group_sums(1 + L, "same_image")

            for L in range(2):
                src = XA if L == 0 else XP3
                if L == 0:
                    pe.wait_ge(s_xa, 3 * NCH)
                else:
                    pe.wait_ge(s_x3, NCH)
                pe.wait_ge(s_dw3, L + 1)
                for ch in range(NCH):
                    for k in range(K):
                        t_.matmul(ps(ch, 0, CH), cols(W_DT + k * P, P),
                                  ap(src + (ch * CR + 1 + k // 3) * XW + 1 + k % 3, [[XW, CR], [1, W]]),
                                  start=(k == 0), stop=False)
                    if ch == 0:
                        pe.wait_ge(s_box, L + 1)
                    t_.matmul(ps(ch, 0, CH), con("same_image"), cols(V3 + ch * CH, CH), start=False,
                              stop=True).then_inc(s_dp, 1)
                pe.wait_ge(s_d2, NCH * (L + 1))
                group_sums(3 + L, "same_channel")

        @block.gpsimd
        def _(pool):
            g = nc.gpsimd
            count = [0]

            def link(ins):
                count[0] += 1
                ins.then_inc(s_g, 1)
                pool.wait_ge(s_g, count[0])

            for buf in T_PAD[:3]:
                g.memset(cols(buf, PADN), 0.0)
            g.memset(cols(T_PAD[3], PADN), 0.0).then_inc(s_padz, 1)

            def clip(t, at):
                pool.wait_ge(s_relu, NCH * (ORDER.index(t) + 1))
                return g.tensor_scalar(cols(T_PAD[PADBUF[t]], PADN), cols(T_PAD[PADBUF[t]], PADN), 6.0, None, ALU.min)

            pool.wait_ge(s_padz, 1)
            for t in BY_TENSOR:
                clip(t, 0).then_inc(s_clip_g, 1)

            g.sem_inc(s_gp, AHEAD)
            for L in range(2):
                pool.wait_ge(s_xb, 16 * B * (L + 1))
                pool.wait_ge(s_od, 64 * (L + 1))
                with pool.Fori(0, BR) as r:
                    with pool.Fori(0, 3) as dy:
                        n = r * 3 + dy
                        for dx in range(3):
                            after = n * 3 + (dx + STEPS * L + 1)
                            pool.wait_ge(s_t, after)
                            pool.wait_ge(s_tr, after)
                            pool.wait_ge(s_gp, n * 3 + (dx + STEPS * L + AHEAD))
                            pool.sem_inc(s_held, 1)
                            grp = lambda q: ap(GRP + (dx * NG + q) * GN_, [[W, C], [1, W]])
                            t2 = ap(TMP + 2 * GN_, [[W, C], [1, W]])
                            for m, dst in ((6, grp(3)), (7, t2), (8, grp(4))):
                                ins = g.tensor_tensor(dst, neighbours(r + dy, dx, m // 3, m % 3), tent(dx, m),
                                                      ALU.mult)
                            ins.then_inc(s_gc, 1)
                            pool.wait_ge(s_gc, after)
                            g.tensor_tensor(grp(3), grp(3), t2, ALU.add).then_inc(s_gp, 1)

            pool.wait_ge(s_xa, 3 * NCH)
            g.memset(cols(XP3, XN), 0.0).then_inc(s_cz, 1)

def layout(i):
    f = lambda a: np.ascontiguousarray(np.asarray(a), dtype=np.float32)
    vectors = np.zeros((P, NVEC), np.float32)
    weights = np.zeros((P, NWREP), np.float32)

    def vec(name, value):
        o, w = VEC[name]
        vectors[:, o:o + w] = value.reshape(P, w)

    def wrep(name, value):
        o, w = WREP[name]
        weights[:, o:o + w] = value.reshape(P, w)

    per_channel = lambda a: np.tile(f(a), B)
    for name, key in [("gn_w", "L0_conv_gn_w"), ("gn_b", "L0_conv_gn_b"), ("gate_b", "L0_conv_gate_b"),
                      ("upd_b", "L0_conv_upd_b"), ("g3", "L1_conv_g3"), ("b3", "L1_conv_b3"), ("m3", "L1_conv_m3"),
                      ("v3", "L1_conv_v3"), ("dg0", "L2_conv_g1"), ("dbe0", "L2_conv_be1"), ("db0", "L2_conv_b1"),
                      ("dg1", "L2_conv_g2"), ("dbe1", "L2_conv_be2"), ("db1", "L2_conv_b2"),
                      ("gamma0", "L3_conv_gamma1"), ("beta0", "L3_conv_beta1"), ("gamma1", "L3_conv_gamma2"),
                      ("beta1", "L3_conv_beta2")]:
        vec(name, per_channel(i[key]))
    by_tile = lambda a: np.tile(f(a), (B,) + (1,) * (f(a).ndim - 1)).reshape(NT, P, -1).transpose(1, 0, 2)
    for name in ("g1", "b1", "m1", "v1", "g2", "b2", "m2", "v2"):
        vec(name, by_tile(i["L1_conv_" + name]))
    vec("wd", by_tile(f(i["L1_conv_wd"]).reshape(HID, K)))
    vec("br", np.tile(f(i["L1_conv_br"]), (P, 1)))
    for n in (0, 1):
        col = np.zeros(P, np.float32)
        col[:OM] = np.tile(f(i[f"L2_conv_ob{n + 1}"]).reshape(K, 2).T.reshape(-1), BR)
        vec(f"ob{n}", col)

    per_image = lambda a: np.tile(f(a), (B, 1))
    wrep("gate", per_image(f(i["L0_conv_gate_w"]).T))
    wrep("upd", per_image(f(i["L0_conv_upd_w"]).T))
    wrep("w1", per_image(f(i["L1_conv_w1"]).T))
    wrep("wr", per_image(f(i["L1_conv_wr"]).T))
    wrep("we", by_tile(f(i["L1_conv_we"]).transpose(2, 0, 1).reshape(HID, E * C)))
    for n in (0, 1):
        ow = f(i[f"L2_conv_ow{n + 1}"]).reshape(K, 2, C, 3, 3).transpose(3, 2, 4, 1, 0)
        band = np.zeros((BR + 2, C, 3, BR, 2, K), np.float32)
        for r in range(BR):
            band[r:r + 3, :, :, r] = ow
        wrep(f"ow{n}", np.concatenate([band.reshape(OK, -1), np.zeros((P - OK, 3 * OM), np.float32)]))
        w = f(i[f"L2_conv_w{n + 1}"]).reshape(C, C, K)
        wt = w.transpose(1, 2, 0).reshape(C, -1)
        wrep(f"cw{n}", per_image(wt))
        wrep(f"sw{n}", np.repeat(wt, B, axis=0))
        cen = f(i[f"L3_conv_centers{n + 1}"])
        wrep(f"dt{n}", per_image(cen.reshape(C, C, K).transpose(1, 2, 0).reshape(C, -1)))
        wrep(f"cn{n}", per_image(cen))
    return vectors, weights


def kernel(**inputs):
    import concourse.bacc as _bacc
    from concourse.bass_utils import run_bass_kernel_spmd as _run

    nc = _bacc.Bacc("TRN2", target_bir_lowering=False, num_devices=1)
    vectors, weights = layout(inputs)
    const, entries = constants()
    arrays = {"in_x": np.ascontiguousarray(inputs["x"]), "in_const": const, "in_entries": entries, "in_vectors": vectors,
              "in_weights": weights}
    args = [nc.dram_tensor(k, a.shape, F32, kind="ExternalInput").ap() for k, a in arrays.items()]
    args.append(nc.dram_tensor("out_0", (B, C, H, W), F32, kind="ExternalOutput").ap())
    build(nc, *args)
    r = _run(nc, [arrays], core_ids=[0])
    return r.results[0]["out_0"]
```

```python
from contextlib import ExitStack

import numpy as np
import concourse.bass as bass
from concourse import mybir

F32 = mybir.dt.float32
I32 = mybir.dt.int32
BF16 = mybir.dt.bfloat16
ALU = mybir.AluOpType
ACT = mybir.ActivationFunctionType
AX = mybir.AxisListType

P = 128
B, C, H, W = 8, 16, 64, 64
N = H * W
CH = 512
NCH = N // CH
PIECE = N // 4
CR = CH // W
HID, NT = 96, B * 96 // P
E = 8
K = 9
PW = W + 2
PADN = PW * PW
XW = W + 4
XN = XW * XW
BLK = 16
BR = H // BLK
BPX = BR * W
HB = 5 * XW
OR = 6
OG, OLAST = H // OR, H % OR
OM = OR * 2 * K
OK = (OR + 2) * C
EPS = 1e-5
D2_EPS = 1e-12
REACH = 67
SPAN = REACH + 1
NG = 5

VEC = {}
for name, width in [("gn_w", 1), ("gn_b", 1), ("gate_b", 1), ("upd_b", 1), ("g3", 1), ("b3", 1), ("m3", 1),
                    ("v3", 1), ("dg0", 1), ("dbe0", 1), ("db0", 1), ("dg1", 1), ("dbe1", 1), ("db1", 1),
                    ("gamma0", 1), ("beta0", 1), ("gamma1", 1), ("beta1", 1),
                    ("g1", NT), ("b1", NT), ("m1", NT), ("v1", NT), ("g2", NT), ("b2", NT), ("m2", NT),
                    ("v2", NT), ("wd", NT * K), ("br", E), ("ob0", 1), ("ob1", 1)]:
    VEC[name] = (sum(w for _, w in VEC.values()), width)
NVEC = sum(w for _, w in VEC.values())

WREP = {}
for name, width in [("gate", C), ("upd", C), ("w1", HID), ("wr", E),
                    ("cw0", K * C), ("cw1", K * C), ("sw0", K * C), ("sw1", K * C), ("dt0", K * C),
                    ("dt1", K * C), ("cn0", K * C), ("cn1", K * C), ("we", NT * E * C)]:
    WREP[name] = (sum(w for _, w in WREP.values()), width)
NWREP = sum(w for _, w in WREP.values())

CONST = {}
for name, width in [("ident", P), ("same_image", P), ("same_channel", P), ("same_pair", P), ("px8", 8),
                    ("blkhot", BLK), ("steps", 2 * SPAN + 1), ("rows", BR), ("columns", W)]:
    CONST[name] = (sum(w for _, w in CONST.values()), width)
NCONST = sum(w for _, w in CONST.values())


def constants():
    c = np.zeros((P, NCONST), np.float32)
    p = np.arange(P)

    def put(name, value):
        o, w = CONST[name]
        c[:, o:o + w] = value

    put("ident", p[:, None] == p[None, :])
    put("same_image", p[:, None] // C == p[None, :] // C)
    put("same_channel", p[:, None] % C == p[None, :] % C)
    put("same_pair", p[:, None] // 2 == p[None, :] // 2)
    put("px8", p[:, None] % 8 == np.arange(8)[None, :])
    put("blkhot", p[:, None] % BLK == np.arange(BLK)[None, :])
    put("steps", np.arange(-SPAN, SPAN + 1)[None, :])
    put("rows", BLK * np.arange(BR)[None, :])
    put("columns", np.arange(W)[None, :])
    e = np.arange(K * BLK)
    entries = np.stack([e + 1, e // BLK, e // BLK // 3, e // BLK % 3, e % BLK]).astype(np.float32)
    return c, entries


def build(nc, x, const, entries, vectors, weights, offset_weights, out):
    with ExitStack() as ctx:
        SIZE = 53200
        arena = ctx.enter_context(nc.sbuf_tensor("arena", [P, SIZE], F32))
        taken = [0]

        def place(width, at=None):
            if at is None:
                at = taken[0]
                taken[0] += width
            assert at + width <= SIZE, (at, width)
            return at

        def ap(at, dims, p0=0, pn=P):
            return bass.AP(arena, at + p0 * SIZE, [[SIZE, pn]] + [list(d) for d in dims])

        def cols(at, n, p0=0, pn=P):
            return ap(at, [[1, n]], p0, pn)

        CON = place(NCONST)
        VE = place(NVEC)
        WR = place(NWREP)

        def con(name, i=0, n=None):
            o, w = CONST[name]
            return cols(CON + o + i, w if n is None else n)

        def vec(name, i=0, n=1, pn=P):
            o, _ = VEC[name]
            return cols(VE + o + i, n, 0, pn)

        SMALL = place(720)
        small_at = [SMALL]

        def small(n):
            small_at[0] += n
            assert small_at[0] <= SMALL + 720
            return small_at[0] - n

        MATS = place(2 * P + 2 * NT * P + K * P)
        W_GATE, W_UPD, W_HID = MATS, MATS + P, MATS + 2 * P
        W_OUT = W_HID + NT * P
        W_DIAG = W_OUT + NT * P
        LATE = MATS - WREP["we"][1]
        W_SAMP = place(K * P, LATE)
        ZERO = place(CH // 2, W_SAMP + K * P)
        W_OFF = place(3 * OM, ZERO + CH // 2)
        LATE_END = W_OFF + 3 * OM

        BIG = taken[0]
        T_HID = [place(N) for _ in range(NT)]
        T_PAD = [place(PADN) for _ in range(4)]
        XIN = place(N)

        XA = T_PAD[0]
        XB = LATE_END
        GRP = XB + 2 * C * HB
        GN_ = C * W
        assert GRP + 3 * NG * C * W <= XA
        YA = XB
        assert N <= C * HB
        OFFB = XA + XN
        XC = GRP + 3 * NG * C * W - (OG + 1) * B * XW
        assert XC >= T_HID[4]
        TXY = OFFB + 2 * K * BPX
        TROW = 3 * W
        TT = TXY + 6 * K * W
        TMP = TT + 3 * 9 * W
        ST = TMP + 3 * GN_
        YB = ST + 3 * GN_
        place(0, YB + GN_)
        EARLY = 3

        def offc(g_):
            return ST + g_ * CH if g_ < EARLY else GRP + NG * GN_ + (g_ - EARLY) * CH

        assert EARLY * OR >= BLK and offc(OG + 1) <= XC

        PROJ = T_PAD[3] + PADN - 2 * CH

        xa_d = nc.dram_tensor("padded_image", [B, C, XN], F32, kind="Internal").ap()
        rows_d = nc.dram_tensor("padded_image_by_rows", [XW, C, B, XW], F32, kind="Internal").ap()
        off_d = nc.dram_tensor("offsets", [H, 2 * K, B, W], F32, kind="Internal").ap()
        y_d = nc.dram_tensor("sampled", [C, BR, B * BLK, W], F32, kind="Internal").ap()
        flag_d = nc.dram_tensor("reach", [P, 2 * K], F32, kind="Internal").ap()

        psum = ctx.enter_context(nc.psum_tensor("psum", [P, 8, CH], F32))

        def ps(bank, off, n, pn=P):
            return psum[0:pn, bank, off:off + n]

        def ap_ps(bank, dims):
            return bass.AP(psum, bank * CH, [[8 * CH, P]] + [list(d) for d in dims])

        def sem(name):
            return ctx.enter_context(nc.semaphore(name))

        s_const, s_vec, s_wrep = sem("const_loaded"), sem("vec_loaded"), sem("weights_loaded")
        s_x = [sem(f"x_loaded_{i}") for i in range(4)]
        s_out = sem("out_stored")
        s_v, s_a, s_g = sem("vector_chain"), sem("scalar_chain"), sem("gpsimd_chain")
        s_stat, s_grp, s_var, s_std, s_coef = (sem("stats_ready"), sem("group_sums_ready"), sem("variance_ready"),
                                               sem("deviation_ready"), sem("coefficients_ready"))
        s_w0, s_w1, s_wo = sem("gate_weights_ready"), sem("hidden_weights_ready"), sem("out_weights_ready")
        s_ko, s_woz = sem("experts_mixed"), sem("out_weights_cleared")
        s_hn = sem("normed_ready")
        s_gate, s_upd = sem("gate_products_ready"), sem("update_products_ready")
        s_g_act, s_blend = sem("gate_chunks_ready"), sem("update_chunks_ready")
        s_xsum, s_pool_w, s_route, s_rsig = (sem("layer0_ready"), sem("pooled_weights_ready"),
                                             sem("routing_logits_ready"), sem("routing_ready"))
        s_rl = sem("routing_biased")
        s_bn, s_bnstd = sem("bn_variance_ready"), sem("bn_deviation_ready")
        s_bnc = sem("bn_coefficients_ready")
        s_padz = sem("hidden_padding_cleared")
        s_c1 = sem("hidden_products_ready")
        s_relu = sem("hidden_chunks_written")
        s_clip_g = sem("hidden_clipped_by_gpsimd")
        s_dwv, s_dwa = sem("depthwise_by_vector"), sem("depthwise_by_tensor")
        s_dw = sem("depthwise_products_ready")
        s_diag = sem("diagonals_ready")
        s_hid = sem("hidden_tiles_finished")
        s_prod, s_padd = sem("depthwise_products_by_scalar"), sem("depthwise_sums_by_gpsimd")
        s_proj, s_projn = sem("projection_ready"), sem("projection_normed")
        s_xa = sem("layer_result_in_padded_image")

        s_sw = sem("sample_weights_ready")
        s_rd = sem("padded_rows_stored")
        s_ow = sem("offset_weights_loaded")
        s_xc = [sem(f"rows_image_loaded_{h}") for h in range(2)]
        s_oc, s_oe = sem("offset_products_ready"), sem("offsets_written")
        s_xd = sem("padded_image_stored")
        s_xb = [sem("even_block_rows_loaded"), sem("odd_block_rows_loaded")]
        s_od = [sem("first_offsets_stored"), sem("other_offsets_stored")]
        s_ob = [sem("first_rows_offsets_loaded"), sem("other_rows_offsets_loaded")]
        s_am = sem("block_maxima_ready")
        s_fd, s_fb = sem("reach_stored"), sem("reach_loaded")
        s_tn, s_ab = sem("tents_ready"), sem("distances_to_neighbours_ready")
        s_t0, s_tg = sem("first_tent_products_ready"), sem("tent_products_by_gpsimd_ready")
        s_gv, s_gp = sem("vector_groups_ready"), sem("gpsimd_groups_ready")
        s_tr, s_st, s_cn = sem("samples_turned"), sem("turned_samples_copied"), sem("samples_contracted")
        s_acc, s_yb, s_ys = sem("row_accumulated"), sem("row_copied"), sem("row_stored")
        s_ya = [sem(f"convolution_loaded_{i}") for i in range(4)]
        s_rw, s_ro, s_rs, s_rp = (sem("far_weights_ready"), sem("far_offsets_spread"), sem("far_samples_ready"),
                                  sem("far_products_ready"))
        s_any, s_fc = sem("farthest_known"), sem("far_chain")
        s_gc = sem("gpsimd_products_ready")
        s_z = sem("zeros_ready")
        s_held = sem("held")
        s_nrm = sem("normed_relu_ready")
        s_dw3, s_cz = sem("distance_weights_ready"), sem("second_padding_cleared")
        s_sq, s_box = sem("squares_ready"), sem("box_sums_ready")
        s_dp, s_d2, s_dist = sem("distance_products_ready"), sem("squared_distances_ready"), sem("distances_ready")
        s_x3, s_fin, s_res = sem("second_input_ready"), sem("final_sums_ready"), sem("results_ready")

        AHEAD = 3
        STEPS = BR * K

        block = ctx.enter_context(nc.Block())

        ORDER = [0, 4, 5, 1, 2, 3]
        PADBUF = {0: 0, 4: 3, 5: 2, 1: 1, 2: 0, 3: 1}
        BY_VECTOR, BY_TENSOR, BY_GPSIMD = [0, 1, 2, 3], 4, 5
        HALF = N // 2
        PROD = T_HID[3]

        STAT, MV, GV, NC_ = small(6 * NCH), small(4), small(4), small(4)
        ROUT, ROUTL = small(NT * E), small(NT * E)
        KO = small(NT * C)
        BN = small(4 * NT)
        BV = small(2 * NT + 1)
        S3, B3 = small(1), small(1)
        WDS = small(NT * K)
        XS = small(1)

        FMAX = small(2 * K)
        COUNT = small(1)
        ENTRY = small(6)
        LAST = small(1)
        C2 = small(2)

        T0, T1, T2, T3, T4, T5 = T_HID

        FSEL, FW = GRP, GRP + P
        FO = FW + P
        FTY, FTX, FROW, FACC = (FO + (2 + i) * BPX for i in range(4))
        FALL = TXY
        FKEY = FALL + P * 2 * K
        FHIT = FKEY + K * BLK
        FATTR = FHIT + K * BLK
        FREACH = FATTR + 6 * K * BLK
        FNUMBER = FREACH + 2 * K * BLK
        FTAP = FNUMBER + K * BLK

        SQ3 = BIG
        HS3 = SQ3 + XN
        V3 = HS3 + PW * W
        D3 = V3 + N
        XP3 = D3 + N
        W_DT = [place(K * P, OFFB), place(K * P, OFFB + K * P)]
        OUT3 = V3
        assert XP3 + XN <= XA and OFFB == XA + XN

        def xa_rows(ch):
            return ap(XA + (ch * CR + 2) * XW + 2, [[XW, CR], [1, W]])

        def pad_rows(buf, row, col):
            return ap(buf + row * PW + col, [[PW, CR], [1, W]])

        def loaded(eng, at, low, high):
            return eng.value_load(cols(at, 1, 0, 1).bitcast(I32), min_val=low, max_val=high)

        def neighbours(u, dy, dx, j, i):
            return ap(XB + u * C * HB + (dy + j) * XW + dx + i, [[HB, C], [1, W]])

        def tent(dx, m):
            return ap(TT + (dx * 9 + m) * W, [[0, C], [1, W]])

        def grp(dx, g):
            return ap(GRP + (dx * NG + g) * GN_, [[W, C], [1, W]])

        def tent_products(engine, s_):
            dy, dx = divmod(s_, 3)
            at = TXY + dy * 6 * TROW + dx * W
            return engine.tensor_tensor(ap(TT + dx * 9 * W, [[3 * W, 3], [W, 3], [1, W]]),
                                        ap(at, [[TROW, 3], [0, 3], [1, W]]),
                                        ap(at + 3 * TROW, [[0, 3], [TROW, 3], [1, W]]), ALU.mult)

        @block.sync
        def _(sp):
            for i in range(4):
                sp.dma_start(cols(XIN + i * PIECE, PIECE),
                             x.rearrange("b c h w -> (b c) (h w)")[:, i * PIECE:(i + 1) * PIECE]
                             ).then_inc(s_x[i], 16)
            sp.dma_start(cols(CON, NCONST), const).then_inc(s_const, 16)
            sp.dma_start(cols(VE, NVEC), vectors).then_inc(s_vec, 16)
            sp.dma_start(cols(WR, NWREP), weights).then_inc(s_wrep, 16)
            sp.sem_inc(s_ys, 16)

            def image_part(row, end):
                sp.dma_start(xa_d.rearrange("b c n -> (b c) n")[:, row * XW:end * XW],
                             cols(XA + row * XW, (end - row) * XW)).then_inc(s_xd, 16)

            def result_row(L, r):
                sp.dma_start(cols(YA + r * PIECE, PIECE),
                             y_d[:, r].rearrange("o (b q) x -> b o (q x)", b=B)).then_inc(s_ya[r], 16)

            def block_rows(L, r):
                for b in range(B):
                    sp.dma_start(ap(XB + r % 2 * C * HB, [[HB, C], [1, HB]], b * BLK, BLK),
                                 bass.AP(xa_d.tensor, b * C * XN + r * BLK * XW, [[XW, BLK], [XN, C], [1, HB]])
                                 ).then_inc(s_xb[r % 2], 16)

            for L in range(2):
                for h, (ready, row, end) in enumerate(((NCH // 2, 0, H // 2 + 2), (NCH, H // 2 + 2, XW))):
                    sp.wait_ge(s_xa, NCH * L + ready)
                    for b in range(B):
                        sp.dma_start(rows_d[row:end, :, b, :].rearrange("h c x -> c h x"),
                                     ap(XA + row * XW, [[XW, end - row], [1, XW]], b * C, C)).then_inc(s_rd, 16)
                    if h == 0:
                        if L == 0:
                            sp.wait_ge(s_proj, NCH)
                        sp.dma_start(cols(W_OFF, 3 * OM), offset_weights[L]).then_inc(s_ow, 16)
                        image_part(row, end)
                    sp.wait_ge(s_rd, 16 * B * (2 * L + h + 1))
                    g0, g1 = ((0, 4), (4, OG))[h]
                    sp.dma_start(ap(XC + g0 * B * XW, [[B * XW, g1 - g0], [1, B * XW]], 0, OK),
                                 bass.AP(rows_d.tensor, (g0 * OR + 1) * C * B * XW,
                                         [[B * XW, OK], [OR * C * B * XW, g1 - g0], [1, B * XW]])
                                 ).then_inc(s_xc[h], 16)
                sp.dma_start(cols(XC + OG * B * XW, B * XW, 0, (OLAST + 2) * C),
                             bass.AP(rows_d.tensor, (OG * OR + 1) * C * B * XW,
                                     [[B * XW, (OLAST + 2) * C], [1, B * XW]])).then_inc(s_xc[1], 16)

                def block_offsets(r, done):
                    for b in range(B):
                        sp.dma_start(ap(OFFB + r * 2 * K * W, [[W, 2 * K], [1, W]], b * BLK, BLK),
                                     bass.AP(off_d.tensor, r * BLK * 2 * K * CH + b * W,
                                             [[2 * K * CH, BLK], [CH, 2 * K], [1, W]])).then_inc(done, 16)

                for n, (g0, g1, rows_) in enumerate(((0, EARLY, OR), (EARLY, 7, OR), (7, OG, OR), (OG, OG + 1, OLAST))):
                    sp.wait_ge(s_oe, (OG + 1) * L + g1)
                    sp.dma_start(bass.AP(off_d.tensor, g0 * OM * CH,
                                         [[CH, rows_ * 2 * K], [OM * CH, g1 - g0], [1, CH]]),
                                 ap(offc(g0), [[CH, g1 - g0], [1, CH]], 0, rows_ * 2 * K)
                                 ).then_inc(s_od[n > 0], 16)
                    if n == 0:
                        sp.wait_ge(s_xd, 32 * L + 16)
                        block_rows(L, 0)
                        sp.wait_ge(s_od[0], 16 * (L + 1))
                        block_offsets(0, s_ob[0])
                        image_part(H // 2 + 2, XW)
                        sp.wait_ge(s_xd, 32 * (L + 1))
                        block_rows(L, 1)
                sp.wait_ge(s_od[1], 48 * (L + 1))
                for r in range(1, BR):
                    block_offsets(r, s_ob[1])
                for r in range(BR):
                    if r < BR - 2:
                        sp.wait_ge(s_gv, K * (r + 1) + STEPS * L + AHEAD)
                        sp.wait_ge(s_gp, K * (r + 1) + STEPS * L + AHEAD)
                        block_rows(L, r + 2)
                    if r == BR - 1:
                        sp.wait_ge(s_gv, K * r + STEPS * L + AHEAD)
                        sp.wait_ge(s_gp, K * r + STEPS * L + AHEAD)
                        sp.wait_ge(s_ys, 16 * BR * L + 16 * r + 16)
                        for done in range(r):
                            result_row(L, done)
                        sp.wait_ge(s_am, L + 1)
                        sp.dma_start(flag_d, cols(FMAX, 2 * K)).then_inc(s_fd, 16)
                        sp.wait_ge(s_fd, 16 * (L + 1))
                        sp.wait_ge(s_gp, STEPS * (L + 1) + AHEAD)
                        sp.dma_start(cols(FALL, P * 2 * K, 0, 1),
                                     flag_d.rearrange("p k -> (p k)").unsqueeze(0)).then_inc(s_fb, 16)
                        sp.dma_start(cols(FNUMBER, 5 * K * BLK, 0, 1),
                                     entries.rearrange("k q -> (k q)").unsqueeze(0)).then_inc(s_fb, 16)
                    sp.wait_ge(s_yb, BR * L + r + 2)
                    sp.dma_start(y_d[:, r].rearrange("o p x -> p o x"), ap(YB, [[W, C], [1, W]])).then_inc(s_ys, 16)
                sp.wait_ge(s_ys, 16 * BR * (L + 1) + 16)
                result_row(L, BR - 1)
            for ch in range(NCH):
                sp.wait_ge(s_res, ch + 1)
                sp.dma_start(out.rearrange("b c h w -> (b c) (h w)")[:, ch * CH:(ch + 1) * CH],
                             cols(OUT3 + ch * CH, CH)).then_inc(s_out, 16)
            sp.wait_ge(s_out, 16 * NCH)
            sp.wait_ge(s_held, 2 * BR)

        @block.vector
        def _(dve):
            v = nc.vector
            count = [0]

            def link(ins):
                count[0] += 1
                ins.then_inc(s_v, 1)
                dve.wait_ge(s_v, count[0])

            def channel_stats(src, arrived, count_, shift=None):
                for ch in range(NCH):
                    if ch % 2 == 0:
                        dve.wait_ge(arrived[ch // 2], count_)
                    ins = v.bn_stats(cols(STAT + 6 * ch, 6), cols(src + ch * CH, CH))
                link(ins)
                link(v.bn_aggr(cols(MV, 2), cols(STAT, 6 * NCH)))
                if shift is not None:
                    link(v.tensor_tensor(cols(MV, 1), cols(MV, 1), shift, ALU.add))
                v.scalar_tensor_tensor(cols(MV + 1, 1), cols(MV, 1), cols(MV, 1), cols(MV + 1, 1), ALU.mult,
                                       ALU.add).then_inc(s_stat, 1)

            def norm_coefficients(n, count_, gamma, beta, shift=None):
                dve.wait_ge(s_grp, n + 1)
                link(v.tensor_scalar(cols(GV, 2), ps(0, 0, 2), 1.0 / count_, None, ALU.mult))
                link(v.tensor_tensor(cols(GV + 2, 1), cols(GV, 1), cols(GV, 1), ALU.mult))
                link(v.tensor_tensor(cols(GV + 2, 1), cols(GV + 1, 1), cols(GV + 2, 1), ALU.subtract))
                v.tensor_scalar(cols(GV + 2, 1), cols(GV + 2, 1), EPS, None, ALU.add).then_inc(s_var, 1)
                dve.wait_ge(s_std, n + 1)
                link(v.reciprocal(cols(NC_ + 2, 1), cols(GV + 3, 1)))
                link(v.tensor_tensor(cols(NC_, 1), cols(NC_ + 2, 1), gamma, ALU.mult))
                if shift is not None:
                    link(v.tensor_tensor(cols(GV, 1), cols(GV, 1), shift, ALU.subtract))
                link(v.tensor_tensor(cols(NC_ + 3, 1), cols(GV, 1), cols(NC_, 1), ALU.mult))
                v.tensor_tensor(cols(NC_ + 1, 1), beta, cols(NC_ + 3, 1), ALU.subtract).then_inc(s_coef, 1)

            channel_stats(XIN, s_x, 16)
            dve.wait_ge(s_const, 16)
            dve.wait_ge(s_vec, 16)
            dve.wait_ge(s_wrep, 16)

            def by_image(at, name, width):
                o, _ = CONST["same_image"]
                return v.tensor_tensor(ap(at, [[width, B], [1, width]]),
                                       ap(WR + WREP[name][0], [[0, B], [1, width]]),
                                       ap(CON + o, [[C, B], [0, width]]), ALU.mult)

            by_image(W_GATE, "gate", C).then_inc(s_w0, 1)
            by_image(W_UPD, "upd", C).then_inc(s_w0, 1)
            norm_coefficients(0, 2, vec("gn_w"), vec("gn_b"))
            by_image(W_HID, "w1", HID).then_inc(s_w1, 1)

            v.tensor_scalar(cols(BV, NT), vec("v1", 0, NT), EPS, None, ALU.add)
            v.tensor_scalar(cols(BV + NT, NT), vec("v2", 0, NT), EPS, None, ALU.add)
            v.tensor_scalar(cols(BV + 2 * NT, 1), vec("v3"), EPS, None, ALU.add).then_inc(s_bn, 1)

            for ch in range(NCH):
                dve.wait_ge(s_g_act, ch + 1)
                link(v.tensor_scalar(cols(T3 + ch * CH, CH), cols(T1 + ch * CH, CH), -1.0, 1.0, ALU.mult, ALU.add))
                dve.wait_ge(s_upd, ch + 1)
                v.scalar_tensor_tensor(cols(T0 + ch * CH, CH), ps(4 + ch % 4, 0, CH), vec("upd_b"),
                                       cols(T3 + ch * CH, CH), ALU.add, ALU.mult).then_inc(s_blend, 1)
            dve.wait_ge(s_blend, NCH)
            link(v.memset(ap(T1, [[W, H]]), 0.0))
            link(v.tensor_tensor_scan(cols(T4, N), cols(T1, N), cols(T0, N), 0.0, ALU.mult, ALU.add))
            link(v.tensor_tensor(ap(T5, [[H, W], [1, H]]), ap(T3, [[1, W], [W, H]]), ap(T4, [[1, W], [W, H]]),
                                 ALU.mult))
            dve.wait_ge(s_a, NCH)
            link(v.memset(ap(T2, [[H, W]]), 0.0))
            link(v.tensor_tensor_scan(cols(T1, N), cols(T2, N), cols(T5, N), 0.0, ALU.mult, ALU.add))
            v.tensor_tensor(ap(XIN, [[W, H], [1, W]]), ap(XIN, [[W, H], [1, W]]), ap(T1, [[1, H], [H, W]]),
                            ALU.add).then_inc(s_xsum, 1)

            dve.wait_ge(s_xsum, 1)
            link(v.tensor_reduce(cols(XS, 1), cols(XIN, N), AX.X, ALU.add))
            o = CONST["same_image"][0]
            v.tensor_scalar(ap(W_OUT, [[HID, B], [1, HID]]), ap(CON + o, [[C, B], [0, HID]]), cols(XS, 1), None,
                            ALU.mult).then_inc(s_pool_w, 1)
            dve.wait_ge(s_bnstd, 1)
            link(v.reciprocal(cols(BV, 2 * NT + 1), cols(BV, 2 * NT + 1)))
            link(v.tensor_tensor(cols(BN, NT), cols(BV, NT), vec("g1", 0, NT), ALU.mult))
            link(v.tensor_tensor(cols(BN + 2 * NT, NT), cols(BV + NT, NT), vec("g2", 0, NT), ALU.mult))
            link(v.tensor_tensor(cols(S3, 1), cols(BV + 2 * NT, 1), vec("g3"), ALU.mult))
            link(v.tensor_tensor(cols(BN + NT, NT), vec("m1", 0, NT), cols(BN, NT), ALU.mult))
            link(v.tensor_tensor(cols(BN + 3 * NT, NT), vec("m2", 0, NT), cols(BN + 2 * NT, NT), ALU.mult))
            link(v.tensor_tensor(cols(B3, 1), vec("m3"), cols(S3, 1), ALU.mult))
            link(v.tensor_tensor(cols(BN + NT, NT), vec("b1", 0, NT), cols(BN + NT, NT), ALU.subtract))
            link(v.tensor_tensor(cols(BN + 3 * NT, NT), vec("b2", 0, NT), cols(BN + 3 * NT, NT), ALU.subtract))
            link(v.tensor_tensor(cols(B3, 1), vec("b3"), cols(B3, 1), ALU.subtract))
            v.tensor_tensor(ap(WDS, [[K, NT], [1, K]]), ap(VE + VEC["wd"][0], [[K, NT], [1, K]]),
                            ap(BN + 2 * NT, [[1, NT], [0, K]]), ALU.mult).then_inc(s_bnc, 1)
            dve.wait_ge(s_bnc, 1)

            def diagonals(t):
                v.tensor_tensor(ap(W_DIAG, [[P, K], [1, P]]), ap(CON + CONST["ident"][0], [[0, K], [1, P]]),
                                ap(WDS + t * K, [[1, K], [0, P]]), ALU.mult).then_inc(s_diag, 1)

            diagonals(BY_TENSOR)
            dve.wait_ge(s_route, 1)
            v.scalar_tensor_tensor(ap(ROUTL, [[E, NT], [1, E]]), ap_ps(7, [[E, NT], [1, E]]), 1.0 / N,
                                   ap(VE + VEC["br"][0], [[0, NT], [1, E]]), ALU.mult, ALU.add).then_inc(s_rl, 1)
            dve.wait_ge(s_rsig, 1)

            def mix_experts():
                link(v.tensor_tensor(ap(W_OUT, [[E * C, NT], [C, E], [1, C]]),
                                     ap(WR + WREP["we"][0], [[E * C, NT], [C, E], [1, C]]),
                                     ap(ROUT, [[E, NT], [1, E], [0, C]]), ALU.mult))
                v.tensor_reduce(ap(KO, [[C, NT], [1, C]]), ap(W_OUT, [[E * C, NT], [1, C], [C, E]]), AX.X,
                                ALU.add).then_inc(s_ko, 1)

            mix_experts()

            for t in BY_VECTOR:
                buf, dst = T_PAD[PADBUF[t]], T_HID[t]
                shifted = lambda dy, dx: ap(buf + dy * PW + dx, [[PW, H], [1, W]])
                full = ap(dst, [[W, H], [1, W]])
                dve.wait_ge(s_relu, NCH * (ORDER.index(t) + 1))
                if dst == PROD:
                    dve.wait_ge(s_padd, 2 * (K - 1))
                link(v.tensor_scalar(cols(buf, PADN), cols(buf, PADN), 6.0, None, ALU.min))
                link(v.tensor_scalar(full, shifted(0, 0), cols(WDS + t * K, 1), cols(BN + 3 * NT + t, 1),
                                     ALU.mult, ALU.add))
                for k in range(1, K):
                    link(v.scalar_tensor_tensor(full, shifted(k // 3, k % 3), cols(WDS + t * K + k, 1), full,
                                                ALU.mult, ALU.add))
                v.tensor_scalar(cols(dst, N), cols(dst, N), 0.0, 6.0, ALU.max, ALU.min).then_inc(s_dwv, 1)
            dve.wait_ge(s_dwv, len(BY_VECTOR))
            v.memset(cols(XA, 2 * XW + 2), 0.0)
            v.memset(ap(XA + 3 * XW - 2, [[XW, H], [1, 4]]), 0.0)
            link(v.memset(cols(XA + (H + 2) * XW + 2, XN - (H + 2) * XW - 2), 0.0))
            for ch in range(NCH):
                dve.wait_ge(s_projn, ch + 1)
                v.tensor_tensor(xa_rows(ch), ap(PROJ + (ch % 2) * CH, [[W, CR], [1, W]]),
                                ap(XIN + ch * CH, [[W, CR], [1, W]]), ALU.add).then_inc(s_xa, 1)

            def sample_weights(L):
                if L == 0:
                    v.memset(cols(ZERO, CH // 2), 0.0).then_inc(s_z, 1)
                v.tensor_tensor(ap(W_SAMP, [[8, K * C], [1, 8]]),
                                ap(WR + WREP[f"sw{L}"][0], [[1, K * C], [0, 8]]),
                                ap(CON + CONST["px8"][0], [[0, K * C], [1, 8]]), ALU.mult).then_inc(s_sw, 1)

            def reach(L):
                dve.wait_ge(s_ob[1], 16 * B * (BR - 1) * (L + 1))
                v.tensor_reduce(cols(FMAX, 2 * K), ap(OFFB, [[W, 2 * K], [2 * K * W, BR], [1, W]]), AX.XY, ALU.max,
                                apply_absolute_value=True).then_inc(s_am, 1)

            def sample_row(L, r, u):
                base = count[0]
                count[0] = base + r * ROW_LINKS
                for s_ in range(K):
                    dy, dx = divmod(s_, 3)
                    step = r * K + (s_ + STEPS * L)
                    if s_ == 0:
                        dve.wait_ge(s_tn, r * 3 + (3 * BR * L + 1))
                        dve.wait_ge(s_gp, step + 1)
                        tent_products(v, 0).then_inc(s_t0, 1)
                        dve.wait_ge(s_t0, r + (BR * L + 1))
                    else:
                        if (u, s_) == (0, 1):
                            dve.wait_ge(s_od[1], 48 * (L + 1))
                        dve.wait_ge(s_tg, r * (K - 1) + ((K - 1) * BR * L + s_))
                    dve.wait_ge(s_tr, step + 1)

                    def product(m, dst):
                        j, i = divmod(m, 3)
                        return v.tensor_tensor(dst, neighbours(u, dy, dx, j, i), tent(dx, m), ALU.mult)

                    t0, t1 = ap(TMP, [[W, C], [1, W]]), ap(TMP + GN_, [[W, C], [1, W]])
                    product(0, grp(dx, 0))
                    product(1, t1)
                    product(2, grp(dx, 1))
                    dve.wait_ge(s_gv, step + AHEAD)
                    product(3, t0)
                    link(product(4, grp(dx, 2)))
                    v.tensor_tensor(grp(dx, 0), grp(dx, 0), t1, ALU.add)
                    link(v.tensor_tensor(grp(dx, 1), grp(dx, 1), t0, ALU.add))
                    link(product(5, t0))
                    v.tensor_tensor(grp(dx, 2), grp(dx, 2), t0, ALU.add).then_inc(s_gv, 1)
                count[0] = base

            ROW_LINKS = 3 * K

            def far_link(ins, last=False):
                ins.then_inc(s_fc, 1)
                if last:
                    dve.wait_ge(s_fc, dve.snap(far_chain) + 1)
                dve.reg_add(far_chain, far_chain, 1)
                if not last:
                    dve.wait_ge(s_fc, dve.snap(far_chain))

            far_chain = dve.alloc_register("far_chain")
            far_done = dve.alloc_register("far_done_by_vector")
            dve.reg_mov(far_chain, 0)
            dve.reg_mov(far_done, 0)

            def far_block(L):
                every = lambda at, n: ap(at, [[K * BLK, n], [1, K * BLK]], 0, 1)
                far_link(v.tensor_reduce(cols(LAST, 1, 0, 1), every(FKEY, 1), AX.X, ALU.max))
                far_link(v.tensor_scalar(every(FHIT, 1), every(FKEY, 1), cols(LAST, 1, 0, 1), None, ALU.is_equal))
                v.tensor_tensor(every(FATTR, 4), every(FTAP, 4),
                                ap(FHIT, [[0, 4], [1, K * BLK]], 0, 1), ALU.mult)
                far_link(v.tensor_tensor(every(FATTR + 4 * K * BLK, 2), every(FREACH, 2),
                                      ap(FHIT, [[0, 2], [1, K * BLK]], 0, 1), ALU.mult))
                far_link(v.tensor_reduce(cols(FATTR, 6, 0, 1), every(FATTR, 6), AX.X, ALU.add))
                far_link(v.tensor_copy(cols(ENTRY, 6, 0, 1).bitcast(I32), cols(FATTR, 6, 0, 1)))
                v.scalar_tensor_tensor(every(FKEY, 1), every(FHIT, 1), -float(K * BLK + 1), every(FKEY, 1),
                                       ALU.mult, ALU.add).then_inc(s_fc, 1)
                dve.reg_add(far_chain, far_chain, 1)
                ky, kx, blk = (loaded(dve, ENTRY + i, 0, h) for i, h in ((1, 2), (2, 2), (3, BLK - 1)))
                far_y, far_x = (loaded(dve, ENTRY + i, 1, REACH) for i in (4, 5))
                rows = ap(CON + CONST["rows"][0], [[1, BR], [0, W]])
                columns = ap(CON + CONST["columns"][0], [[0, BR], [1, W]])
                step_at = lambda i: cols(CON + CONST["steps"][0] + i, 1)
                img = lambda at: ap(at, [[W, BR], [1, W]])
                dve.wait_ge(s_fc, dve.snap(far_chain))
                v.tensor_scalar(cols(FSEL, P), con("same_image"), cols(CON + CONST["blkhot"][0] + blk, 1), None,
                                ALU.mult)
                v.tensor_tensor(ap(FW, [[C, B], [1, C]]),
                                ap(WR + WREP[f"cw{L}"][0] + kx * C + ky * (3 * C), [[0, B], [1, C]]),
                                ap(CON + CONST["same_image"][0], [[C, B], [0, C]]), ALU.mult).then_inc(s_rw, 1)
                dve.reg_add(far_done, far_done, 1)
                dve.wait_ge(s_ro, dve.snap(far_done))
                far_link(v.tensor_copy(cols(FO, 2 * BPX), ps(0, 0, 2 * BPX)))
                for off, at, plane, size in ((FO, step_at(blk + ky + (SPAN - 1)), rows, H),
                                             (FO + BPX, step_at(kx + (SPAN - 1)), columns, W)):
                    far_link(v.tensor_scalar(cols(off, BPX), cols(off, BPX), at, None, ALU.add))
                    far_link(v.tensor_tensor(img(off), img(off), plane, ALU.add))
                    far_link(v.tensor_scalar(cols(off, BPX), cols(off, BPX), -1.0, float(size), ALU.max, ALU.min))
                    far_link(v.tensor_tensor(img(off), img(off), plane, ALU.subtract))
                    far_link(v.tensor_scalar(cols(off, BPX), cols(off, BPX), at, None, ALU.subtract))

                def tent_before_relu(dst, off, i):
                    far_link(v.tensor_scalar(cols(dst, BPX), cols(off, BPX), -1.0, step_at(i + 1), ALU.mult, ALU.add))
                    far_link(v.scalar_tensor_tensor(cols(dst, BPX), cols(off, BPX), step_at(i - 1), cols(dst, BPX),
                                                    ALU.subtract, ALU.min))

                far_link(v.memset(cols(FACC, BPX), 0.0), last=True)

                def row_of_neighbours(j, column_ranges):
                    tent_before_relu(FTY, FO, j)
                    far_link(v.tensor_scalar(cols(FTY, BPX), cols(FTY, BPX), 0.0, None, ALU.max))
                    far_link(v.memset(cols(FROW, BPX), 0.0), last=True)
                    for first, end in column_ranges:
                        with dve.Fori(first, end) as i:
                            tent_before_relu(FTX, FO + BPX, i)
                            at = (blk + ky + j + (1 - SPAN)) * XW + kx + i + (1 - SPAN)
                            far_link(v.scalar_tensor_tensor(img(FTX), img(FTX), 0.0,
                                                            ap(XA + at, [[BLK * XW, BR], [1, W]]), ALU.max,
                                                            ALU.mult))
                            far_link(v.tensor_tensor(cols(FROW, BPX), cols(FROW, BPX), cols(FTX, BPX), ALU.add),
                                     last=True)
                    far_link(v.tensor_tensor(cols(FROW, BPX), cols(FROW, BPX), cols(FTY, BPX), ALU.mult))
                    far_link(v.tensor_tensor(cols(FACC, BPX), cols(FACC, BPX), cols(FROW, BPX), ALU.add), last=True)

                with dve.If(far_y > 1):
                    for first, end in ((SPAN - far_y, SPAN - 1), (SPAN + 2, SPAN + far_y + 1)):
                        with dve.Fori(first, end) as j:
                            row_of_neighbours(j, [(SPAN - 1, SPAN + 2)])
                with dve.If(far_x > 1):
                    with dve.Fori(SPAN - far_y, SPAN + far_y + 1) as j:
                        row_of_neighbours(j, [(SPAN - far_x, SPAN - 1), (SPAN + 2, SPAN + far_x + 1)])
                dve.sem_inc(s_rs, 1)
                dve.wait_ge(s_rp, dve.snap(far_done))
                for i in range(4):
                    dve.wait_ge(s_ya[i], 16 * (L + 1))
                own = ap(YA + blk * W, [[BLK * W, BR], [1, W]])
                far_link(v.tensor_tensor(own, own, ap_ps(1, [[W, BR], [1, W]]),
                                         ALU.add), last=True)

            def far_samples(L):
                dve.wait_ge(s_fb, 32 * (L + 1))
                flat = lambda at: cols(at, K * BLK, 0, 1)
                both = cols(FREACH, 2 * K * BLK, 0, 1)
                link(v.tensor_reduce(ap(FREACH, [[BLK, 2 * K], [1, BLK]], 0, 1),
                                     ap(FALL, [[1, 2 * K], [2 * K, BLK], [2 * K * BLK, B]], 0, 1), AX.X, ALU.max))
                link(v.tensor_scalar(cols(FATTR, 2 * K * BLK, 0, 1), both, REACH - 1.0, None, ALU.min))
                link(v.scalar_tensor_tensor(both, both, 1.0, cols(FATTR, 2 * K * BLK, 0, 1), ALU.is_gt, ALU.mult))
                link(v.tensor_scalar(both, both, 1.0, None, ALU.add))
                link(v.tensor_tensor(flat(FHIT), flat(FREACH), flat(FREACH + K * BLK), ALU.max))
                link(v.tensor_scalar(flat(FHIT), flat(FHIT), 1.0, None, ALU.is_gt))
                link(v.tensor_reduce(cols(LAST, 1, 0, 1), flat(FHIT), AX.X, ALU.add))
                v.tensor_tensor(flat(FKEY), flat(FHIT), flat(FNUMBER), ALU.mult)
                v.tensor_copy(cols(COUNT, 1, 0, 1).bitcast(I32), cols(LAST, 1, 0, 1)).then_inc(s_any, 1)
                dve.wait_ge(s_any, L + 1)
                dve.wait_ge(s_acc, BR * (L + 1))
                many = loaded(dve, COUNT, 0, K * BLK)
                with dve.If(many > 0):
                    with dve.Fori(0, many):
                        far_block(L)

            def distance_weights(L):
                o = WR + WREP[f"dt{L}"][0]
                link(v.tensor_scalar(cols(o, K * C), cols(o, K * C), -2.0, None, ALU.mult))
                v.tensor_tensor(ap(W_DT[L], [[P, K], [C, B], [1, C]]), ap(o, [[C, K], [0, B], [1, C]]),
                                ap(CON + CONST["same_image"][0], [[0, K], [C, B], [0, C]]),
                                ALU.mult).then_inc(s_dw3, 1)
                link(v.tensor_tensor_reduce(cols(TMP, K * C), cols(WR + WREP[f"cn{L}"][0], K * C),
                                            cols(WR + WREP[f"cn{L}"][0], K * C), 1.0, 0.0, ALU.mult, ALU.add,
                                            cols(C2 + L, 1)))

            def layer2(L):
                sample_weights(L)
                dve.wait_ge(s_sw, L + 1)
                with dve.Fori(0, BR // 2) as pair:
                    for u in range(2):
                        dve.wait_ge(s_xb[u], pair * (16 * B) + 16 * B * (BR // 2 * L + 1))
                        sample_row(L, pair * 2 + u, u)
                count[0] = count[0] + BR * ROW_LINKS
                reach(L)
                far_samples(L)
                channel_stats(YA, s_ya, 16 * (L + 1), vec(f"db{L}"))
                norm_coefficients(1 + L, C, vec(f"dg{L}"), vec(f"dbe{L}"), vec(f"db{L}"))
                for ch in range(NCH):
                    dve.wait_ge(s_nrm, NCH * L + ch + 1)
                    v.tensor_tensor(xa_rows(ch), xa_rows(ch), ap(YA + ch * CH, [[W, CR], [1, W]]),
                                    ALU.add).then_inc(s_xa, 1)

            v.sem_inc(s_gv, AHEAD)
            dve.wait_ge(s_proj, NCH)
            for L in range(2):
                layer2(L)

            def distance(L):
                src = XA if L == 0 else XP3
                dve.wait_ge(s_sq, L + 1)
                sq = lambda dx: ap(SQ3 + XW + 1 + dx, [[XW, PW], [1, W]])
                hs = ap(HS3, [[W, PW], [1, W]])
                link(v.tensor_tensor(hs, sq(0), sq(1), ALU.add))
                link(v.tensor_tensor(hs, hs, sq(2), ALU.add))
                link(v.tensor_tensor(cols(V3, N), cols(HS3, N), cols(HS3 + W, N), ALU.add))
                v.tensor_tensor(cols(V3, N), cols(V3, N), cols(HS3 + 2 * W, N), ALU.add).then_inc(s_box, 1)
                for ch in range(NCH):
                    dve.wait_ge(s_dp, NCH * L + ch + 1)
                    v.tensor_scalar(cols(D3 + ch * CH, CH), ps(ch % 8, 0, CH), cols(C2 + L, 1), D2_EPS, ALU.add,
                                    ALU.max).then_inc(s_d2, 1)
                for ch in range(NCH):
                    dve.wait_ge(s_dist, NCH * L + ch + 1)
                    ins = v.bn_stats(cols(STAT + 6 * ch, 6), cols(D3 + ch * CH, CH))
                link(ins)
                link(v.bn_aggr(cols(MV, 2), cols(STAT, 6 * NCH)))
                v.scalar_tensor_tensor(cols(MV + 1, 1), cols(MV, 1), cols(MV, 1), cols(MV + 1, 1), ALU.mult,
                                       ALU.add).then_inc(s_stat, 1)
                norm_coefficients(3 + L, B, vec(f"gamma{L}"), vec(f"beta{L}"))

            dve.wait_ge(s_xa, 3 * NCH)
            distance_weights(0)
            distance_weights(1)
            distance(0)
            distance(1)
            dve.wait_ge(s_coef, 5)
            for ch in range(NCH):
                v.scalar_tensor_tensor(ap(D3 + ch * CH, [[W, CR], [1, W]]), ap(D3 + ch * CH, [[W, CR], [1, W]]),
                                       cols(NC_, 1), xa_rows(ch), ALU.mult, ALU.add).then_inc(s_fin, 1)

        @block.scalar
        def _(act):
            a = nc.scalar

            def deviation(n):
                act.wait_ge(s_var, n + 1)
                a.activation(cols(GV + 3, 1), cols(GV + 2, 1), ACT.Sqrt).then_inc(s_std, 1)

            deviation(0)
            act.wait_ge(s_bn, 1)
            a.activation(cols(BV, 2 * NT + 1), cols(BV, 2 * NT + 1), ACT.Sqrt).then_inc(s_bnstd, 1)
            act.wait_ge(s_coef, 1)
            for ch in range(NCH):
                a.activation(cols(T0 + ch * CH, CH), cols(XIN + ch * CH, CH), ACT.Identity, bias=cols(NC_ + 1, 1),
                             scale=cols(NC_, 1)).then_inc(s_hn, 1)
            for ch in range(NCH):
                act.wait_ge(s_gate, ch + 1)
                a.activation(cols(T1 + ch * CH, CH), ps(ch % 4, 0, CH), ACT.Sigmoid,
                             bias=vec("gate_b")).then_inc(s_g_act, 1)
                a.activation(ap(T2 + ch * CR, [[1, CR], [H, W]]), ap_ps(ch % 4, [[W, CR], [1, W]]), ACT.Sigmoid,
                             bias=vec("gate_b")).then_inc(s_a, 1)

            act.wait_ge(s_rl, 1)
            a.activation(cols(ROUT, NT * E), cols(ROUTL, NT * E), ACT.Sigmoid).then_inc(s_rsig, 1)
            act.wait_ge(s_bnc, 1)
            act.wait_ge(s_padz, 1)

            def hidden(q):
                t = ORDER[q]
                if t == 2:
                    act.wait_ge(s_dwv, 1)
                if t == 3:
                    act.wait_ge(s_dwv, 2)
                for ch in range(NCH):
                    act.wait_ge(s_c1, NCH * q + ch + 1)
                    a.activation(pad_rows(T_PAD[PADBUF[t]], ch * CR + 1, 1), ap_ps(ch % 4, [[W, CR], [1, W]]),
                                 ACT.Relu, bias=cols(BN + NT + t, 1), scale=cols(BN + t, 1)).then_inc(s_relu, 1)

            def depthwise_relu(ch):
                act.wait_ge(s_dw, ch + 1)
                a.activation(cols(T_HID[BY_TENSOR] + ch * CH, CH), ps(4 + ch % 4, 0, CH), ACT.Relu,
                             bias=cols(BN + 3 * NT + BY_TENSOR, 1)).then_inc(s_dwa, 1)

            def products(k):
                t = BY_GPSIMD
                for h in range(2):
                    src = ap(T_PAD[PADBUF[t]] + (h * H // 2 + k // 3) * PW + k % 3, [[PW, H // 2], [1, W]])
                    if k == 0:
                        a.activation(ap(T_HID[t] + h * HALF, [[W, H // 2], [1, W]]), src, ACT.Identity,
                                     bias=cols(BN + 3 * NT + t, 1), scale=cols(WDS + t * K, 1)).then_inc(s_prod, 1)
                    else:
                        if k > 1:
                            act.wait_ge(s_padd, 2 * (k - 2) + h + 1)
                        a.activation(ap(PROD + h * HALF, [[W, H // 2], [1, W]]), src, ACT.Identity,
                                     scale=cols(WDS + t * K + k, 1)).then_inc(s_prod, 1)

            for q in range(4):
                hidden(q)
            act.wait_ge(s_clip_g, 2)
            products(0)
            for ch in range(NCH):
                depthwise_relu(ch)
                products(ch + 1)
                if ch == NCH // 2 - 1:
                    hidden(4)
            hidden(5)
            for ch in range(NCH):
                act.wait_ge(s_proj, ch + 1)
                if ch >= 2:
                    act.wait_ge(s_xa, ch - 1)
                a.activation(cols(PROJ + (ch % 2) * CH, CH), ps(ch, 0, CH), ACT.Identity, bias=cols(B3, 1),
                             scale=cols(S3, 1)).then_inc(s_projn, 1)

            def tents(L, r, dy):
                for i in range(3):
                    ins = a.activation(ap(TXY + (dy * 6 + i) * TROW, [[3 * TROW, 2], [1, TROW]]),
                                       ap(OFFB + dy * TROW + r * (2 * K * W), [[K * W, 2], [1, TROW]]), ACT.Abs,
                                       bias=cols(CON + CONST["steps"][0] + SPAN + 1 - i, 1))
                ins.then_inc(s_ab, 1)
                act.wait_ge(s_ab, r * 3 + (dy + 3 * BR * L + 1))
                planes = cols(TXY + dy * 6 * TROW, 6 * TROW)
                a.activation(planes, planes, ACT.Relu, bias=con("columns", 1, 1), scale=-1.0).then_inc(s_tn, 1)

            def finish_row(L, r, ahead):
                for s_ in range(K):
                    dy, dx = divmod(s_, 3)
                    step = r * K + (s_ + STEPS * L)
                    act.wait_ge(s_tr, step + 1 + AHEAD)
                    act.wait_ge(s_cn, step + 1)
                    a.activation(cols(ST + dx * GN_, GN_), ap_ps(2 * dx, [[1, GN_]]), ACT.Copy).then_inc(s_st, 1)
                    if ahead and dx == 2:
                        act.wait_ge(s_tg, r * (K - 1) + ((K - 1) * BR * L + s_))
                        tents(L, r + 1, dy)
                act.wait_ge(s_acc, r + (BR * L + 1))
                act.wait_ge(s_ys, r * 16 + (16 * BR * L + 16))
                a.activation(ap(YB, [[1, 8], [W, C], [8, 8]]), ap_ps(6, [[P, 8], [8, C], [1, 8]]),
                             ACT.Copy).then_inc(s_yb, 1)

            a.sem_inc(s_st, AHEAD)
            a.sem_inc(s_yb, 1)
            for L in range(2):
                for g_ in range(OG + 1):
                    mn = (OR if g_ < OG else OLAST) * 2 * K
                    act.wait_ge(s_oc, g_ + 1 + (OG + 1) * L)
                    a.activation(cols(offc(g_), CH, 0, mn), ps(g_ % 8, 0, CH, mn), ACT.Identity,
                                 bias=vec(f"ob{L}", 0, 1, mn)).then_inc(s_oe, 1)
                    if g_ == 2 * EARLY - 1:
                        act.wait_ge(s_ob[0], 16 * B * (L + 1))
                        for dy in range(3):
                            tents(L, 0, dy)
                act.wait_ge(s_ob[1], 16 * B * (BR - 1) * (L + 1))
                with act.Fori(0, BR - 1) as r:
                    finish_row(L, r, True)
                finish_row(L, BR - 1, False)
                deviation(1 + L)
                act.wait_ge(s_coef, 2 + L)
                for ch in range(NCH):
                    a.activation(cols(YA + ch * CH, CH), cols(YA + ch * CH, CH), ACT.Relu, bias=cols(NC_ + 1, 1),
                                 scale=cols(NC_, 1)).then_inc(s_nrm, 1)

            for L in range(2):
                if L == 0:
                    act.wait_ge(s_xa, 3 * NCH)
                    a.activation(cols(SQ3, XN), cols(XA, XN), ACT.Square).then_inc(s_sq, 1)
                else:
                    act.wait_ge(s_x3, NCH)
                    a.activation(cols(SQ3, XN), cols(XP3, XN), ACT.Square).then_inc(s_sq, 1)
                for ch in range(NCH):
                    act.wait_ge(s_d2, NCH * L + ch + 1)
                    a.activation(cols(D3 + ch * CH, CH), cols(D3 + ch * CH, CH), ACT.Sqrt).then_inc(s_dist, 1)
                deviation(3 + L)
                act.wait_ge(s_coef, 4 + L)
                if L == 0:
                    act.wait_ge(s_cz, 1)
                    for ch in range(NCH):
                        a.activation(ap(XP3 + (ch * CR + 2) * XW + 2, [[XW, CR], [1, W]]),
                                     ap(D3 + ch * CH, [[W, CR], [1, W]]), ACT.Relu, bias=cols(NC_ + 1, 1),
                                     scale=cols(NC_, 1)).then_inc(s_x3, 1)
                else:
                    for ch in range(NCH):
                        act.wait_ge(s_fin, ch + 1)
                        a.activation(cols(OUT3 + ch * CH, CH), cols(D3 + ch * CH, CH), ACT.Relu,
                                     bias=cols(NC_ + 1, 1)).then_inc(s_res, 1)

        @block.tensor
        def _(pe):
            t_ = nc.tensor

            def group_sums(n, mask):
                pe.wait_ge(s_stat, n + 1)
                t_.matmul(ps(0, 0, 2), con(mask), cols(MV, 2), start=True, stop=True).then_inc(s_grp, 1)

            pe.wait_ge(s_const, 16)
            group_sums(0, "same_pair")
            pe.wait_ge(s_w0, 2)
            for ch in range(NCH):
                pe.wait_ge(s_hn, ch + 1)
                if ch >= 4:
                    pe.wait_ge(s_a, ch - 3)
                else:
                    pe.wait_ge(s_coef, 1)
                t_.matmul(ps(ch % 4, 0, CH), cols(W_GATE, P), cols(T0 + ch * CH, CH), start=True,
                          stop=True).then_inc(s_gate, 1)
                if ch >= 4:
                    pe.wait_ge(s_blend, ch - 3)
                t_.matmul(ps(4 + ch % 4, 0, CH), cols(W_UPD, P), cols(T0 + ch * CH, CH), start=True,
                          stop=True).then_inc(s_upd, 1)

            pe.wait_ge(s_pool_w, 1)
            pe.wait_ge(s_blend, NCH)
            for t in range(NT):
                ins = t_.matmul(ps(7, t * E, E), cols(W_OUT + t * P, P), cols(WR + WREP["wr"][0], E),
                                start=(t == 0), stop=True, skip_group_check=True)
            ins.then_inc(s_route, 1)
            pe.wait_ge(s_w1, 1)
            pe.wait_ge(s_xsum, 1)
            pe.wait_ge(s_a, NCH)

            def hidden(q):
                t = ORDER[q]
                for ch in range(NCH):
                    n = NCH * q + ch
                    if n >= 4:
                        pe.wait_ge(s_relu, n - 3)
                    t_.matmul(ps(ch % 4, 0, CH), cols(W_HID + t * P, P), cols(XIN + ch * CH, CH), start=True,
                              stop=True).then_inc(s_c1, 1)

            def depthwise(chunks):
                for ch in chunks:
                    if ch >= 4:
                        pe.wait_ge(s_dwa, ch - 3)
                    for k in range(K):
                        ins = t_.matmul(ps(4 + ch % 4, 0, CH), cols(W_DIAG + k * P, P),
                                        pad_rows(T_PAD[PADBUF[BY_TENSOR]], ch * CR + k // 3, k % 3),
                                        start=(k == 0), stop=(k == K - 1))
                    ins.then_inc(s_dw, 1)

            for q in range(4):
                hidden(q)
            pe.wait_ge(s_diag, 1)
            pe.wait_ge(s_clip_g, 1)
            pe.wait_ge(s_rl, 1)
            depthwise(range(NCH // 2))
            hidden(4)
            depthwise(range(NCH // 2, NCH))
            hidden(5)
            pe.wait_ge(s_wo, 1)
            pe.wait_ge(s_relu, NCH * NT)
            pe.wait_ge(s_dwa, NCH)
            for t, done, count_ in ((0, s_dwv, 1), (1, s_dwv, 2), (2, s_dwv, 3), (BY_GPSIMD, s_hid, 1),
                                    (BY_TENSOR, s_hid, 2), (3, s_dwv, 4)):
                pe.wait_ge(done, count_)
                for ch in range(NCH):
                    ins = t_.matmul(ps(ch, 0, CH), cols(W_OUT + t * P, P), cols(T_HID[t] + ch * CH, CH),
                                    start=(t == 0), stop=(t == 3))
                    if t == 3:
                        ins.then_inc(s_proj, 1)

            pe.wait_ge(s_z, 1)
            far_done = pe.alloc_register("far_done_by_tensor")
            pe.reg_mov(far_done, 0)
            t_.sem_inc(s_tr, AHEAD)
            t_.sem_inc(s_cn, AHEAD)
            for L in range(2):
                def offsets(bank, at, rows_):
                    kn, mn = (rows_ + 2) * C, rows_ * 2 * K
                    for dx in range(3):
                        ins = t_.matmul(ps(bank, 0, CH, mn), cols(W_OFF + dx * OM, mn, 0, kn),
                                        ap(XC + 1 + dx + at, [[XW, B], [1, W]], 0, kn), start=(dx == 0),
                                        stop=(dx == 2))
                    ins.then_inc(s_oc, 1)

                pe.wait_ge(s_ow, 16 * (L + 1))
                for g_ in range(OG + 1):
                    if g_ in (0, 4):
                        h = g_ // 4
                        pe.wait_ge(s_xc[h], 16 * (h + 1) * (L + 1))
                    if g_ >= 8:
                        pe.wait_ge(s_oe, g_ - 7 + (OG + 1) * L)
                    offsets(g_ % 8, g_ * B * XW, OR if g_ < OG else OLAST)
                pe.wait_ge(s_oe, (OG + 1) * (L + 1))
                pe.wait_ge(s_sw, L + 1)
                with pe.Fori(0, BR) as r:
                    zeros = cols(ZERO, CH // 2).bitcast(BF16)

                    def turn(s_):
                        dx = s_ % 3
                        step = r * K + (s_ + STEPS * L)
                        pe.wait_ge(s_gv, step + 1 + AHEAD)
                        pe.wait_ge(s_gp, step + 1 + AHEAD)
                        pe.wait_ge(s_st, step + 1)
                        for i in range(8):
                            for g in range(NG):
                                ins = t_.matmul(ps(2 * dx + i // 4, (i % 4) * P, P),
                                                ap(GRP + (dx * NG + g) * GN_ + i, [[8, P]]),
                                                con("ident"), start=(g == 0 and i % 4 == 0),
                                                stop=(g == NG - 1), skip_group_check=True)
                        ins.then_inc(s_tr, 1)

                    def contract(s_):
                        dx = s_ % 3
                        step = r * K + (s_ + STEPS * L)
                        pe.wait_ge(s_st, step + 1 + AHEAD)
                        for i in range(8):
                            ins = t_.matmul(ps(6 + i // 4, (i % 4) * P, P), cols(ST + dx * GN_ + i * P, P),
                                            cols(W_SAMP + s_ * P, P), start=False, stop=False,
                                            skip_group_check=True)
                        ins.then_inc(s_cn, 1)

                    turn(0)
                    for s_ in range(1, K):
                        turn(s_)
                        if s_ == 1:
                            pe.wait_ge(s_yb, r + (BR * L + 1))
                            for h in range(2):
                                t_.matmul(ps(6 + h, 0, CH), zeros[:, 0:P], zeros, start=True, stop=False,
                                          skip_group_check=True)
                        contract(s_ - 1)
                    contract(K - 1)
                    for h in range(2):
                        ins = t_.matmul(ps(6 + h, 0, CH), zeros[:, 0:P], zeros, start=False, stop=True,
                                        skip_group_check=True)
                    ins.then_inc(s_acc, 1)

                def far_block():
                    pe.wait_ge(s_rw, pe.snap(far_done) + 1)
                    pe.reg_add(far_done, far_done, 1)
                    tap = loaded(pe, ENTRY, 0, K - 1)
                    for ax in range(2):
                        ins = t_.matmul(ps(0, ax * BPX, BPX), cols(FSEL, P),
                                        ap(OFFB + ax * K * W + tap * W, [[2 * K * W, BR], [1, W]]), start=(ax == 0),
                                        stop=True, skip_group_check=True)
                    ins.then_inc(s_ro, 1)
                    pe.wait_ge(s_rs, pe.snap(far_done))
                    t_.matmul(ps(1, 0, BPX), cols(FW, P), cols(FACC, BPX), start=True, stop=True).then_inc(s_rp, 1)

                pe.wait_ge(s_yb, BR * (L + 1) + 1)
                pe.wait_ge(s_any, L + 1)
                many = loaded(pe, COUNT, 0, K * BLK)
                with pe.If(many > 0):
                    with pe.Fori(0, many):
                        far_block()
                group_sums(1 + L, "same_image")

            for L in range(2):
                src, arrived, base = (XA, s_xa, 2 * NCH) if L == 0 else (XP3, s_x3, 0)
                pe.wait_ge(s_dw3, L + 1)

                def taps(ch):
                    pe.wait_ge(arrived, base + min(ch + 2, NCH))
                    for k in range(K):
                        t_.matmul(ps(ch, 0, CH), cols(W_DT[L] + k * P, P),
                                  ap(src + (ch * CR + 1 + k // 3) * XW + 1 + k % 3, [[XW, CR], [1, W]]),
                                  start=(k == 0), stop=False)

                def window_squares(ch):
                    t_.matmul(ps(ch, 0, CH), con("same_image"), cols(V3 + ch * CH, CH), start=False,
                              stop=True).then_inc(s_dp, 1)

                LAG = 4
                for ch in range(NCH):
                    taps(ch)
                    if ch == LAG:
                        pe.wait_ge(s_box, L + 1)
                    if ch >= LAG:
                        window_squares(ch - LAG)
                for ch in range(NCH - LAG, NCH):
                    window_squares(ch)
                pe.wait_ge(s_d2, NCH * (L + 1))
                group_sums(3 + L, "same_channel")

        @block.gpsimd
        def _(pool):
            g = nc.gpsimd
            count = [0]

            def link(ins):
                count[0] += 1
                ins.then_inc(s_g, 1)
                pool.wait_ge(s_g, count[0])

            for buf in T_PAD[:3]:
                g.memset(cols(buf, PADN), 0.0)
            g.memset(cols(T_PAD[3], PADN), 0.0).then_inc(s_padz, 1)

            pool.wait_ge(s_padz, 1)
            for t in (BY_TENSOR, BY_GPSIMD):
                pool.wait_ge(s_relu, NCH * (ORDER.index(t) + 1))
                g.tensor_scalar(cols(T_PAD[PADBUF[t]], PADN), cols(T_PAD[PADBUF[t]], PADN), 6.0, None,
                                ALU.min).then_inc(s_clip_g, 1)
            pool.wait_ge(s_ko, 1)
            g.memset(cols(W_OUT, NT * P), 0.0).then_inc(s_woz, 1)
            pool.wait_ge(s_woz, 1)
            for t in range(NT):
                for p0 in range(0, P, 32):
                    b = (t * P + p0) // HID
                    link(g.tensor_copy(ap(W_OUT + t * P + b * C, [[1, C]], p0, 32),
                                       ap(KO + t * C, [[1, C]], p0, 32)))
            g.sem_inc(s_wo, 1)
            for k in range(1, K):
                for h in range(2):
                    n = 2 * (k - 1) + h
                    half = cols(T_HID[BY_GPSIMD] + h * HALF, HALF)
                    pool.wait_ge(s_prod, 2 * k + h + 1)
                    if k > 1:
                        pool.wait_ge(s_padd, n - 1)
                    g.tensor_tensor(half, half, cols(PROD + h * HALF, HALF), ALU.add).then_inc(s_padd, 1)
            pool.wait_ge(s_padd, 2 * (K - 1))
            g.tensor_scalar(cols(T_HID[BY_GPSIMD], N), cols(T_HID[BY_GPSIMD], N), 0.0, 6.0, ALU.max,
                            ALU.min).then_inc(s_hid, 1)
            pool.wait_ge(s_dwa, NCH)
            g.tensor_scalar(cols(T_HID[BY_TENSOR], N), cols(T_HID[BY_TENSOR], N), 6.0, None,
                            ALU.min).then_inc(s_hid, 1)

            g.sem_inc(s_gp, AHEAD)
            for L in range(2):
                with pool.Fori(0, BR // 2) as pair:
                    for u, s_ in ((u, s_) for u in range(2) for s_ in range(K)):
                        r = pair * 2 + u
                        dy, dx = divmod(s_, 3)
                        step = r * K + (s_ + STEPS * L)
                        if s_ == 0:
                            pool.wait_ge(s_xb[u], pair * (16 * B) + 16 * B * (BR // 2 * L + 1))
                            pool.wait_ge(s_t0, r + (BR * L + 1))
                        else:
                            if (u, s_) == (0, 1):
                                pool.wait_ge(s_od[1], 48 * (L + 1))
                            pool.wait_ge(s_tg, r * (K - 1) + ((K - 1) * BR * L + s_))
                        pool.wait_ge(s_tr, step + 1)
                        pool.wait_ge(s_gp, step + AHEAD)
                        if s_ < K - 1:
                            pool.wait_ge(s_gv, step + 2)
                            pool.wait_ge(s_tn, r * 3 + ((s_ + 1) // 3 + 3 * BR * L + 1))
                            tent_products(g, s_ + 1).then_inc(s_tg, 1)
                        else:
                            pool.sem_inc(s_held, 1)
                        t2 = ap(TMP + 2 * GN_, [[W, C], [1, W]])
                        for m, dst in ((6, grp(dx, 3)), (7, t2), (8, grp(dx, 4))):
                            ins = g.tensor_tensor(dst, neighbours(u, dy, dx, m // 3, m % 3), tent(dx, m),
                                                  ALU.mult)
                        ins.then_inc(s_gc, 1)
                        pool.wait_ge(s_gc, step + 1)
                        g.tensor_tensor(grp(dx, 3), grp(dx, 3), t2, ALU.add).then_inc(s_gp, 1)

            pool.wait_ge(s_xa, 3 * NCH)
            g.memset(cols(XP3, XN), 0.0).then_inc(s_cz, 1)

def layout(i):
    f = lambda a: np.ascontiguousarray(np.asarray(a), dtype=np.float32)
    vectors = np.zeros((P, NVEC), np.float32)
    weights = np.zeros((P, NWREP), np.float32)
    offset_weights = np.zeros((2, OK, 3 * OM), np.float32)

    def vec(name, value):
        o, w = VEC[name]
        vectors[:, o:o + w] = value.reshape(P, w)

    def wrep(name, value):
        o, w = WREP[name]
        weights[:, o:o + w] = value.reshape(P, w)

    per_channel = lambda a: np.tile(f(a), B)
    for name, key in [("gn_w", "L0_conv_gn_w"), ("gn_b", "L0_conv_gn_b"), ("gate_b", "L0_conv_gate_b"),
                      ("upd_b", "L0_conv_upd_b"), ("g3", "L1_conv_g3"), ("b3", "L1_conv_b3"), ("m3", "L1_conv_m3"),
                      ("v3", "L1_conv_v3"), ("dg0", "L2_conv_g1"), ("dbe0", "L2_conv_be1"), ("db0", "L2_conv_b1"),
                      ("dg1", "L2_conv_g2"), ("dbe1", "L2_conv_be2"), ("db1", "L2_conv_b2"),
                      ("gamma0", "L3_conv_gamma1"), ("beta0", "L3_conv_beta1"), ("gamma1", "L3_conv_gamma2"),
                      ("beta1", "L3_conv_beta2")]:
        vec(name, per_channel(i[key]))
    by_tile = lambda a: np.tile(f(a), (B,) + (1,) * (f(a).ndim - 1)).reshape(NT, P, -1).transpose(1, 0, 2)
    for name in ("g1", "b1", "m1", "v1", "g2", "b2", "m2", "v2"):
        vec(name, by_tile(i["L1_conv_" + name]))
    vec("wd", by_tile(f(i["L1_conv_wd"]).reshape(HID, K)))
    vec("br", np.tile(f(i["L1_conv_br"]), (P, 1)))
    for n in (0, 1):
        col = np.zeros(P, np.float32)
        col[:OM] = np.tile(f(i[f"L2_conv_ob{n + 1}"]).reshape(K, 2).T.reshape(-1), OR)
        vec(f"ob{n}", col)

    per_image = lambda a: np.tile(f(a), (B, 1))
    wrep("gate", per_image(f(i["L0_conv_gate_w"]).T))
    wrep("upd", per_image(f(i["L0_conv_upd_w"]).T))
    wrep("w1", per_image(f(i["L1_conv_w1"]).T))
    wrep("wr", per_image(f(i["L1_conv_wr"]).T))
    wrep("we", by_tile(f(i["L1_conv_we"]).transpose(2, 0, 1).reshape(HID, E * C)))
    for n in (0, 1):
        ow = f(i[f"L2_conv_ow{n + 1}"]).reshape(K, 2, C, 3, 3).transpose(3, 2, 4, 1, 0)
        band = offset_weights[n].reshape(OR + 2, C, 3, OR, 2, K)
        for r in range(OR):
            band[r:r + 3, :, :, r] = ow
        w = f(i[f"L2_conv_w{n + 1}"]).reshape(C, C, K)
        wt = w.transpose(1, 2, 0).reshape(C, -1)
        wrep(f"cw{n}", per_image(wt))
        wrep(f"sw{n}", np.repeat(wt, B, axis=0))
        cen = f(i[f"L3_conv_centers{n + 1}"])
        wrep(f"dt{n}", per_image(cen.reshape(C, C, K).transpose(1, 2, 0).reshape(C, -1)))
        wrep(f"cn{n}", per_image(cen))
    return vectors, weights, offset_weights


def kernel(**inputs):
    import concourse.bacc as _bacc
    from concourse.bass_utils import run_bass_kernel_spmd as _run

    nc = _bacc.Bacc("TRN2", target_bir_lowering=False, num_devices=1)
    vectors, weights, offset_weights = layout(inputs)
    const, entries = constants()
    arrays = {"in_x": np.ascontiguousarray(inputs["x"]), "in_const": const, "in_entries": entries, "in_vectors": vectors,
              "in_weights": weights, "in_offset_weights": offset_weights}
    args = [nc.dram_tensor(k, a.shape, F32, kind="ExternalInput").ap() for k, a in arrays.items()]
    args.append(nc.dram_tensor("out_0", (B, C, H, W), F32, kind="ExternalOutput").ap())
    build(nc, *args)
    r = _run(nc, [arrays], core_ids=[0])
    return r.results[0]["out_0"]
```
